# Optimizing a Trainium2 kernel written in Bass

```python
import numpy as np
import jax
import jax.numpy as jnp

def _softmax(x, axis=-1):
    return jax.nn.softmax(x, axis=axis)

def _gelu(x):
    return jax.nn.gelu(x, approximate=True)

def _silu(x):
    return jax.nn.silu(x)

def _sigmoid(x):
    return jax.nn.sigmoid(x)

def _layernorm(x, axis=-1, eps=1e-05):
    m = jnp.mean(x, axis=axis, keepdims=True)
    v = jnp.var(x, axis=axis, keepdims=True)
    return (x - m) / jnp.sqrt(v + eps)

def _scatter_add(tgt, idx, src, axis=0):
    return tgt.at[idx].add(src)

def _segment_sum(src, seg, n):
    return jax.ops.segment_sum(src, seg, n)
kernel_name = 'mk_adj_ffn_d4_adj_r2_3319c2'

def setup_inputs(seed: int=0):
    np.random.seed(seed)
    _w = jnp.asarray

    def _rec_inputs():
        import jax
        import jax.numpy as jnp
        _gk = jax.random.key(seed)
        x = -0.0002928 + 1 * jax.random.normal(jax.random.fold_in(_gk, 1), (1354, 128), jnp.float32)
        _a = jax.random.bernoulli(jax.random.fold_in(_gk, 2), 0.00295421, (1354, 1354))
        _a = jnp.logical_or(_a, jnp.eye(1354, dtype=bool))
        _af = _a.astype(jnp.float32)
        _af = _af * jax.random.uniform(jax.random.fold_in(_gk, 3), (1354, 1354), jnp.float32, 0.05, 1)
        adj = _af
        return (x, adj)
    x, adj = _rec_inputs()

    def _L0_gnn_setup():
        import jax, jax.numpy as jnp
        import numpy as np
        EPS = 1e-12
        key = jax.random.key(seed)
        k1, k2, k3 = jax.random.split(key, 3)
        N, F_IN, F_OUT = (8192, 128, 128)
        feat = jax.random.normal(k1, (N, F_IN), dtype=jnp.float32)
        A = jax.random.uniform(k2, (N, N), dtype=jnp.float32)
        bound = float(np.sqrt(6.0 / (F_IN + F_OUT)))
        W = jax.random.uniform(k3, (F_IN, F_OUT), minval=-bound, maxval=bound, dtype=jnp.float32)
        return {'feat': feat, 'A': A, 'W': W}
    _L0_gnn_all = _L0_gnn_setup()
    _L0_gnn_in = {k: v for k, v in _L0_gnn_all.items() if k in ('W',)}
    del _L0_gnn_all

    def _L0_ffn_setup():
        import jax, jax.numpy as jnp
        import numpy as np
        C = 128
        EPS = 1e-05
        N_ITERS = 30

        def _layernorm(x, w, bias):
            mu = jnp.mean(x, axis=-1, keepdims=True)
            var = jnp.mean(jnp.square(x - mu), axis=-1, keepdims=True)
            return (x - mu) * jax.lax.rsqrt(var + EPS) * w + bias
        key = jax.random.key(seed)
        kx, kw, kb, klw, klb = jax.random.split(key, 5)
        x = jax.random.normal(kx, (8, 1024, C), dtype=jnp.float32)
        bound = 1.0 / np.sqrt(C)
        W = jax.random.uniform(kw, (C, C), minval=-bound, maxval=bound, dtype=jnp.float32)
        b = jax.random.uniform(kb, (C,), minval=-bound, maxval=bound, dtype=jnp.float32)
        ln_w = jnp.ones((C,), dtype=jnp.float32)
        ln_b = jnp.zeros((C,), dtype=jnp.float32)
        return {'x': x, 'ln_w': ln_w, 'ln_b': ln_b, 'W': W, 'b': b}
    _L0_ffn_all = _L0_ffn_setup()
    _L0_ffn_in = {k: v for k, v in _L0_ffn_all.items() if k in ('ln_w', 'ln_b', 'W', 'b')}
    del _L0_ffn_all

    def _L1_gnn_setup():
        import jax, jax.numpy as jnp
        import numpy as np
        key = jax.random.key(seed)
        k1, k2, k3, k4 = jax.random.split(key, 4)
        N, H = (4096, 128)
        inputs = jax.random.normal(k1, (N, H), dtype=jnp.float32)
        adj = jax.random.uniform(k2, (N, N), dtype=jnp.float32)
        W = jax.random.normal(k3, (H, H), dtype=jnp.float32)
        b = jax.random.normal(k4, (H,), dtype=jnpp.float32) if False else jax.random.normal(k4, (H,), dtype=jnp.float32)
        return {'inputs': inputs, 'adj': adj, 'W': W, 'b': b}
    _L1_gnn_all = _L1_gnn_setup()
    _L1_gnn_in = {k: v for k, v in _L1_gnn_all.items() if k in ('W', 'b')}
    del _L1_gnn_all

    def _L1_ffn_setup():
        import jax, jax.numpy as jnp
        import numpy as np
        B, T, C = (64, 192, 128)
        NH, NKV = (4, 2)
        HD = C // NH
        NREP = NH // NKV
        NE, TOPK = (8, 2)
        HID = int(8 / 3 * C)
        EPS_RMS = 1e-06

        def _rope_tables(t_len):
            inv_freq = 1.0 / 10000.0 ** (np.arange(0, HD, 2, dtype=np.float32) / HD)
            t = np.arange(t_len, dtype=np.float32)
            freqs = np.outer(t, inv_freq)
            emb = np.concatenate([freqs, freqs], axis=-1)
            return (jnp.asarray(np.cos(emb)), jnp.asarray(np.sin(emb)))

        def _rotate_half(x):
            h = x.shape[-1] // 2
            return jnp.concatenate([-x[..., h:], x[..., :h]], axis=-1)

        def _rmsnorm(v, w):
            return v * jax.lax.rsqrt(jnp.mean(v * v, axis=-1, keepdims=True) + EPS_RMS) * w
        key = jax.random.key(seed)
        ks = jax.random.split(key, 10)
        s = lambda k, shape: jax.random.normal(k, shape, jnp.float32) * 0.02
        return {'x': jax.random.normal(ks[0], (B, T, C), jnp.float32), 'ln1_w': jnp.ones((C,), jnp.float32), 'ln2_w': jnp.ones((C,), jnp.float32), 'wq': s(ks[1], (NH * HD, C)), 'wk': s(ks[2], (NKV * HD, C)), 'wv': s(ks[3], (NKV * HD, C)), 'wo': s(ks[4], (C, C)), 'router_w': s(ks[5], (NE, C)), 'w1': s(ks[6], (NE, HID, C)), 'w2': s(ks[7], (NE, C, HID)), 'w3': s(ks[8], (NE, HID, C))}
    _L1_ffn_all = _L1_ffn_setup()
    _L1_ffn_in = {k: v for k, v in _L1_ffn_all.items() if k in ('ln1_w', 'ln2_w', 'wq', 'wk', 'wv', 'wo', 'router_w', 'w1', 'w2', 'w3')}
    del _L1_ffn_all

    def _L2_gnn_setup():
        import jax, jax.numpy as jnp
        import numpy as np
        N = 5000
        F = 128
        key = jax.random.key(seed)
        k1, k2 = jax.random.split(key)
        x = jax.random.normal(k1, (N, F), dtype=jnp.float32)
        A = jax.random.uniform(k2, (N, N), dtype=jnp.float32)
        W = jnp.ones((F,), dtype=jnp.float32)
        return {'input': x, 'A': A, 'W': W}
    _L2_gnn_all = _L2_gnn_setup()
    _L2_gnn_in = {k: v for k, v in _L2_gnn_all.items() if k in ('W',)}
    del _L2_gnn_all

    def _L2_ffn_setup():
        import jax, jax.numpy as jnp
        import numpy as np
        E, D, H, TOP_K = (6, 128, 128, 2)
        ROUTER_H = D // 2
        key = jax.random.key(seed)
        ks = jax.random.split(key, 12)
        s = 1.0 / np.sqrt(D)
        sh = 1.0 / np.sqrt(H)
        sr = 1.0 / np.sqrt(ROUTER_H)
        return {'features': jax.random.normal(ks[0], (8, 2048, D), dtype=jnp.float32), 'router_w1': jax.random.uniform(ks[1], (D, ROUTER_H), jnp.float32, -s, s), 'router_b1': jnp.zeros((ROUTER_H,), jnp.float32), 'router_w2': jax.random.uniform(ks[2], (ROUTER_H, E), jnp.float32, -sr, sr), 'router_b2': jnp.zeros((E,), jnp.float32), 'expert_w1': jax.random.uniform(ks[3], (E, D, H), jnp.float32, -s, s), 'expert_b1': jnp.zeros((E, H), jnp.float32), 'expert_w2': jax.random.uniform(ks[4], (E, H, H), jnp.float32, -sh, sh), 'expert_b2': jnp.zeros((E, H), jnp.float32), 'expert_w3': jax.random.uniform(ks[5], (E, H, D), jnp.float32, -sh, sh), 'expert_b3': jnp.zeros((E, D), jnp.float32)}
    _L2_ffn_all = _L2_ffn_setup()
    _L2_ffn_in = {k: v for k, v in _L2_ffn_all.items() if k in ('router_w1', 'router_b1', 'router_w2', 'router_b2', 'expert_w1', 'expert_b1', 'expert_w2', 'expert_b2', 'expert_w3', 'expert_b3')}
    del _L2_ffn_all

    def _L3_gnn_setup():
        import jax, jax.numpy as jnp
        import numpy as np
        N = 4096
        D_IN = 128
        D_OUT = 128
        key = jax.random.key(seed)
        k1, k2, k3 = jax.random.split(key, 3)
        input = jax.random.normal(k1, (N, D_IN), dtype=jnp.float32)
        adjacencyMatrix = jax.random.uniform(k2, (N, N), dtype=jnp.float32)
        W = jax.random.normal(k3, (D_OUT, D_IN), dtype=jnp.float32) * (1.0 / np.sqrt(D_IN))
        return {'input': input, 'adjacencyMatrix': adjacencyMatrix, 'W': W}
    _L3_gnn_all = _L3_gnn_setup()
    _L3_gnn_in = {k: v for k, v in _L3_gnn_all.items() if k in ('W',)}
    del _L3_gnn_all

    def _L3_ffn_setup():
        import jax, jax.numpy as jnp
        import numpy as np
        BN_EPS = 0.001

        def _bn(h, g, b, m, v):
            return g * (h - m) * jax.lax.rsqrt(v + BN_EPS) + b
        key = jax.random.key(seed)
        ks = jax.random.split(key, 8)
        B, F, Df = (128, 64, 128)
        E, H, D = (8, 128, 128)
        s1 = 1.0 / np.sqrt(Df)
        s2 = 1.0 / np.sqrt(H)
        return {'x': jax.random.normal(ks[0], (B, F, Df), jnp.float32), 'Wr': jax.random.normal(ks[1], (Df, E), jnp.float32) * s1, 'br': jnp.zeros((E,), jnp.float32), 'W1': jax.random.normal(ks[2], (E, Df, H), jnp.float32) * s1, 'b1': jnp.zeros((E, H), jnp.float32), 'g1': jnp.ones((E, H), jnp.float32), 'be1': jnp.zeros((E, H), jnp.float32), 'm1': jnp.zeros((E, H), jnp.float32), 'v1': jnp.ones((E, H), jnp.float32), 'W2': jax.random.normal(ks[3], (E, H, H), jnp.float32) * s2, 'b2': jnp.zeros((E, H), jnp.float32), 'g2': jnp.ones((E, H), jnp.float32), 'be2': jnp.zeros((E, H), jnp.float32), 'm2': jnp.zeros((E, H), jnp.float32), 'v2': jnp.ones((E, H), jnp.float32), 'Wo': jax.random.normal(ks[4], (E, H, D), jnp.float32) * s2, 'bo': jnp.zeros((E, D), jnp.float32)}
    _L3_ffn_all = _L3_ffn_setup()
    _L3_ffn_in = {k: v for k, v in _L3_ffn_all.items() if k in ('Wr', 'br', 'W1', 'b1', 'g1', 'be1', 'm1', 'v1', 'W2', 'b2', 'g2', 'be2', 'm2', 'v2', 'Wo', 'bo')}
    del _L3_ffn_all
    return {'x': x, 'adj': adj, 'L0_gnn_W': _L0_gnn_in['W'], 'L0_ffn_ln_w': _L0_ffn_in['ln_w'], 'L0_ffn_ln_b': _L0_ffn_in['ln_b'], 'L0_ffn_W': _L0_ffn_in['W'], 'L0_ffn_b': _L0_ffn_in['b'], 'L1_gnn_W': _L1_gnn_in['W'], 'L1_gnn_b': _L1_gnn_in['b'], 'L1_ffn_ln1_w': _L1_ffn_in['ln1_w'], 'L1_ffn_ln2_w': _L1_ffn_in['ln2_w'], 'L1_ffn_wq': _L1_ffn_in['wq'], 'L1_ffn_wk': _L1_ffn_in['wk'], 'L1_ffn_wv': _L1_ffn_in['wv'], 'L1_ffn_wo': _L1_ffn_in['wo'], 'L1_ffn_router_w': _L1_ffn_in['router_w'], 'L1_ffn_w1': _L1_ffn_in['w1'], 'L1_ffn_w2': _L1_ffn_in['w2'], 'L1_ffn_w3': _L1_ffn_in['w3'], 'L2_gnn_W': _L2_gnn_in['W'], 'L2_ffn_router_w1': _L2_ffn_in['router_w1'], 'L2_ffn_router_b1': _L2_ffn_in['router_b1'], 'L2_ffn_router_w2': _L2_ffn_in['router_w2'], 'L2_ffn_router_b2': _L2_ffn_in['router_b2'], 'L2_ffn_expert_w1': _L2_ffn_in['expert_w1'], 'L2_ffn_expert_b1': _L2_ffn_in['expert_b1'], 'L2_ffn_expert_w2': _L2_ffn_in['expert_w2'], 'L2_ffn_expert_b2': _L2_ffn_in['expert_b2'], 'L2_ffn_expert_w3': _L2_ffn_in['expert_w3'], 'L2_ffn_expert_b3': _L2_ffn_in['expert_b3'], 'L3_gnn_W': _L3_gnn_in['W'], 'L3_ffn_Wr': _L3_ffn_in['Wr'], 'L3_ffn_br': _L3_ffn_in['br'], 'L3_ffn_W1': _L3_ffn_in['W1'], 'L3_ffn_b1': _L3_ffn_in['b1'], 'L3_ffn_g1': _L3_ffn_in['g1'], 'L3_ffn_be1': _L3_ffn_in['be1'], 'L3_ffn_m1': _L3_ffn_in['m1'], 'L3_ffn_v1': _L3_ffn_in['v1'], 'L3_ffn_W2': _L3_ffn_in['W2'], 'L3_ffn_b2': _L3_ffn_in['b2'], 'L3_ffn_g2': _L3_ffn_in['g2'], 'L3_ffn_be2': _L3_ffn_in['be2'], 'L3_ffn_m2': _L3_ffn_in['m2'], 'L3_ffn_v2': _L3_ffn_in['v2'], 'L3_ffn_Wo': _L3_ffn_in['Wo'], 'L3_ffn_bo': _L3_ffn_in['bo']}

def reference(x, adj, L0_gnn_W, L0_ffn_ln_w, L0_ffn_ln_b, L0_ffn_W, L0_ffn_b, L1_gnn_W, L1_gnn_b, L1_ffn_ln1_w, L1_ffn_ln2_w, L1_ffn_wq, L1_ffn_wk, L1_ffn_wv, L1_ffn_wo, L1_ffn_router_w, L1_ffn_w1, L1_ffn_w2, L1_ffn_w3, L2_gnn_W, L2_ffn_router_w1, L2_ffn_router_b1, L2_ffn_router_w2, L2_ffn_router_b2, L2_ffn_expert_w1, L2_ffn_expert_b1, L2_ffn_expert_w2, L2_ffn_expert_b2, L2_ffn_expert_w3, L2_ffn_expert_b3, L3_gnn_W, L3_ffn_Wr, L3_ffn_br, L3_ffn_W1, L3_ffn_b1, L3_ffn_g1, L3_ffn_be1, L3_ffn_m1, L3_ffn_v1, L3_ffn_W2, L3_ffn_b2, L3_ffn_g2, L3_ffn_be2, L3_ffn_m2, L3_ffn_v2, L3_ffn_Wo, L3_ffn_bo):
    import jax
    import jax.numpy as jnp

    def _L0_gnn_ref(feat, A, W):
        import jax, jax.numpy as jnp
        import numpy as np
        EPS = 1e-12
        N = A.shape[0]
        A_hat = A + jnp.eye(N, dtype=A.dtype)
        d = jnp.sum(A_hat, axis=1)
        dinv = 1.0 / jnp.sqrt(d)
        A_norm = dinv[:, None] * A_hat * dinv[None, :]
        feat_agg = A_norm @ feat
        agg = jax.nn.relu(feat_agg @ W)
        norm = jnp.linalg.norm(agg, axis=1, keepdims=True)
        out = agg / jnp.maximum(norm, EPS)
        return out

    def _L0_ffn_ref(x, ln_w, ln_b, W, b):
        import jax, jax.numpy as jnp
        import numpy as np
        C = 128
        EPS = 1e-05
        N_ITERS = 30

        def _layernorm(x, w, bias):
            mu = jnp.mean(x, axis=-1, keepdims=True)
            var = jnp.mean(jnp.square(x - mu), axis=-1, keepdims=True)
            return (x - mu) * jax.lax.rsqrt(var + EPS) * w + bias

        def step(h, _):
            h = h + 0.01 * jnp.tanh(h)
            h = h * jax.nn.sigmoid(h)
            h = _layernorm(h, ln_w, ln_b)
            h = jnp.einsum('bsc,dc->bsd', h, W) + b
            return (h, None)
        x, _ = jax.lax.scan(step, x, None, length=N_ITERS)
        return x

    def _L1_gnn_ref(inputs, adj, W, b):
        import jax, jax.numpy as jnp
        import numpy as np
        N = adj.shape[0]
        adj_hat = adj + jnp.eye(N, dtype=adj.dtype)
        deg = jnp.sum(adj_hat, axis=1, keepdims=True)
        adj_norm = adj_hat / deg
        pre_sup = inputs @ W
        out = adj_norm @ pre_sup + b
        return jnp.tanh(out)

    def _L1_ffn_ref(x, ln1_w, ln2_w, wq, wk, wv, wo, router_w, w1, w2, w3):
        import jax, jax.numpy as jnp
        import numpy as np
        B, T, C = (64, 192, 128)
        NH, NKV = (4, 2)
        HD = C // NH
        NREP = NH // NKV
        NE, TOPK = (8, 2)
        HID = int(8 / 3 * C)
        EPS_RMS = 1e-06

        def _rope_tables(t_len):
            inv_freq = 1.0 / 10000.0 ** (np.arange(0, HD, 2, dtype=np.float32) / HD)
            t = np.arange(t_len, dtype=np.float32)
            freqs = np.outer(t, inv_freq)
            emb = np.concatenate([freqs, freqs], axis=-1)
            return (jnp.asarray(np.cos(emb)), jnp.asarray(np.sin(emb)))

        def _rotate_half(x):
            h = x.shape[-1] // 2
            return jnp.concatenate([-x[..., h:], x[..., :h]], axis=-1)

        def _rmsnorm(v, w):
            return v * jax.lax.rsqrt(jnp.mean(v * v, axis=-1, keepdims=True) + EPS_RMS) * w
        Bx, Tx, Cx = x.shape
        h = _rmsnorm(x, ln1_w)
        q = (h @ wq.T).reshape(Bx, Tx, NH, HD).transpose(0, 2, 1, 3)
        k = (h @ wk.T).reshape(Bx, Tx, NKV, HD).transpose(0, 2, 1, 3)
        v = (h @ wv.T).reshape(Bx, Tx, NKV, HD).transpose(0, 2, 1, 3)
        cos, sin = _rope_tables(Tx)
        cos, sin = (cos[None, None], sin[None, None])
        q = q * cos + _rotate_half(q) * sin
        k = k * cos + _rotate_half(k) * sin
        k = jnp.repeat(k, NREP, axis=1)
        v = jnp.repeat(v, NREP, axis=1)
        scores = jnp.einsum('bhtd,bhsd->bhts', q, k) / jnp.sqrt(jnp.float32(HD))
        causal = jnp.tril(jnp.ones((Tx, Tx), dtype=bool))
        scores = jnp.where(causal[None, None], scores, jnp.float32(-1e+30))
        att = jax.nn.softmax(scores, axis=-1)
        y = jnp.einsum('bhts,bhsd->bhtd', att, v).transpose(0, 2, 1, 3).reshape(Bx, Tx, Cx)
        x = x + y @ wo.T
        flat = _rmsnorm(x, ln2_w).reshape(-1, Cx)
        probs = jax.nn.softmax(flat @ router_w.T, axis=-1)
        tp, ti = jax.lax.top_k(probs, TOPK)
        tp = tp / (jnp.sum(tp, axis=-1, keepdims=True) + 1e-09)
        weights = jnp.sum(tp[..., None] * jax.nn.one_hot(ti, NE, dtype=flat.dtype), axis=1)
        out = jnp.zeros_like(flat)
        for e in range(NE):
            hh = jax.nn.silu(flat @ w1[e].T) * (flat @ w3[e].T)
            out = out + weights[:, e:e + 1] * (hh @ w2[e].T)
        return x + out.reshape(Bx, Tx, Cx)

    def _L2_gnn_ref(input, A, W):
        import jax, jax.numpy as jnp
        import numpy as np
        N = 5000
        F = 128
        hidden = input * W
        return A @ hidden

    def _L2_ffn_ref(features, router_w1, router_b1, router_w2, router_b2, expert_w1, expert_b1, expert_w2, expert_b2, expert_w3, expert_b3):
        import jax, jax.numpy as jnp
        import numpy as np
        E, D, H, TOP_K = (6, 128, 128, 2)
        ROUTER_H = D // 2
        rh = jax.nn.relu(features @ router_w1 + router_b1)
        expert_logits = jax.nn.softmax(rh @ router_w2 + router_b2, axis=-1)
        top_w, top_i = jax.lax.top_k(expert_logits, TOP_K)
        routing_weights = jax.nn.softmax(top_w, axis=-1)
        h1 = jax.nn.relu(jnp.einsum('bsd,edh->bseh', features, expert_w1) + expert_b1)
        h2 = jax.nn.relu(jnp.einsum('bseh,ehf->bsef', h1, expert_w2) + expert_b2)
        expert_out = jnp.einsum('bsef,efo->bseo', h2, expert_w3) + expert_b3
        sel = jnp.take_along_axis(expert_out, top_i[:, :, :, None], axis=2)
        combined = jnp.sum(sel * routing_weights[..., None], axis=2)
        return combined

    def _L3_gnn_ref(input, adjacencyMatrix, W):
        import jax, jax.numpy as jnp
        import numpy as np
        N = 4096
        D_IN = 128
        D_OUT = 128
        d_inv_sqrt = jnp.sum(adjacencyMatrix, axis=1) ** (-0.5)
        A_norm = adjacencyMatrix * d_inv_sqrt[:, None] * d_inv_sqrt[None, :]
        h = A_norm @ input
        return h @ W.T

    def _L3_ffn_ref(x, Wr, br, W1, b1, g1, be1, m1, v1, W2, b2, g2, be2, m2, v2, Wo, bo):
        import jax, jax.numpy as jnp
        import numpy as np
        BN_EPS = 0.001

        def _bn(h, g, b, m, v):
            return g * (h - m) * jax.lax.rsqrt(v + BN_EPS) + b
        feat = jnp.mean(x, axis=0)
        w = jax.nn.softmax(feat @ Wr + br, axis=-1)
        h = jnp.einsum('bfd,edh->bfeh', x, W1) + b1
        h = jax.nn.relu(_bn(h, g1, be1, m1, v1))
        h = jnp.einsum('bfeh,ehk->bfek', h, W2) + b2
        h = jax.nn.relu(_bn(h, g2, be2, m2, v2))
        y = jnp.einsum('bfeh,ehd->bfed', h, Wo) + bo
        return jnp.einsum('bfed,fe->bfd', y, w)
    x = x + _L0_gnn_ref(_layernorm(x, axis=-1), adj, L0_gnn_W)
    x = x + _L0_ffn_ref(_layernorm(x, axis=-1)[None], L0_ffn_ln_w, L0_ffn_ln_b, L0_ffn_W, L0_ffn_b)[0]
    x = x + _L1_gnn_ref(_layernorm(x, axis=-1), adj, L1_gnn_W, L1_gnn_b)
    x = x + _L1_ffn_ref(_layernorm(x, axis=-1)[None], L1_ffn_ln1_w, L1_ffn_ln2_w, L1_ffn_wq, L1_ffn_wk, L1_ffn_wv, L1_ffn_wo, L1_ffn_router_w, L1_ffn_w1, L1_ffn_w2, L1_ffn_w3)[0]
    x = x + _L2_gnn_ref(_layernorm(x, axis=-1), adj, L2_gnn_W)
    x = x + _L2_ffn_ref(_layernorm(x, axis=-1)[None], L2_ffn_router_w1, L2_ffn_router_b1, L2_ffn_router_w2, L2_ffn_router_b2, L2_ffn_expert_w1, L2_ffn_expert_b1, L2_ffn_expert_w2, L2_ffn_expert_b2, L2_ffn_expert_w3, L2_ffn_expert_b3)[0]
    x = x + _L3_gnn_ref(_layernorm(x, axis=-1), adj, L3_gnn_W)
    x = x + _L3_ffn_ref(_layernorm(x, axis=-1)[None], L3_ffn_Wr, L3_ffn_br, L3_ffn_W1, L3_ffn_b1, L3_ffn_g1, L3_ffn_be1, L3_ffn_m1, L3_ffn_v1, L3_ffn_W2, L3_ffn_b2, L3_ffn_g2, L3_ffn_be2, L3_ffn_m2, L3_ffn_v2, L3_ffn_Wo, L3_ffn_bo)[0]
    return x

_drawn_inputs = setup_inputs


def setup_inputs(seed=0):
    import zlib

    import numpy as np

    out = dict(_drawn_inputs(seed))
    spreads = {'L0_ffn_ln_w': (1.0, 0.2),
     'L0_ffn_ln_b': (0.0, 0.1),
     'L1_ffn_ln1_w': (1.0, 0.6),
     'L1_ffn_ln2_w': (1.0, 0.6),
     'L2_gnn_W': (1.0, 0.2),
     'L2_ffn_router_b1': (0.0, 0.641),
     'L2_ffn_router_b2': (0.0, 0.554),
     'L2_ffn_expert_b1': (0.0, 0.8),
     'L2_ffn_expert_b2': (0.0, 0.8),
     'L2_ffn_expert_b3': (0.0, 1.505),
     'L3_ffn_br': (0.0, 0.8),
     'L3_ffn_b1': (0.0, 0.8),
     'L3_ffn_g1': (1.0, 0.6),
     'L3_ffn_be1': (0.0, 2.0),
     'L3_ffn_m1': (0.0, 0.8),
     'L3_ffn_v1': (1.0, 0.6),
     'L3_ffn_b2': (0.0, 2.0),
     'L3_ffn_g2': (1.0, 0.6),
     'L3_ffn_be2': (0.0, 2.0),
     'L3_ffn_m2': (0.0, 0.8),
     'L3_ffn_v2': (1.0, 0.6),
     'L3_ffn_bo': (0.0, 1.809)}
    factors = {'L1_ffn_wq': 8.0,
     'L1_ffn_wk': 8.0,
     'L1_ffn_wv': 5.834,
     'L1_ffn_wo': 5.233,
     'L1_ffn_router_w': 8.0,
     'L1_ffn_w1': 8.0,
     'L1_ffn_w2': 8.0,
     'L1_ffn_w3': 8.0,
     'L2_ffn_router_w1': 2.962,
     'L2_ffn_router_w2': 3.337,
     'L2_ffn_expert_w1': 4.415,
     'L2_ffn_expert_w2': 3.791,
     'L2_ffn_expert_w3': 2.933}
    for name, (base, spread) in spreads.items():
        noise = np.random.default_rng([zlib.crc32(name.encode()), seed]).standard_normal(out[name].shape)
        drawn = base * np.exp(spread * noise) if base else spread * noise
        out[name] = jnp.asarray(drawn.astype(out[name].dtype))
    for name, factor in factors.items():
        out[name] = (out[name] * factor).astype(out[name].dtype)
    return out
```

```python
from contextlib import ExitStack

import numpy as np

import concourse.bass as bass
from concourse import mybir

F32 = mybir.dt.float32
F32R = mybir.dt.float32r
ALU = mybir.AluOpType
ACT = mybir.ActivationFunctionType
AX = mybir.AxisListType

P = 128
T = 1354
NT = -(-T // P)
TP = NT * P
GROUPS = [range(4 * g, min(4 * g + 4, NT)) for g in range(-(-NT // 4))]
NG = len(GROUPS)
WIDTH = [P * len(g) for g in GROUPS]
COLS = [slice(512 * g, 512 * g + WIDTH[g]) for g in range(NG)]
FG = [range(3 * g, min(3 * g + 3, NT)) for g in range(-(-NT // 3))]
NF = len(FG)
FCOLS = [slice(P * g[0], P * (g[-1] + 1)) for g in FG]
EPS_LN = 1e-5
ITERS = 30
HID = 3 * P
EPS_RMS = 1e-6
EPS_BN = 1e-3
E1, E2, E3 = 8, 6, 8
MASKED = -1e30
GAIN = 100.0
HEADS, KV_HEADS, HD = 4, 2, 32


def tile(buf, t):
    return buf[:, t * P:(t + 1) * P]


def recurrent_slots(eng, slot):
    end = ITERS * NF

    def fixed(n):
        slot(lambda c: (n + c) % NF, lambda c: n + c + 1, lambda c: 0 <= n + c < end)

    for n in range(-NF, 0):
        fixed(n)
    with eng.Fori(0, ITERS - 1) as i:
        for k in range(NF):
            slot(lambda c: (k + c) % NF, lambda c: i * NF + (k + c + 1), lambda c: True)
    for n in range(end - NF, end):
        fixed(n)


def build(nc, d, out, adj_lo_dram):
    ctx = ExitStack()
    with ctx:
        def sb(name, shape, dt=F32):
            return ctx.enter_context(nc.sbuf_tensor(name, shape, dt))

        def sem(name):
            return ctx.enter_context(nc.semaphore(name))

        adj_hi = sb("adj_hi", [P, NT, TP], F32R)
        adj_lo = sb("adj_lo", [P, NT, TP], F32R)
        x = sb("x", [P, TP])
        xn = sb("xn", [P, TP])
        split_hi = sb("split_hi", [P, TP], F32R)
        split_lo = sb("split_lo", [P, TP], F32R)
        R = [sb(f"work{i}", [P, TP]) for i in range(5)]
        ident = sb("ident", [P, P])
        ident_r = sb("ident_r", [P, P], F32R)
        ones = sb("ones", [P, P])
        ones_r = sb("ones_r", [P, P], F32R)
        mean_w = sb("mean_w", [P, P])
        gnn_w = sb("gnn_w", [P, 3, P])
        l1_bias = sb("l1_bias", [P, P])
        l2_scale = sb("l2_scale", [P, 1])
        f0_wt = sb("f0_wt", [P, P])
        f0_lnw = sb("f0_lnw", [P, 1])
        f0_lnb = sb("f0_lnb", [P, 1])
        f0_b = sb("f0_b", [P, P])
        f0_lnb_b = sb("f0_lnb_b", [P, P])
        f0_m = sb("f0_m", [P, P])
        a_w = sb("a_w", [P, 448])
        a_whi = sb("a_whi", [P, 448], F32R)
        a_wlo = sb("a_wlo", [P, 448], F32R)
        a_ln1 = sb("a_ln1", [P, 1])
        a_ln2 = sb("a_ln2", [P, 1])
        a_wo = sb("a_wo", [P, P])
        a_router = sb("a_router", [P, E1])
        a_rhi = sb("a_rhi", [P, E1], F32R)
        a_rlo = sb("a_rlo", [P, E1], F32R)
        mask_f = sb("mask_f", [P, 2 * P])
        mask = sb("mask", [P, 2 * P], F32R)
        k_pad = sb("k_pad", [P, 1])
        mxc = sb("mxc", [P, NT * HEADS, NG])
        m_neg = sb("m_neg", [P, 16])
        m_hi = sb("m_hi", [P, 16], F32R)
        lg = sb("lg", [P, NT, 8])
        probs = sb("probs", [P, NT, 8])
        first = sb("first", [P, NT, 8])
        second = sb("second", [P, NT, 8])
        score = sb("score", [P, NT, 8])
        wgt = sb("wgt", [P, NT, 8])
        descend = sb("descend", [P, 8])
        rt = sb("rt", [P, 6, NT])
        w_raw = R[0][:, 0:2 * HID]
        w_hi = [sb(f"w_hi{i}", [P, 2 * HID], F32R) for i in range(2)]
        w_lo = [sb(f"w_lo{i}", [P, 2 * HID], F32R) for i in range(2)]
        w2_both = sb("w2_both", [P, 2 * HID])
        w2 = [w2_both[:, HID * i:HID * (i + 1)] for i in range(2)]
        k_scratch = w2_both[0:64, :]
        wcol = [sb(f"wcol{i}", [P, NT]) for i in range(2)]
        pcol = [sb(f"pcol{i}", [P, 4]) for i in range(2)]
        par2 = sb("par2", [P, 4, 8])
        par3 = sb("par3", [P, 4, 8])
        bn = sb("bn", [P, 10, 8])
        r2_w1 = sb("r2_w1", [P, P])
        r2_hi = sb("r2_hi", [P, P], F32R)
        r2_lo = sb("r2_lo", [P, P], F32R)
        r2_b1 = sb("r2_b1", [P, 1])
        r2_w2 = sb("r2_w2", [P, 8])
        r2_b2 = sb("r2_b2", [P, 8])
        r3_w = sb("r3_w", [P, 8])
        r3_hi = sb("r3_hi", [P, 8], F32R)
        r3_lo = sb("r3_lo", [P, 8], F32R)
        r3_b = sb("r3_b", [P, 8])
        b3 = sb("b3", [8, 2, P])
        stats = sb("stats", [P, NT, 6])
        mv = sb("mv", [P, NT, 2])
        rs = sb("rs", [P, NT])
        rss = sb("rss", [P, NT])
        deg = sb("deg", [P, NT])
        deg1 = sb("deg1", [P, NT])
        rdeg = sb("rdeg", [P, NT])
        dinv = sb("dinv", [P, NT])
        sinv = sb("sinv", [P, NT])
        power = sb("power", [P, NT])
        eps_h = sb("eps_h", [P, NT])
        ssq = sb("ssq", [P, NT])
        rnorm = sb("rnorm", [P, NT])
        PS = [ctx.enter_context(nc.psum_tensor(f"bank{b}", [P, 512], F32)) for b in range(8)]

        s_small = sem("small_loaded")
        s_x = sem("x_loaded")
        s_adj = [sem(f"adj_loaded{i}") for i in range(4)]
        s_adj_hi = sem("adj_hi_ready")
        s_adj_lo = sem("adj_lo_ready")
        s_adj_out = sem("adj_lo_stored")
        s_consts = sem("constants_ready")
        s_deg_row = sem("degree_rows_summed")
        s_deg_sb = sem("degree_row_copied")
        s_deg_col = sem("degree_columns_done")
        s_deg = sem("degrees_ready")
        s_dinv = sem("inverse_roots_ready")
        s_f0_m = sem("f0_scaled_weight")
        s_f0_mm = sem("f0_column_means")
        s_f0_w = sem("f0_weight_ready")
        s_var = sem("ln_variance_ready")
        s_rstd = sem("ln_rstd_ready")
        s_feat = sem("features_ready")
        s_hi = sem("split_hi_ready")
        s_lo = sem("split_lo_ready")
        s_agg = sem("aggregated")
        s_aggt = sem("aggregate_copied")
        s_mix = sem("mixed")
        s_relu = sem("relu_ready")
        s_ssq = sem("squares_summed")
        s_rnorm = sem("row_norms_ready")
        s_pre = sem("l1_tanh_input")
        s_tanh1 = sem("l1_tanh_ready")
        s_xup = sem("x_updated")
        s_h = sem("h_ready")
        s_t = sem("tanh_ready")
        s_h1 = sem("h_plus_tanh")
        s_sg = sem("sigmoid_ready")
        s_h2 = sem("h_gated")
        s_st = sem("h_stats_ready")
        s_hv = sem("h_variance_ready")
        s_ve = sem("h_variance_eps")
        s_hr = sem("h_rstd_ready")
        s_tr = sem("h_transposed")
        s_ht = sem("h_transposed_copied")
        s_p = sem("h_projected")
        s_tin = sem("to_transpose_ready")
        s_tt = sem("operand_transposed")
        s_thi = sem("operand_hi_ready")
        s_tlo = sem("operand_lo_ready")
        s_small2 = sem("small2_loaded")
        s_trig = sem("rope_tables_loaded")
        s_xn = sem("xn_ready")
        s_sq3 = sem("rms_squares_summed")
        s_rms = sem("rms_ready")
        s_whi = sem("attention_weights_hi")
        s_wlo = sem("attention_weights_lo")
        s_q = sem("qk_projected")
        s_v = sem("v_projected")
        s_vc = sem("v_copied")
        s_qr = sem("q_roped")
        s_qh = sem("q_hi_ready")
        s_ql = sem("q_lo_ready")
        s_kr = sem("k_roped")
        s_kh = sem("k_hi_ready")
        s_kl = sem("k_lo_ready")
        s_stack = sem("qk_stacked")
        s_mx = sem("scores_for_max")
        s_mxr = sem("scores_reduced")
        s_m = sem("max_ready")
        s_mt = sem("max_transposed")
        s_mrow = sem("max_rows_placed")
        s_sc = sem("scores_ready")
        s_e = sem("exp_ready")
        s_pv = sem("pv_done")
        s_y = sem("head_output_ready")
        s_wo = sem("attention_projected")
        s_x2 = sem("attention_residual")
        s_lgp = sem("router_product")
        s_lg = sem("logits_shifted")
        s_ex = sem("router_exp")
        s_wgt = sem("expert_weights_ready")
        s_hid = sem("router_hidden_product")
        s_hidc = sem("router_hidden_ready")
        s_m2 = sem("top2_difference")
        s_e2 = sem("top2_exp")
        s_reload = sem("adj_lo_reloaded")
        s_raw = sem("moe_raw_loaded")
        s_w2 = [sem(f"moe_w2_loaded{i}") for i in range(2)]
        s_mhi = sem("moe_weights_hi")
        s_mlo = sem("moe_weights_lo")
        s_mp = sem("moe_up_products")
        s_ms = sem("moe_silu_ready")
        s_mh = sem("moe_hidden_ready")
        s_my = sem("moe_down_product")
        s_ma = sem("moe_accumulated")
        s_wcol = sem("moe_column_ready")
        s_wt = sem("weights_transposed")
        s_wtc = sem("weights_transposed_copied")
        s_b3 = sem("bias_product")
        s_par = sem("bn_ready")
        s_bnr = sem("bn_roots")
        s_exp = [{k: sem(f"l{n}_{k}") for k in ("even_loaded", "odd_loaded", "w1_hi", "w1_lo", "product1", "hidden1", "product2", "hidden2",
                                                "product3", "accumulated")} for n in (2, 3)]
        s_final = sem("result_ready")
        s_out = sem("out_stored")
        s_dve = sem("vector_order")
        s_act = sem("scalar_order")
        s_pool = sem("gpsimd_order")

        QS = [adj_lo[:, h, :] for h in range(HEADS)]
        KS = [adj_lo[:, HEADS + v, :] for v in range(KV_HEADS)]
        QH, QL, KHL = (adj_lo[:, HEADS + KV_HEADS + n, :] for n in range(3))
        VA = R[0][:].rearrange("p (t v c) -> p t v c", v=KV_HEADS, c=2 * HD)
        PT = [R[1][:, 0:512], R[1][:, 512:1024], R[2][:, 0:512]]
        RL = R[2][0:HD, 512:1024]
        YT = R[3]
        MT = R[4][:, 0:512].rearrange("p (t h c) -> p t h c", h=HEADS, c=HD)
        HB = [[R[1 + j][:, 512 * b:512 * b + 512] for j in range(3)] for b in range(2)]
        SB = [R[4][:, 512 * b:512 * b + 512] for b in range(2)]
        SMALL2 = [(a_w, "a_w"), (a_ln1, "a_ln1"), (a_ln2, "a_ln2"), (a_wo, "a_wo"), (a_router, "a_router"), (mask_f, "mask"),
                  (k_pad, "k_pad"), (descend, "descend"), (par2, "par2"), (bn, "bn"), (r2_w1, "r2_w1"), (r2_b1, "r2_b1"),
                  (r2_w2, "r2_w2"), (r2_b2, "r2_b2"), (r3_w, "r3_w"), (r3_b, "r3_b"), (b3, "b3")]

        def max_pieces(g, h):
            for t in GROUPS[g]:
                for c in range(g + 1):
                    yield t, 512 * c, (512 if c < g else (t - 4 * g + 1) * P), c

        def key_steps(g):
            for kt in range(GROUPS[g][-1] + 1):
                yield kt, max(0, kt - 4 * g) * P

        schedule = [("max", 0, h, piece) for h in range(HEADS) for piece in max_pieces(0, h)] + [("rows", 0, 0, None)]
        for g in range(NG):
            for h in range(HEADS):
                ahead = list(max_pieces(g + 1, h)) if g + 1 < NG else []
                steps = list(key_steps(g))
                for n, step in enumerate(steps):
                    schedule.append(("key", g, h, step))
                    take = len(ahead) // (len(steps) - n)
                    schedule += [("max", g + 1, h, piece) for piece in ahead[:take]]
                    ahead = ahead[take:]
                schedule.append(("head", g, h, None))
            if g + 1 < NG:
                schedule.append(("rows", g + 1, 0, None))

        block = ctx.enter_context(nc.Block())

        @block.sync
        def _(sp):
            for t, src in ((ident, "ident"), (f0_wt, "f0_wt"), (f0_lnw, "f0_lnw"), (f0_lnb, "f0_lnb"), (f0_b, "f0_b")):
                sp.dma_start(t[:], d[src]).then_inc(s_small, 16)
            sp.dma_start(x[:].rearrange("p (t c) -> p t c", c=P),
                         d["x"].rearrange("(t p) c -> p t c", p=P)).then_inc(s_x, 16)
            for k in range(NT):
                if k >= 4:
                    sp.wait_ge(s_adj_lo, k - 3)
                sp.dma_start(R[k % 4][:], d["adj_t"][k * P:(k + 1) * P, :]).then_inc(s_adj[k % 4], 16)
            for t, src in ((gnn_w, "gnn_w"), (l1_bias, "l1_bias"), (l2_scale, "l2_scale")):
                sp.dma_start(t[:], d[src]).then_inc(s_small, 16)
            for t, src in SMALL2:
                sp.dma_start(t[:], d[src]).then_inc(s_small2, 16)
            sp.wait_ge(s_adj_lo, NT)
            sp.dma_start(adj_lo_dram, adj_lo[:].bitcast(F32)).then_inc(s_adj_out, 16)
            sp.wait_ge(s_ssq, NG)
            sp.dma_start(R[3][:], d["cos"]).then_inc(s_trig, 16)
            sp.dma_start(R[4][:], d["sin"]).then_inc(s_trig, 16)
            sp.wait_ge(s_ql, NG)
            sp.wait_ge(s_kl, NG)
            for h in range(HEADS):
                rows = slice(HD * h, HD * (h + 1))
                for part, src in enumerate((QH, QH, QL)):
                    sp.dma_start(QS[h][HD * part:HD * (part + 1), :].bitcast(F32), src[rows, :].bitcast(F32)).then_inc(s_stack, 16)
            for v in range(KV_HEADS):
                for part, first_row in enumerate((0, 64, 0)):
                    rows = slice(first_row + HD * v, first_row + HD * (v + 1))
                    sp.dma_start(KS[v][HD * part:HD * (part + 1), :].bitcast(F32), KHL[rows, :].bitcast(F32)).then_inc(s_stack, 16)

            def moe_up(e):
                sp.dma_start(w_raw.rearrange("p (a n) -> p a n", a=1), d["moe_w13"][:, bass.ds(e, 1), :]).then_inc(s_raw, 16)

            def moe_down(e, s):
                sp.dma_start(w2[s].rearrange("p (a n) -> p a n", a=1), d["moe_w2"][:, bass.ds(e, 1), :]).then_inc(s_w2[s], 16)

            moe_down(0, 0)
            moe_down(1, 1)
            sp.wait_ge(s_y, NG * HEADS)
            sp.wait_ge(s_adj_out, 16)
            sp.dma_start(adj_lo[:].bitcast(F32), adj_lo_dram).then_inc(s_reload, 16)
            sp.wait_ge(s_tt, 2 * NG)
            moe_up(0)
            with sp.Fori(0, E1 // 2 - 1) as i:
                for s in range(2):
                    sp.wait_ge(s_mlo, i * 2 + (s + 1))
                    moe_up(i * 2 + (s + 1))
                    sp.wait_ge(s_my, i * 6 + (3 * (s + 1) + 2))
                    moe_down(i * 2 + (s + 2), s)
            sp.wait_ge(s_mlo, E1 - 1)
            moe_up(E1 - 1)
            for n, experts, src in ((0, E2, "l2_w"), (1, E3, "l3_w")):
                sems = s_exp[n]
                loaded = (sems["even_loaded"], sems["odd_loaded"])

                def load(e, s):
                    sp.dma_start(w2[s].rearrange("p (a n) -> p a n", a=1), d[src][:, bass.ds(e, 1), :]).then_inc(loaded[s], 16)

                if n == 0:
                    sp.wait_ge(s_my, 3 * E1 + 2)
                else:
                    sp.wait_ge(s_exp[0]["product3"], 3 * E2)
                load(0, 0)
                load(1, 1)
                with sp.Fori(0, experts // 2 - 1) as i:
                    for s in range(2):
                        sp.wait_ge(sems["product3"], i * 6 + 3 * (s + 1))
                        load(i * 2 + (s + 2), s)

        @block.tensor
        def _(pe):
            mm = nc.tensor.matmul

            pe.wait_ge(s_consts, 2)
            for k in range(NT):
                pe.wait_ge(s_adj_hi, k + 1)
                pe.wait_ge(s_adj_lo, k + 1)
                for g in range(NG):
                    mm(PS[g][:, 0:WIDTH[g]], ones_r[:], adj_hi[:, k, COLS[g]], start=(k == 0), stop=False)
                    last = mm(PS[g][:, 0:WIDTH[g]], ones_r[:], adj_lo[:, k, COLS[g]], start=False, stop=(k == NT - 1))
            last.then_inc(s_deg_row, 1)
            pe.wait_ge(s_f0_m, 2)
            mm(PS[7][:, 0:P], mean_w[:], f0_m[:], start=True, stop=True)
            mm(PS[7][:, P:2 * P], f0_lnb_b[:], f0_wt[:], start=True, stop=True).then_inc(s_f0_mm, 1)
            pe.wait_ge(s_deg_sb, 1)
            for t in range(NT):
                last = mm(PS[6][:, t:t + 1], R[4][0:1, t * P:(t + 1) * P], ones[0:1, 0:1], start=True, stop=True)
            last.then_inc(s_deg_col, 1)

            def aggregate(q, self_loop):
                for g in range(NG):
                    pe.wait_ge(s_hi, NG * aggregate.calls + g + 1)
                    pe.wait_ge(s_lo, NG * aggregate.calls + g + 1)
                    if g < NG - 1:
                        for k in GROUPS[g]:
                            for c in range(NG):
                                tile_product(k, c, k == 0, False)
                            if self_loop:
                                self_product(k)
                for c in range(NG):
                    for k in GROUPS[-1]:
                        last = tile_product(k, c, False, k == NT - 1 and not (self_loop and c == NG - 1))
                    if self_loop and c == NG - 1:
                        for k in GROUPS[-1]:
                            last = self_product(k, stop=k == NT - 1)
                    last.then_inc(s_agg, 1)
                aggregate.calls += 1

            aggregate.calls = 0

            def tile_product(k, c, first, end):
                dst = PS[c][:, 0:WIDTH[c]]
                mm(dst, tile(split_hi, k), adj_hi[:, k, COLS[c]], start=first, stop=False)
                mm(dst, tile(split_hi, k), adj_lo[:, k, COLS[c]], start=False, stop=False)
                return mm(dst, tile(split_lo, k), adj_hi[:, k, COLS[c]], start=False, stop=end)

            def self_product(k, stop=False):
                dst = tile(PS[k // 4], k % 4)
                mm(dst, tile(split_hi, k), ident_r[:], start=False, stop=False)
                return mm(dst, tile(split_lo, k), ident_r[:], start=False, stop=stop)

            def mix(q, w):
                for g in range(NG):
                    pe.wait_ge(s_aggt, NG * q + g + 1)
                    for t in GROUPS[g]:
                        dst = tile(PS[3 + g], t % 4)
                        if w is None:
                            last = nc.tensor.transpose(dst, tile(R[1], t), ident[:])
                        else:
                            last = mm(dst, tile(R[1], t), gnn_w[:, w, :], start=True, stop=True)
                    last.then_inc(s_mix, 1)

            pe.wait_ge(s_small, 8 * 16)
            aggregate(0, True)
            mix(0, 0)
            pe.wait_ge(s_f0_w, 1)

            def slot(place, count, valid):
                if valid(2):
                    g = place(2)
                    pe.wait_ge(s_h2, count(2))
                    for n, t in enumerate(FG[g]):
                        last = nc.tensor.transpose(tile(PS[g], n), tile(R[0], t), ident[:])
                    last.then_inc(s_tr, 1)
                if valid(1):
                    g = place(1)
                    pe.wait_ge(s_ht, count(1))
                    for n, t in enumerate(FG[g]):
                        last = mm(tile(PS[NF + g], n), tile(R[2], t), f0_m[:], start=True, stop=True)
                    last.then_inc(s_p, 1)

            recurrent_slots(pe, slot)
            aggregate(1, True)
            mix(1, 1)

            def transpose_operand(n):
                for g in range(NG):
                    pe.wait_ge(s_tin, NG * n + g + 1)
                    for t in GROUPS[g]:
                        last = nc.tensor.transpose(tile(PS[g], t % 4), tile(R[0], t), ident[:])
                    last.then_inc(s_tt, 1)

            def three(dst, a_hi, a_lo, b_hi, b_lo, start=True, stop=True):
                mm(dst, a_hi, b_hi, start=start, stop=False)
                mm(dst, a_hi, b_lo, start=False, stop=False)
                return mm(dst, a_lo, b_hi, start=False, stop=stop)

            transpose_operand(0)
            pe.wait_ge(s_wlo, 1)
            for g in range(NG):
                pe.wait_ge(s_tlo, NG if g == 1 else g + 1)
                if g == 2:
                    pe.wait_ge(s_kr, 1)
                banks = (0, 1, 2) if g == 1 else (3, 4, 5)
                for n, b in enumerate(banks):
                    w = slice(P * n, P * (n + 1))
                    last = three(PS[b][:, 0:WIDTH[g]], a_whi[:, w], a_wlo[:, w], split_hi[:, COLS[g]], split_lo[:, COLS[g]])
                last.then_inc(s_q, 1)
                if g == 2:
                    pe.wait_ge(s_vc, 1)
                for t in GROUPS[g]:
                    last = three(PS[6 + g % 2][:, (t % 4) * 64:(t % 4 + 1) * 64], tile(split_hi, t), tile(split_lo, t),
                                 a_whi[:, 384:448], a_wlo[:, 384:448])
                last.then_inc(s_v, 1)

            pe.wait_ge(s_stack, 18 * 16)
            pe.wait_ge(s_kr, NG)
            pe.wait_ge(s_vc, NG)
            n_max = n_key = n_head = 0
            pending = []

            def values(n, g, h, step, first_key, last_key):
                kt, o = step
                pe.wait_ge(s_e, n + 1)
                mm(PS[5 + (g * HEADS + h) % 2][0:2 * HD, o:WIDTH[g]], VA[:, kt, h // 2, :], PT[n % 3][:, 0:WIDTH[g] - o],
                   start=first_key, stop=last_key).then_inc(s_pv, 1)

            for kind, g, h, item in schedule:
                if kind == "max":
                    t, k0, width, c = item
                    if n_max >= 3:
                        pe.wait_ge(s_mxr, n_max - 2)
                    dst = PS[n_max % 3]
                    last = mm(dst[:, 0:width], QS[h][0:96, t * P:(t + 1) * P], KS[h // 2][0:96, k0:k0 + width], start=True, stop=c < g)
                    if c == g:
                        last = mm(dst[:, width - P:width], ident_r[:], mask[:, 0:P], start=False, stop=True)
                    last.then_inc(s_mx, 1)
                    n_max += 1
                elif kind == "rows":
                    pe.wait_ge(s_m, g + 1)
                    for t in GROUPS[g]:
                        last = nc.tensor.transpose(tile(PS[7], t % 4), R[4][:, (t % 4) * P:(t % 4 + 1) * P], ident[:])
                    last.then_inc(s_mt, 1)
                elif kind == "key":
                    kt, o = item
                    if kt == 0 and h == 0:
                        pe.wait_ge(s_mrow, g + 1)
                    if n_key >= 2:
                        pe.wait_ge(s_e, n_key - 1)
                    dst = PS[3 + n_key % 2]
                    diagonal = kt >= 4 * g
                    last = mm(dst[:, 0:WIDTH[g] - o], KS[h // 2][:, kt * P:(kt + 1) * P], QS[h][:, 512 * g + o:512 * g + WIDTH[g]],
                              start=True, stop=not diagonal)
                    if diagonal:
                        last = mm(dst[:, 0:P], ident_r[:], mask[:, P:2 * P], start=False, stop=True)
                    last.then_inc(s_sc, 1)
                    if kt == 0 and n_head >= 2:
                        pe.wait_ge(s_y, n_head - 1)
                    if len(pending) > 0:
                        values(*pending.pop(0))
                    pending.append((n_key, g, h, item, kt == 0, kt == GROUPS[g][-1]))
                    n_key += 1
                else:
                    values(*pending.pop(0))
                    n_head += 1
            for g in range(NG):
                pe.wait_ge(s_y, HEADS * (g + 1))
                if g == 0:
                    pe.wait_ge(s_mxr, n_max)
                for t in GROUPS[g]:
                    last = mm(tile(PS[g], t % 4), tile(YT, t), a_wo[:], start=True, stop=True)
                last.then_inc(s_wo, 1)
            transpose_operand(1)
            pe.wait_ge(s_tlo, 2 * NG)
            pe.wait_ge(s_y, NG * HEADS)
            for t in range(NT):
                last = three(PS[6][:, t * 8:t * 8 + 8], tile(split_hi, t), tile(split_lo, t), a_rhi[:], a_rlo[:])
            last.then_inc(s_lgp, 1)

            def moe_pair(i, e0):
                def ups(s, g):
                    u = 3 * s + g
                    if g == 0:
                        pe.wait_ge(s_mlo, e0 + (s + 1))
                    for j in range(3):
                        n = 3 * u + j
                        pe.wait_ge(s_mh, i * 18 + (n + 1))
                        for b in (0, 2):
                            w = slice(HID * (b // 2) + P * j, HID * (b // 2) + P * (j + 1))
                            last = three(PS[b + n % 2][:, 0:WIDTH[g]], w_hi[s][:, w], w_lo[s][:, w], split_hi[:, COLS[g]], split_lo[:, COLS[g]])
                        last.then_inc(s_mp, 1)

                def down(s, g):
                    u = 3 * s + g
                    if g == 0:
                        pe.wait_ge(s_w2[s], i * 16 + 16)
                    pe.wait_ge(s_mh, i * 18 + (3 * u + 5))
                    pe.wait_ge(s_ma, i * 6 + (u + 2))
                    for t in GROUPS[g]:
                        for j in range(3):
                            last = mm(tile(PS[4 + u % 2], t % 4), tile(HB[u % 2][j], t % 4), w2[s][:, j * P:(j + 1) * P],
                                      start=j == 0, stop=j == 2)
                    last.then_inc(s_my, 1)

                units = [(s, g) for s in range(2) for g in range(NG)]
                for n, unit in enumerate(units):
                    ups(*unit)
                    if n > 0:
                        down(*units[n - 1])
                down(*units[-1])

            with pe.Fori(0, E1 // 2 - 1) as i:
                moe_pair(i, i * 2)
            moe_pair(E1 // 2 - 1, E1 - 2)

            pe.wait_ge(s_reload, 16)
            pe.wait_ge(s_ma, 3 * E1 + 3)
            aggregate(2, False)
            mix(2, None)

            def bias_term(n, experts):
                pe.wait_ge(s_wgt, n + 1)
                for g in range(NG):
                    for t in GROUPS[g]:
                        last = mm(PS[g][0:experts, (t % 4) * P:(t % 4 + 1) * P], wgt[:, t, 0:experts], ident[:], start=True, stop=True)
                    last.then_inc(s_wt, 1)
                for g in range(NG):
                    pe.wait_ge(s_wtc, NG * n + g + 1)
                    for t in GROUPS[g]:
                        last = mm(tile(PS[3 + g], t % 4), R[3][0:experts, t * P:(t + 1) * P], b3[0:experts, n, :], start=True, stop=True)
                    last.then_inc(s_b3, 1)

            def expert_pair(n, i, e0):
                sems = s_exp[n]

                def one(s, g):
                    u = 3 * s + g
                    if g == 0:
                        pe.wait_ge(sems["w1_lo"], e0 + (s + 1))
                    three(PS[u % 2][:, 0:WIDTH[g]], w_hi[s][:, 0:P], w_lo[s][:, 0:P], split_hi[:, COLS[g]], split_lo[:, COLS[g]]).then_inc(sems["product1"], 1)

                def two(s, g):
                    u = 3 * s + g
                    pe.wait_ge(sems["hidden1"], i * 6 + (u + 1))
                    mm(PS[2 + u % 2][:, 0:WIDTH[g]], w2[s][:, P:2 * P], HB[u % 2][0][:, 0:WIDTH[g]], start=True, stop=True).then_inc(sems["product2"], 1)

                def last_layer(s, g):
                    u = 3 * s + g
                    pe.wait_ge(sems["hidden2"], i * 6 + (u + 1))
                    pe.wait_ge(sems["accumulated"], i * 6 + (u + 2))
                    for t in GROUPS[g]:
                        last = mm(tile(PS[4 + u % 2], t % 4), tile(HB[u % 2][1], t % 4), w2[s][:, 2 * P:3 * P], start=True, stop=True)
                    last.then_inc(sems["product3"], 1)

                units = [(s, g) for s in range(2) for g in range(NG)]
                for m in range(len(units) + 2):
                    if m < len(units):
                        one(*units[m])
                    if 0 <= m - 1 < len(units):
                        two(*units[m - 1])
                    if m >= 2:
                        last_layer(*units[m - 2])

            transpose_operand(2)
            pe.wait_ge(s_tlo, 3 * NG)
            pe.wait_ge(s_xup, 1)
            pe.wait_ge(s_wlo, 3)
            for g in range(NG):
                three(PS[3 + g][:, 0:WIDTH[g]], r2_hi[:], r2_lo[:], split_hi[:, COLS[g]], split_lo[:, COLS[g]]).then_inc(s_hid, 1)
            for t in range(NT):
                if t % 4 == 0:
                    pe.wait_ge(s_hidc, t // 4 + 1)
                last = mm(PS[6][:, t * 8:t * 8 + E2], R[1][0:64, t * P:(t + 1) * P], r2_w2[0:64, 0:E2], start=True, stop=True)
            last.then_inc(s_lgp, 1)
            bias_term(0, E2)
            pe.wait_ge(s_xup, 2)
            with pe.Fori(0, E2 // 2 - 1) as i:
                expert_pair(0, i, i * 2)
            expert_pair(0, E2 // 2 - 1, E2 - 2)

            pe.wait_ge(s_exp[0]["accumulated"], 3 * E2 + 3)
            aggregate(3, False)
            mix(3, 2)
            transpose_operand(3)
            pe.wait_ge(s_tlo, 4 * NG)
            for t in range(NT):
                last = three(PS[6][:, t * 8:t * 8 + 8], tile(split_hi, t), tile(split_lo, t), r3_hi[:], r3_lo[:])
            last.then_inc(s_lgp, 1)
            bias_term(1, E3)
            pe.wait_ge(s_xup, 4)
            with pe.Fori(0, E3 // 2 - 1) as i:
                expert_pair(1, i, i * 2)
            expert_pair(1, E3 // 2 - 1, E3 - 2)

        @block.scalar
        def _(act):
            order = [0]

            def link(ins):
                order[0] += 1
                ins.then_inc(s_act, 1)
                act.wait_ge(s_act, order[0])

            for k in range(NT):
                act.wait_ge(s_adj[k % 4], 16 * (k // 4 + 1))
                nc.scalar.activation(adj_hi[:, k, :], R[k % 4][:], ACT.Copy).then_inc(s_adj_hi, 1)
            act.wait_ge(s_deg_row, 1)
            for g in range(NG):
                ins = nc.scalar.activation(R[4][0:1, COLS[g]], PS[g][0:1, 0:WIDTH[g]], ACT.Copy)
            ins.then_inc(s_deg_sb, 1)

            def hi_part(n):
                for g in range(NG):
                    act.wait_ge(s_feat, NG * n + g + 1)
                    nc.scalar.activation(split_hi[:, COLS[g]], R[0][:, COLS[g]], ACT.Copy).then_inc(s_hi, 1)

            def copy_aggregate(q):
                for g in range(NG):
                    act.wait_ge(s_agg, NG * q + g + 1)
                    if q == 2:
                        ins = nc.scalar.activation(R[1][:, COLS[g]], PS[g][:, 0:WIDTH[g]], ACT.Identity, scale=l2_scale[:, 0:1])
                    else:
                        ins = nc.scalar.activation(R[1][:, COLS[g]], PS[g][:, 0:WIDTH[g]], ACT.Copy)
                    ins.then_inc(s_aggt, 1)

            hi_part(0)
            copy_aggregate(0)
            for g in range(NG):
                act.wait_ge(s_relu, g + 1)
                for t in GROUPS[g]:
                    ins = nc.scalar.activation(tile(R[3], t), tile(R[2], t), ACT.Square, accum_out=ssq[:, t:t + 1])
                ins.then_inc(s_ssq, 1)
            nc.scalar.preload_act_table(ACT.Sigmoid)

            def slot(place, count, valid):
                if valid(3):
                    c = FCOLS[place(3)]
                    act.wait_ge(s_h1, count(3))
                    nc.scalar.activation(R[1][:, c], R[0][:, c], ACT.Sigmoid, scale=1 / GAIN).then_inc(s_sg, 1)
                if valid(4):
                    c = FCOLS[place(4)]
                    act.wait_ge(s_h, count(4))
                    nc.scalar.activation(R[1][:, c], R[0][:, c], ACT.Tanh, scale=1 / GAIN).then_inc(s_t, 1)
                if valid(2):
                    g = place(2)
                    act.wait_ge(s_tr, count(2))
                    nc.scalar.activation(R[2][:, FCOLS[g]], PS[g][:, 0:P * len(FG[g])], ACT.Copy).then_inc(s_ht, 1)

            recurrent_slots(act, slot)
            hi_part(1)
            copy_aggregate(1)
            for g in range(NG):
                act.wait_ge(s_pre, g + 1)
                nc.scalar.activation(R[2][:, COLS[g]], R[2][:, COLS[g]], ACT.Tanh).then_inc(s_tanh1, 1)

            def squares(n):
                for g in range(NG):
                    if n == 0:
                        act.wait_ge(s_xn, g + 1)
                    else:
                        act.wait_ge(s_x2, g + 1)
                    for t in GROUPS[g]:
                        ins = nc.scalar.activation(tile(R[1], t), tile(xn, t), ACT.Square, accum_out=ssq[:, t:t + 1])
                    ins.then_inc(s_sq3, 1)

            def operand_hi(n):
                for g in range(NG):
                    act.wait_ge(s_tt, NG * n + g + 1)
                    nc.scalar.activation(split_hi[:, COLS[g]], PS[g][:, 0:WIDTH[g]], ACT.Copy).then_inc(s_thi, 1)

            act.wait_ge(s_small2, 16 * len(SMALL2))
            nc.scalar.activation(a_whi[:], a_w[:], ACT.Copy, scale=a_ln1[:, 0:1])
            nc.scalar.activation(a_rhi[:], a_router[:], ACT.Copy, scale=a_ln2[:, 0:1])
            nc.scalar.activation(r2_hi[:], r2_w1[:], ACT.Copy)
            nc.scalar.activation(r3_hi[:], r3_w[:], ACT.Copy).then_inc(s_whi, 1)
            squares(0)
            operand_hi(0)
            for g in range(NG):
                act.wait_ge(s_qr, g + 1)
                nc.scalar.activation(QH[:, COLS[g]], R[1][:, COLS[g]], ACT.Copy).then_inc(s_qh, 1)
                act.wait_ge(s_kr, g + 1)
                nc.scalar.activation(KHL[0:64, COLS[g]], R[2][0:64, COLS[g]], ACT.Copy).then_inc(s_kh, 1)
                act.wait_ge(s_v, g + 1)
                n = len(GROUPS[g])
                nc.scalar.activation(VA[:, 4 * g:4 * g + n, :, 0:HD],
                                     PS[6 + g % 2][:, 0:64 * n].rearrange("p (t v c) -> p t v c", v=KV_HEADS, c=HD), ACT.Copy).then_inc(s_vc, 1)
            n_key = 0
            for kind, g, h, item in schedule:
                if kind == "rows":
                    act.wait_ge(s_mt, g + 1)
                    if g == 0:
                        act.wait_ge(s_stack, 18 * 16)
                    for hh in range(HEADS):
                        ins = nc.scalar.activation(QS[hh][96:128, COLS[g]], PS[7][HD * hh:HD * (hh + 1), 0:WIDTH[g]], ACT.Copy)
                    ins.then_inc(s_mrow, 1)
                elif kind == "key":
                    kt, o = item
                    act.wait_ge(s_sc, n_key + 1)
                    if n_key >= 3:
                        act.wait_ge(s_pv, n_key - 2)
                    nc.scalar.activation(PT[n_key % 3][:, 0:WIDTH[g] - o], PS[3 + n_key % 2][:, 0:WIDTH[g] - o], ACT.Exp,
                                         scale=float(HD) ** -0.5).then_inc(s_e, 1)
                    n_key += 1
            squares(1)
            operand_hi(1)

            def router_exp(n):
                act.wait_ge(s_lg, n + 1)
                nc.scalar.activation(probs[:], lg[:], ACT.Exp).then_inc(s_ex, 1)

            router_exp(0)

            nc.scalar.preload_act_table(ACT.Silu)

            def split_moe(s, count):
                act.wait_ge(s_raw, count)
                nc.scalar.activation(w_hi[s][:], w_raw, ACT.Copy, scale=a_ln2[:, 0:1]).then_inc(s_mhi, 1)

            def moe_pair(i, e0, last):
                for s in range(2):
                    for g in range(NG):
                        for j in range(3):
                            n = 9 * s + 3 * g + j
                            act.wait_ge(s_mp, i * 18 + (n + 1))
                            nc.scalar.activation(SB[n % 2][:, 0:WIDTH[g]], PS[n % 2][:, 0:WIDTH[g]], ACT.Silu).then_inc(s_ms, 1)
                        if g == 0 and not (last and s == 1):
                            split_moe(1 - s, (e0 + (s + 2)) * 16)

            split_moe(0, 16)
            with act.Fori(0, E1 // 2 - 1) as i:
                moe_pair(i, i * 2, False)
            moe_pair(E1 // 2 - 1, E1 - 2, True)
            hi_part(2)
            copy_aggregate(2)

            def expert_pair(n, i, e0, last):
                sems = s_exp[n]

                def hidden(layer, s, g):
                    u = 3 * s + g
                    act.wait_ge(sems[f"product{layer}"], i * 6 + (u + 1))
                    nc.scalar.activation(HB[u % 2][layer - 1][:, 0:WIDTH[g]], PS[2 * (layer - 1) + u % 2][:, 0:WIDTH[g]], ACT.Relu,
                                         scale=pcol[s][:, 2 * layer - 2:2 * layer - 1], bias=pcol[s][:, 2 * layer - 1:2 * layer]).then_inc(sems[f"hidden{layer}"], 1)

                units = [(s, g) for s in range(2) for g in range(NG)]
                for m in range(len(units) + 1):
                    if m < len(units):
                        hidden(1, *units[m])
                    if m >= 1:
                        hidden(2, *units[m - 1])
                    if m in (0, 3) and not (last and m == 3):
                        s = 1 - m // 3
                        split_expert(n, s, i * 16 + 16 * (2 - s))

            def split_expert(n, s, count):
                sems = s_exp[n]
                act.wait_ge(sems["odd_loaded" if s else "even_loaded"], count)
                nc.scalar.activation(w_hi[s][:, 0:P], w2[s][:, 0:P], ACT.Copy).then_inc(sems["w1_hi"], 1)

            def transposed_weights(n, experts):
                for g in range(NG):
                    act.wait_ge(s_wt, NG * n + g + 1)
                    nc.scalar.activation(R[3][0:experts, COLS[g]], PS[g][0:experts, 0:WIDTH[g]], ACT.Copy).then_inc(s_wtc, 1)

            operand_hi(2)
            for g in range(NG):
                act.wait_ge(s_hid, g + 1)
                nc.scalar.activation(R[1][:, COLS[g]], PS[3 + g][:, 0:WIDTH[g]], ACT.Relu, bias=r2_b1[:, 0:1]).then_inc(s_hidc, 1)
            router_exp(1)
            act.wait_ge(s_m2, 1)
            nc.scalar.activation(rt[:, 5, :], rt[:, 4, :], ACT.Exp).then_inc(s_e2, 1)
            transposed_weights(0, E2)
            split_expert(0, 0, 16)
            with act.Fori(0, E2 // 2 - 1) as i:
                expert_pair(0, i, i * 2, False)
            expert_pair(0, E2 // 2 - 1, E2 - 2, True)
            hi_part(3)
            copy_aggregate(3)
            operand_hi(3)
            router_exp(2)
            transposed_weights(1, E3)
            split_expert(1, 0, 16)
            with act.Fori(0, E3 // 2 - 1) as i:
                expert_pair(1, i, i * 2, False)
            expert_pair(1, E3 // 2 - 1, E3 - 2, True)

        @block.gpsimd
        def _(pool):
            order = [0]

            def link(ins):
                order[0] += 1
                ins.then_inc(s_pool, 1)
                pool.wait_ge(s_pool, order[0])

            nc.gpsimd.memset(power[:], -0.5)
            nc.gpsimd.memset(eps_h[:], EPS_LN * GAIN * GAIN)
            nc.gpsimd.memset(ones[:], 1.0)
            link(nc.gpsimd.memset(mean_w[:], 1 / P))
            nc.gpsimd.memset(f0_lnb_b[:], 1.0).then_inc(s_consts, 1)

            def rstd(n, scale=None):
                for g in range(NG):
                    c = slice(GROUPS[g][0], GROUPS[g][-1] + 1)
                    pool.wait_ge(s_var, NG * n + g + 1)
                    link(nc.gpsimd.tensor_scalar(rs[:, c], mv[:, c, 1], EPS_LN, None, ALU.add))
                    if scale is None:
                        nc.gpsimd.tensor_tensor(rss[:, c], rs[:, c], power[:, c], ALU.pow).then_inc(s_rstd, 1)
                        continue
                    link(nc.gpsimd.tensor_tensor(rs[:, c], rs[:, c], power[:, c], ALU.pow))
                    if scale is dinv and g == 0:
                        pool.wait_ge(s_deg, 1)
                        nc.gpsimd.tensor_tensor(dinv[:], deg1[:], power[:], ALU.pow).then_inc(s_dinv, 1)
                        pool.wait_ge(s_dinv, 1)
                    if isinstance(scale, float):
                        ins = nc.gpsimd.tensor_scalar(rss[:, c], rs[:, c], scale, None, ALU.mult)
                    else:
                        ins = nc.gpsimd.tensor_tensor(rss[:, c], rs[:, c], scale[:, c], ALU.mult)
                    ins.then_inc(s_rstd, 1)

            rstd(0, dinv)
            nc.gpsimd.tensor_tensor(sinv[:], deg[:], power[:], ALU.pow).then_inc(s_dinv, 1)
            for g in range(NG):
                c = slice(GROUPS[g][0], GROUPS[g][-1] + 1)
                pool.wait_ge(s_ssq, g + 1)
                link(nc.gpsimd.tensor_scalar(ssq[:, c], ssq[:, c], 1e-24, None, ALU.max))
                nc.gpsimd.tensor_tensor(rnorm[:, c], ssq[:, c], power[:, c], ALU.pow).then_inc(s_rnorm, 1)
            rstd(1, GAIN)

            def slot(place, count, valid):
                if valid(1):
                    g = place(1)
                    c = slice(FG[g][0], FG[g][-1] + 1)
                    pool.wait_ge(s_hv, count(1))
                    nc.gpsimd.tensor_tensor(rs[:, c], mv[:, c, 1], eps_h[:, c], ALU.add).then_inc(s_ve, 1)
                    pool.wait_ge(s_ve, count(1))
                    nc.gpsimd.tensor_tensor(rss[:, c], rs[:, c], power[:, c], ALU.pow).then_inc(s_hr, 1)
                if valid(4):
                    c = FCOLS[place(4)]
                    pool.wait_ge(s_t, count(4))
                    nc.gpsimd.tensor_tensor(R[0][:, c], R[0][:, c], R[1][:, c], ALU.add).then_inc(s_h1, 1)

            recurrent_slots(pool, slot)
            rstd(2)

            def rms(n):
                for g in range(NG):
                    c = slice(GROUPS[g][0], GROUPS[g][-1] + 1)
                    pool.wait_ge(s_sq3, NG * n + g + 1)
                    link(nc.gpsimd.tensor_scalar(ssq[:, c], ssq[:, c], 1 / P, EPS_RMS, ALU.mult, ALU.add))
                    nc.gpsimd.tensor_tensor(rnorm[:, c], ssq[:, c], power[:, c], ALU.pow).then_inc(s_rms, 1)

            rstd(3)
            rms(0)
            pool.wait_ge(s_small2, 16 * len(SMALL2))
            for v in (3, 8):
                link(nc.gpsimd.tensor_scalar(bn[:, v, :], bn[:, v, :], EPS_BN, None, ALU.add))
                nc.gpsimd.tensor_tensor(bn[:, v, :], bn[:, v, :], power[:, 0:8], ALU.pow).then_inc(s_bnr, 1)
            rms(1)
            rstd(4)
            rstd(5)
            rstd(6, sinv)
            rstd(7)

        @block.vector
        def _(dve):
            order = [0]

            def link(ins):
                order[0] += 1
                ins.then_inc(s_dve, 1)
                dve.wait_ge(s_dve, order[0])

            def adj_tile(k):
                dve.wait_ge(s_adj_hi, k + 1)
                nc.vector.tensor_tensor(adj_lo[:, k, :], R[k % 4][:], adj_hi[:, k, :].bitcast(F32), ALU.subtract).then_inc(s_adj_lo, 1)

            def norm_stats(src):
                for t in range(NT):
                    ins = nc.vector.bn_stats(stats[:, t, :], tile(src, t))
                link(ins)
                for g in range(NG):
                    for t in GROUPS[g]:
                        ins = nc.vector.bn_aggr(mv[:, t, :], stats[:, t, :])
                    ins.then_inc(s_var, 1)

            def normalise(dst, n, ready, groups=GROUPS):
                for group in groups:
                    dve.wait_ge(s_rstd, NG * n + group[-1] // 4 + 1)
                    for t in group:
                        ins = nc.vector.tensor_scalar(tile(dst, t), tile(x, t), mv[:, t, 0:1], rss[:, t:t + 1], ALU.subtract, ALU.mult)
                    ins.then_inc(ready, 1)

            def lo_part(n):
                for g in range(NG):
                    dve.wait_ge(s_hi, NG * n + g + 1)
                    nc.vector.tensor_tensor(split_lo[:, COLS[g]], R[0][:, COLS[g]], split_hi[:, COLS[g]].bitcast(F32), ALU.subtract).then_inc(s_lo, 1)

            def operand_lo(n):
                for g in range(NG):
                    dve.wait_ge(s_thi, NG * n + g + 1)
                    nc.vector.tensor_tensor(split_lo[:, COLS[g]], PS[g][:, 0:WIDTH[g]], split_hi[:, COLS[g]].bitcast(F32), ALU.subtract).then_inc(s_tlo, 1)

            def times_rms(n):
                for g in range(NG):
                    dve.wait_ge(s_rms, NG * n + g + 1)
                    for t in GROUPS[g]:
                        ins = nc.vector.tensor_scalar(tile(R[0], t), tile(xn, t), rnorm[:, t:t + 1], None, ALU.mult)
                    ins.then_inc(s_tin, 1)

            def over(small, experts):
                return small.unsqueeze(2).to_broadcast([P, NT, experts])

            def softmax(n, experts, bias):
                dve.wait_ge(s_lgp, n + 1)
                src = PS[6][:, 0:NT * 8].rearrange("p (t e) -> p t e", e=8)[:, :, 0:experts]
                l, p = lg[:, :, 0:experts], probs[:, :, 0:experts]
                if bias is None:
                    link(nc.vector.tensor_copy(l, src))
                else:
                    link(nc.vector.tensor_tensor(l, src, bias[:, 0:experts].unsqueeze(1).to_broadcast([P, NT, experts]), ALU.add))
                link(nc.vector.tensor_reduce(rt[:, 0, :], l, AX.X, ALU.max))
                nc.vector.tensor_tensor(l, l, over(rt[:, 0, :], experts), ALU.subtract).then_inc(s_lg, 1)
                dve.wait_ge(s_ex, n + 1)
                link(nc.vector.tensor_reduce(rt[:, 0, :], p, AX.X, ALU.add))
                link(nc.vector.reciprocal(rt[:, 1, :], rt[:, 0, :]))
                link(nc.vector.tensor_tensor(p, p, over(rt[:, 1, :], experts), ALU.mult))

            def best(onehot, src, experts, value):
                sc = score[:, :, 0:experts]
                link(nc.vector.tensor_reduce(rt[:, value, :], src, AX.X, ALU.max))
                link(nc.vector.tensor_tensor(sc, src, over(rt[:, value, :], experts), ALU.is_equal))
                link(nc.vector.tensor_tensor(sc, sc, descend[:, 0:experts].unsqueeze(1).to_broadcast([P, NT, experts]), ALU.mult))
                link(nc.vector.tensor_reduce(rt[:, 0, :], sc, AX.X, ALU.max))
                link(nc.vector.tensor_tensor(onehot, sc, over(rt[:, 0, :], experts), ALU.is_equal))

            def top2(experts):
                f, s2, l, p = (b[:, :, 0:experts] for b in (first, second, lg, probs))
                best(f, p, experts, 2)
                link(nc.vector.scalar_tensor_tensor(l, f, -2.0, p, ALU.mult, ALU.add))
                best(s2, l, experts, 3)

            def accumulate(dst_bank, s, g):
                for t in GROUPS[g]:
                    ins = nc.vector.scalar_tensor_tensor(tile(x, t), tile(dst_bank, t % 4), wcol[s][:, t:t + 1], tile(x, t), ALU.mult, ALU.add)
                return ins

            def later_layers():
                dve.wait_ge(s_small2, 16 * len(SMALL2))
                dve.wait_ge(s_whi, 1)
                nc.vector.scalar_tensor_tensor(a_wlo[:], a_w[:], a_ln1[:, 0:1], a_whi[:].bitcast(F32), ALU.mult, ALU.subtract).then_inc(s_wlo, 1)
                nc.vector.scalar_tensor_tensor(a_rlo[:], a_router[:], a_ln2[:, 0:1], a_rhi[:].bitcast(F32), ALU.mult, ALU.subtract)
                nc.vector.tensor_tensor(r2_lo[:], r2_w1[:], r2_hi[:].bitcast(F32), ALU.subtract).then_inc(s_wlo, 1)
                nc.vector.tensor_tensor(r3_lo[:], r3_w[:], r3_hi[:].bitcast(F32), ALU.subtract).then_inc(s_wlo, 1)
                nc.vector.tensor_copy(mask[:], mask_f[:])
                norm_stats(x)
                normalise(xn, 3, s_xn)
                times_rms(0)
                operand_lo(0)
                dve.wait_ge(s_trig, 32)
                dve.wait_ge(s_adj_out, 16)
                for g in range(NG):
                    bq, br, bk = (0, 1, 2) if g == 1 else (3, 4, 5)
                    w, c = WIDTH[g], COLS[g]
                    dve.wait_ge(s_q, g + 1)
                    nc.vector.tensor_tensor(R[1][:, c], PS[bq][:, 0:w], R[3][:, c], ALU.mult)
                    link(nc.vector.tensor_tensor(R[2][:, c], PS[br][:, 0:w], R[4][:, c], ALU.mult))
                    nc.vector.tensor_tensor(R[1][:, c], R[1][:, c], R[2][:, c], ALU.add).then_inc(s_qr, 1)
                    nc.vector.tensor_tensor(k_scratch[:, 0:w], PS[bk][0:64, 0:w], R[3][0:64, c], ALU.mult)
                    dve.wait_ge(s_qr, g + 1)
                    link(nc.vector.tensor_tensor(R[2][0:64, c], PS[bk][64:128, 0:w], R[4][64:128, c], ALU.mult))
                    nc.vector.tensor_tensor(R[2][0:64, c], R[2][0:64, c], k_scratch[:, 0:w], ALU.add).then_inc(s_kr, 1)
                    dve.wait_ge(s_qh, g + 1)
                    nc.vector.tensor_tensor(QL[:, c], R[1][:, c], QH[:, c].bitcast(F32), ALU.subtract).then_inc(s_ql, 1)
                    dve.wait_ge(s_kh, g + 1)
                    nc.vector.tensor_tensor(KHL[64:128, c], R[2][0:64, c], KHL[0:64, c].bitcast(F32), ALU.subtract).then_inc(s_kl, 1)
                for v in range(KV_HEADS):
                    nc.vector.tensor_scalar(KS[v][96:128, :], ones[96:128, 0:1].to_broadcast([32, TP]), k_pad[96:128, 0:1], None, ALU.mult)
                dve.wait_ge(s_tt, NG)
                nc.vector.memset(VA[:, :, :, HD:2 * HD], 1.0)
                dve.wait_ge(s_kl, NG)
                link(nc.vector.memset(R[4][:, 0:512], 0.0))
                n_max = n_head = 0
                for kind, g, h, item in schedule:
                    if kind == "max":
                        t, k0, width, c = item
                        dve.wait_ge(s_mx, n_max + 1)
                        nc.vector.tensor_reduce(mxc[:, t * HEADS + h, c:c + 1], PS[n_max % 3][:, 0:width], AX.X, ALU.max).then_inc(s_mxr, 1)
                        n_max += 1
                    elif kind == "rows":
                        n = len(GROUPS[g]) * HEADS
                        dve.wait_ge(s_mxr, n_max)
                        link(nc.vector.tensor_reduce(m_neg[:, 0:n], mxc[:, 4 * g * HEADS:4 * g * HEADS + n, 0:g + 1], AX.X, ALU.max))
                        link(nc.vector.tensor_scalar(m_hi[:, 0:n], m_neg[:, 0:n], -1.0, None, ALU.mult))
                        if g > 0:
                            dve.wait_ge(s_mt, g)
                        nt = len(GROUPS[g])
                        hi3 = m_hi[:, 0:n].bitcast(F32).rearrange("p (t h) -> p t h", h=HEADS)
                        nc.vector.tensor_copy(MT[:, 0:nt, :, 0], hi3)
                        nc.vector.scalar_tensor_tensor(MT[:, 0:nt, :, 1], m_neg[:, 0:n].rearrange("p (t h) -> p t h", h=HEADS), -1.0, hi3,
                                                       ALU.mult, ALU.subtract).then_inc(s_m, 1)
                    elif kind == "key":
                        continue
                    else:
                        dve.wait_ge(s_pv, sum(len(list(key_steps(gg))) for gg in range(g)) * HEADS + len(list(key_steps(g))) * (h + 1))
                        bank = PS[5 + n_head % 2]
                        if n_head > 0:
                            dve.wait_ge(s_y, n_head)
                        link(nc.vector.reciprocal(RL[:, 0:WIDTH[g]], bank[HD:2 * HD, 0:WIDTH[g]]))
                        nc.vector.tensor_tensor(YT[HD * h:HD * (h + 1), COLS[g]], bank[0:HD, 0:WIDTH[g]], RL[:, 0:WIDTH[g]], ALU.mult).then_inc(s_y, 1)
                        n_head += 1
                for g in range(NG):
                    dve.wait_ge(s_wo, g + 1)
                    nc.vector.tensor_tensor(xn[:, COLS[g]], xn[:, COLS[g]], PS[g][:, 0:WIDTH[g]], ALU.add).then_inc(s_x2, 1)
                dve.wait_ge(s_x2, NG)
                link(nc.vector.tensor_tensor(x[:], x[:], xn[:], ALU.add))
                times_rms(1)
                operand_lo(1)
                softmax(0, E1, None)
                top2(E1)
                link(nc.vector.tensor_tensor(rt[:, 4, :], rt[:, 2, :], rt[:, 3, :], ALU.add))
                link(nc.vector.tensor_scalar(rt[:, 4, :], rt[:, 4, :], 1e-9, None, ALU.add))
                link(nc.vector.reciprocal(rt[:, 5, :], rt[:, 4, :]))
                link(nc.vector.tensor_tensor(wgt[:], first[:], over(rt[:, 2, :], E1), ALU.mult))
                link(nc.vector.tensor_tensor(second[:], second[:], over(rt[:, 3, :], E1), ALU.mult))
                link(nc.vector.tensor_tensor(wgt[:], wgt[:], second[:], ALU.add))
                link(nc.vector.tensor_tensor(wgt[:], wgt[:], over(rt[:, 5, :], E1), ALU.mult))
                nc.vector.engine_nop().then_inc(s_mh, 2)
                nc.vector.engine_nop().then_inc(s_my, 2)
                nc.vector.engine_nop().then_inc(s_ma, 3)

                def split_moe(s, count):
                    dve.wait_ge(s_mhi, count)
                    nc.vector.scalar_tensor_tensor(w_lo[s][:], w_raw, a_ln2[:, 0:1], w_hi[s][:].bitcast(F32), ALU.mult, ALU.subtract).then_inc(s_mlo, 1)

                def moe_pair(i, e0, last):
                    def hidden(s, g):
                        u = 3 * s + g
                        for j in range(3):
                            n = 3 * u + j
                            dve.wait_ge(s_ms, i * 18 + (n + 1))
                            dve.wait_ge(s_my, i * 6 + (u + 1))
                            nc.vector.tensor_tensor(HB[u % 2][j][:, 0:WIDTH[g]], SB[n % 2][:, 0:WIDTH[g]], PS[2 + n % 2][:, 0:WIDTH[g]],
                                                    ALU.mult).then_inc(s_mh, 1)

                    def sums(s, g):
                        u = 3 * s + g
                        if g == 0:
                            dve.wait_ge(s_ma, i * 6 + (u + 1))
                            nc.vector.tensor_copy(wcol[s][:].unsqueeze(2), wgt[:, :, bass.ds(e0 + s, 1)]).then_inc(s_wcol, 1)
                            dve.wait_ge(s_wcol, e0 + (s + 1))
                        dve.wait_ge(s_my, i * 6 + (u + 3))
                        dve.wait_ge(s_ma, i * 6 + (u + 1))
                        accumulate(PS[4 + u % 2], s, g).then_inc(s_ma, 1)

                    units = [(s, g) for s in range(2) for g in range(NG)]
                    for n, unit in enumerate(units):
                        hidden(*unit)
                        if unit[1] == 0 and not (last and unit[0] == 1):
                            split_moe(1 - unit[0], e0 + (unit[0] + 2))
                        if n > 0:
                            sums(*units[n - 1])
                    sums(*units[-1])

                split_moe(0, 1)
                with dve.Fori(0, E1 // 2 - 1) as i:
                    moe_pair(i, i * 2, False)
                moe_pair(E1 // 2 - 1, E1 - 2, True)
                dve.wait_ge(s_ma, 3 * E1 + 3)
                norm_stats(x)
                normalise(R[0], 4, s_feat)
                lo_part(2)
                for g in range(NG):
                    dve.wait_ge(s_mix, 2 * NG + g + 1)
                    ins = nc.vector.tensor_tensor(x[:, COLS[g]], x[:, COLS[g]], PS[3 + g][:, 0:WIDTH[g]], ALU.add)
                ins.then_inc(s_xup, 1)
                dve.wait_ge(s_xup, 1)

                def add_bias_term(n):
                    for g in range(NG):
                        dve.wait_ge(s_b3, NG * n + g + 1)
                        ins = nc.vector.tensor_tensor(x[:, COLS[g]], x[:, COLS[g]], PS[3 + g][:, 0:WIDTH[g]], ALU.add)
                    return ins

                def experts_layer(n, experts, par):
                    sems = s_exp[n]

                    def split_expert(e, s, count):
                        nc.vector.tensor_copy(pcol[s][:].unsqueeze(2), par[:, :, bass.ds(e, 1)])
                        nc.vector.tensor_copy(wcol[s][:].unsqueeze(2), wgt[:, :, bass.ds(e, 1)])
                        dve.wait_ge(sems["w1_hi"], count)
                        nc.vector.tensor_tensor(w_lo[s][:, 0:P], w2[s][:, 0:P], w_hi[s][:, 0:P].bitcast(F32), ALU.subtract).then_inc(sems["w1_lo"], 1)

                    return split_expert

                def run_experts(n, experts, par):
                    sems = s_exp[n]
                    split_expert = experts_layer(n, experts, par)
                    nc.vector.engine_nop().then_inc(sems["accumulated"], 3)
                    split_expert(0, 0, 1)

                    def both(i, e0, last):
                        dve.wait_ge(sems["accumulated"], i * 6 + 3)
                        split_expert(e0 + 1, 1, e0 + 2)
                        for u in range(6):
                            s, g = u // 3, u % 3
                            dve.wait_ge(sems["product3"], i * 6 + (u + 1))
                            dve.wait_ge(sems["accumulated"], i * 6 + (u + 1))
                            accumulate(PS[4 + u % 2], s, g).then_inc(sems["accumulated"], 1)
                            if u == 2 and not last:
                                split_wait(i, u)
                                split_expert(e0 + 2, 0, e0 + 3)

                    def split_wait(i, u):
                        dve.wait_ge(sems["accumulated"], i * 6 + (u + 4))

                    with dve.Fori(0, experts // 2 - 1) as i:
                        both(i, i * 2, False)
                    both(experts // 2 - 1, experts - 2, True)
                    dve.wait_ge(sems["accumulated"], 3 * experts + 3)

                norm_stats(x)
                normalise(R[0], 5, s_tin)
                operand_lo(2)
                softmax(1, E2, r2_b2)
                top2(E2)
                nc.vector.tensor_tensor(rt[:, 4, :], rt[:, 3, :], rt[:, 2, :], ALU.subtract).then_inc(s_m2, 1)
                dve.wait_ge(s_e2, 1)
                link(nc.vector.tensor_scalar(rt[:, 0, :], rt[:, 5, :], 1.0, None, ALU.add))
                link(nc.vector.reciprocal(rt[:, 1, :], rt[:, 0, :]))
                link(nc.vector.tensor_tensor(rt[:, 5, :], rt[:, 5, :], rt[:, 1, :], ALU.mult))
                w = wgt[:, :, 0:E2]
                link(nc.vector.tensor_tensor(w, first[:, :, 0:E2], over(rt[:, 1, :], E2), ALU.mult))
                link(nc.vector.tensor_tensor(second[:, :, 0:E2], second[:, :, 0:E2], over(rt[:, 5, :], E2), ALU.mult))
                nc.vector.tensor_tensor(w, w, second[:, :, 0:E2], ALU.add).then_inc(s_wgt, 1)
                dve.wait_ge(s_wgt, 1)
                add_bias_term(0).then_inc(s_xup, 1)
                dve.wait_ge(s_xup, 2)
                run_experts(0, E2, par2)
                norm_stats(x)
                normalise(R[0], 6, s_feat)
                lo_part(3)
                for g in range(NG):
                    dve.wait_ge(s_mix, 3 * NG + g + 1)
                    for t in GROUPS[g]:
                        ins = nc.vector.scalar_tensor_tensor(tile(x, t), tile(PS[3 + g], t % 4), sinv[:, t:t + 1], tile(x, t), ALU.mult, ALU.add)
                ins.then_inc(s_xup, 1)
                dve.wait_ge(s_xup, 3)
                dve.wait_ge(s_bnr, 2)
                for k in range(2):
                    link(nc.vector.tensor_tensor(par3[:, 2 * k, :], bn[:, 5 * k, :], bn[:, 5 * k + 3, :], ALU.mult))
                    link(nc.vector.tensor_tensor(par3[:, 2 * k + 1, :], bn[:, 5 * k + 4, :], bn[:, 5 * k + 2, :], ALU.subtract))
                    link(nc.vector.tensor_tensor(par3[:, 2 * k + 1, :], par3[:, 2 * k + 1, :], par3[:, 2 * k, :], ALU.mult))
                    link(nc.vector.tensor_tensor(par3[:, 2 * k + 1, :], par3[:, 2 * k + 1, :], bn[:, 5 * k + 1, :], ALU.add))
                norm_stats(x)
                normalise(R[0], 7, s_tin)
                operand_lo(3)
                softmax(2, E3, r3_b)
                nc.vector.tensor_copy(wgt[:], probs[:]).then_inc(s_wgt, 1)
                dve.wait_ge(s_wgt, 2)
                add_bias_term(1).then_inc(s_xup, 1)
                dve.wait_ge(s_xup, 4)
                run_experts(1, E3, par3)

            dve.wait_ge(s_consts, 1)
            nc.vector.tensor_copy(ones_r[:], ones[:]).then_inc(s_consts, 1)
            dve.wait_ge(s_small, 5 * 16)
            link(nc.vector.tensor_copy(ident_r[:], ident[:]))
            nc.vector.tensor_scalar(f0_m[:], f0_wt[:], f0_lnw[:, 0:1], None, ALU.mult).then_inc(s_f0_m, 1)
            nc.vector.tensor_scalar(f0_lnb_b[:], f0_lnb_b[:], f0_lnb[:, 0:1], None, ALU.mult).then_inc(s_f0_m, 1)
            dve.wait_ge(s_x, 16)
            norm_stats(x)
            for k in range(NT):
                adj_tile(k)
            dve.wait_ge(s_f0_mm, 1)
            link(nc.vector.tensor_tensor(f0_m[:], f0_m[:], PS[7][:, 0:P], ALU.subtract))
            link(nc.vector.tensor_tensor(f0_b[:], f0_b[:], PS[7][:, P:2 * P], ALU.add))
            nc.vector.tensor_scalar(f0_m[:], f0_m[:], GAIN, None, ALU.mult)
            nc.vector.tensor_scalar(f0_b[:], f0_b[:], GAIN, None, ALU.mult).then_inc(s_f0_w, 1)
            dve.wait_ge(s_deg_col, 1)
            nc.vector.tensor_copy(deg[:], PS[6][:, 0:NT])
            nc.vector.tensor_scalar(deg1[:], PS[6][:, 0:NT], 1.0, None, ALU.add).then_inc(s_deg, 1)
            dve.wait_ge(s_deg, 1)
            nc.vector.reciprocal(rdeg[:], deg1[:])
            normalise(R[0], 0, s_feat)
            lo_part(0)
            dve.wait_ge(s_dinv, 1)
            for g in range(NG):
                dve.wait_ge(s_mix, g + 1)
                for t in GROUPS[g]:
                    ins = nc.vector.tensor_scalar(tile(R[2], t), tile(PS[3 + g], t % 4), dinv[:, t:t + 1], 0.0, ALU.mult, ALU.max)
                ins.then_inc(s_relu, 1)
            for g in range(NG):
                dve.wait_ge(s_rnorm, g + 1)
                for t in GROUPS[g]:
                    ins = nc.vector.scalar_tensor_tensor(tile(x, t), tile(R[2], t), rnorm[:, t:t + 1], tile(x, t), ALU.mult, ALU.add)
            link(ins)
            norm_stats(x)
            normalise(R[0], 1, s_h, FG)

            def slot(place, count, valid):
                if valid(0):
                    g = place(0)
                    dve.wait_ge(s_hr, count(0))
                    dve.wait_ge(s_p, count(0))
                    for m, t in enumerate(FG[g]):
                        ins = nc.vector.scalar_tensor_tensor(tile(R[0], t), tile(PS[NF + g], m), rss[:, t:t + 1], f0_b[:], ALU.mult, ALU.add)
                    ins.then_inc(s_h, 1)
                if valid(2):
                    g = place(2)
                    dve.wait_ge(s_h2, count(2))
                    for t in FG[g]:
                        ins = nc.vector.bn_stats(stats[:, t, :], tile(R[0], t))
                    ins.then_inc(s_st, 1)
                    dve.wait_ge(s_st, count(2))
                if valid(3):
                    c = FCOLS[place(3)]
                    dve.wait_ge(s_sg, count(3))
                    nc.vector.tensor_tensor(R[0][:, c], R[0][:, c], R[1][:, c], ALU.mult).then_inc(s_h2, 1)
                if valid(2):
                    for t in FG[place(2)]:
                        ins = nc.vector.bn_aggr(mv[:, t, :], stats[:, t, :])
                    ins.then_inc(s_hv, 1)

            recurrent_slots(dve, slot)
            dve.wait_ge(s_h, NF * (ITERS + 1))
            link(nc.vector.scalar_tensor_tensor(x[:], R[0][:], 1 / GAIN, x[:], ALU.mult, ALU.add))
            norm_stats(x)
            normalise(R[0], 2, s_feat)
            lo_part(1)
            for g in range(NG):
                dve.wait_ge(s_mix, NG + g + 1)
                for t in GROUPS[g]:
                    ins = nc.vector.scalar_tensor_tensor(tile(R[2], t), tile(PS[3 + g], t % 4), rdeg[:, t:t + 1], l1_bias[:], ALU.mult, ALU.add)
                ins.then_inc(s_pre, 1)
            for g in range(NG):
                dve.wait_ge(s_tanh1, g + 1)
                ins = nc.vector.tensor_tensor(x[:, COLS[g]], x[:, COLS[g]], R[2][:, COLS[g]], ALU.add)
            link(ins)
            later_layers()
            nc.vector.engine_nop().then_inc(s_final, 1)

        @block.sync
        def _(sp):
            sp.wait_ge(s_final, 1)
            full = NT - 1
            sp.dma_start(out[0:full * P, :].rearrange("(t p) c -> p t c", p=P),
                         x[:, 0:full * P].rearrange("p (t c) -> p t c", c=P)).then_inc(s_out, 16)
            sp.dma_start(out[full * P:T, :], x[0:T - full * P, full * P:]).then_inc(s_out, 16)
            sp.wait_ge(s_out, 32)


def kernel(**inputs):
    import concourse.bacc as bacc
    from concourse.bass_utils import run_bass_kernel_spmd

    a = {k: np.asarray(v) for k, v in inputs.items()}
    f32 = np.float32

    def rep(v):
        return np.broadcast_to(v, (P,) + v.shape)

    adj_t = np.eye(TP, dtype=f32)
    adj_t[:T, :T] = a["adj"].T
    x_pad = np.zeros((TP, P), f32)
    x_pad[:T] = a["x"]
    arrays = {
        "x": x_pad,
        "adj_t": adj_t,
        "ident": np.eye(P, dtype=f32),
        "f0_wt": a["L0_ffn_W"].T,
        "f0_lnw": a["L0_ffn_ln_w"][:, None],
        "f0_lnb": a["L0_ffn_ln_b"][:, None],
        "f0_b": rep(a["L0_ffn_b"]),
        "gnn_w": np.stack([a["L0_gnn_W"], a["L1_gnn_W"], a["L3_gnn_W"].T], axis=1),
        "l1_bias": rep(a["L1_gnn_b"]),
        "l2_scale": a["L2_gnn_W"][:, None],
    }
    inv_freq = 1.0 / 10000.0 ** (np.arange(0, HD, 2, dtype=f32) / HD)
    freqs = np.outer(np.arange(TP, dtype=f32), inv_freq).astype(f32)
    emb = np.concatenate([freqs, freqs], axis=-1)
    sign = np.where(np.arange(HD) < HD // 2, -1, 1).astype(f32)[:, None]
    arrays["cos"] = np.tile(np.cos(emb).T, (P // HD, 1)).astype(f32)
    arrays["sin"] = np.tile(np.sin(emb).T * sign, (P // HD, 1)).astype(f32)

    def rotated(w):
        return w.reshape(-1, 2, HD // 2, P)[:, ::-1].reshape(w.shape)

    wq, wk, wv = a["L1_ffn_wq"], a["L1_ffn_wk"], a["L1_ffn_wv"]
    arrays["a_w"] = np.concatenate([wq, rotated(wq), wk, rotated(wk), wv]).T
    arrays["a_ln1"] = a["L1_ffn_ln1_w"][:, None]
    arrays["a_ln2"] = a["L1_ffn_ln2_w"][:, None]
    arrays["a_wo"] = a["L1_ffn_wo"].T
    arrays["a_router"] = a["L1_ffn_router_w"].T
    later = np.triu(np.ones((P, P), bool), 1)
    arrays["mask"] = np.concatenate([np.where(later, MASKED, 0), np.where(later.T, MASKED, 0)], axis=1).astype(f32)
    pad_rows = np.zeros((P, 1), f32)
    pad_rows[96:98] = 1
    arrays["k_pad"] = pad_rows
    arrays["descend"] = rep(np.arange(8, 0, -1).astype(f32))
    hid = a["L1_ffn_w1"].shape[1]
    w13 = np.zeros((P, E1, 2, HID), f32)
    w13[:, :, 0, :hid] = a["L1_ffn_w1"].transpose(2, 0, 1)
    w13[:, :, 1, :hid] = a["L1_ffn_w3"].transpose(2, 0, 1)
    arrays["moe_w13"] = w13.reshape(P, E1, 2 * HID)
    down = np.zeros((E1, HID, P), f32)
    down[:, :hid] = a["L1_ffn_w2"].transpose(0, 2, 1)
    arrays["moe_w2"] = down.reshape(E1, 3, P, P).transpose(2, 0, 1, 3).reshape(P, E1, HID)

    def layers3(w1, w2, w3):
        return np.concatenate([w.transpose(1, 0, 2) for w in (w1, w2, w3)], axis=2)

    def columns(v, n=8):
        full = np.zeros((P, n), f32)
        full[:, :v.shape[0]] = v.T
        return full

    arrays["l2_w"] = layers3(a["L2_ffn_expert_w1"], a["L2_ffn_expert_w2"], a["L2_ffn_expert_w3"])
    arrays["l3_w"] = layers3(a["L3_ffn_W1"], a["L3_ffn_W2"], a["L3_ffn_Wo"])
    one = np.ones((P, 8), f32)
    arrays["par2"] = np.stack([one, columns(a["L2_ffn_expert_b1"]), one, columns(a["L2_ffn_expert_b2"])], axis=1)
    arrays["bn"] = np.stack([columns(a["L3_ffn_" + k + n]) for n in "12" for k in ("g", "be", "m", "v", "b")], axis=1)
    rw1 = np.zeros((P, P), f32)
    rw1[:, :64] = a["L2_ffn_router_w1"]
    arrays["r2_w1"] = rw1
    rb1 = np.zeros((P, 1), f32)
    rb1[:64, 0] = a["L2_ffn_router_b1"]
    arrays["r2_b1"] = rb1
    rw2 = np.zeros((P, 8), f32)
    rw2[:64, :E2] = a["L2_ffn_router_w2"]
    arrays["r2_w2"] = rw2
    rb2 = np.zeros(8, f32)
    rb2[:E2] = a["L2_ffn_router_b2"]
    arrays["r2_b2"] = rep(rb2)
    arrays["r3_w"] = a["L3_ffn_Wr"]
    arrays["r3_b"] = rep(a["L3_ffn_br"])
    last_bias = np.zeros((8, 2, P), f32)
    last_bias[:E2, 0] = a["L2_ffn_expert_b3"]
    last_bias[:E3, 1] = a["L3_ffn_bo"]
    arrays["b3"] = last_bias
    nc = bacc.Bacc("TRN2", target_bir_lowering=False, num_devices=1)
    sent, d = {}, {}
    for name, v in arrays.items():
        sent[f"in_{name}"] = np.ascontiguousarray(v)
        d[name] = nc.dram_tensor(f"in_{name}", v.shape, F32, kind="ExternalInput").ap()
    out = nc.dram_tensor("out_x", (T, P), F32, kind="ExternalOutput").ap()
    adj_lo_dram = nc.dram_tensor("adj_lo_store", (P, NT, TP), F32).ap()
    build(nc, d, out, adj_lo_dram)
    r = run_bass_kernel_spmd(nc, [sent], core_ids=[0])
    return r.results[0]["out_x"]
```

```python
from contextlib import ExitStack

import numpy as np

import concourse.bass as bass
from concourse import mybir

F32 = mybir.dt.float32
F32R = mybir.dt.float32r
ALU = mybir.AluOpType
ACT = mybir.ActivationFunctionType
AX = mybir.AxisListType

P = 128
T = 1354
NT = -(-T // P)
TP = NT * P
GROUPS = [range(4 * g, min(4 * g + 4, NT)) for g in range(-(-NT // 4))]
NG = len(GROUPS)
WIDTH = [P * len(g) for g in GROUPS]
COLS = [slice(512 * g, 512 * g + WIDTH[g]) for g in range(NG)]
FG = [range(3 * g, min(3 * g + 3, NT)) for g in range(-(-NT // 3))]
NF = len(FG)
FCOLS = [slice(P * g[0], P * (g[-1] + 1)) for g in FG]
EPS_LN = 1e-5
ITERS = 30
HID = 3 * P
EPS_RMS = 1e-6
EPS_BN = 1e-3
E1, E2, E3 = 8, 6, 8
MASKED = -1e30
GAIN = 100.0
HEADS, KV_HEADS, HD = 4, 2, 32


def tile(buf, t):
    return buf[:, t * P:(t + 1) * P]


def recurrent_slots(eng, slot):
    end = ITERS * NF

    def fixed(n):
        slot(lambda c: (n + c) % NF, lambda c: n + c + 1, lambda c: 0 <= n + c < end)

    for n in range(-NF, 0):
        fixed(n)
    with eng.Fori(0, ITERS - 1) as i:
        for k in range(NF):
            slot(lambda c: (k + c) % NF, lambda c: i * NF + (k + c + 1), lambda c: True)
    for n in range(end - NF, end):
        fixed(n)


class Unit:

    def __init__(self, n, at, expert, pair):
        self.n = n
        self.group = at % NG
        self.slot = at // NG % 2
        self.parity = at % 2
        self.expert = expert
        self.pair = pair


def expert_slots(eng, experts, lag, work, after=None):
    two = 2 * NG
    total = NG * experts

    def fixed(n):
        work(lambda c: Unit(n + c, n + c, (n + c) // NG, (n + c) // two) if 0 <= n + c < total else None)

    for n in range(two):
        fixed(n)
        if after and n in after:
            after[n]()
    with eng.Fori(0, experts // 2 - 2) as i:
        for k in range(two):
            work(lambda c: Unit(i * two + (two + k + c), k + c, i * 2 + (2 + (k + c) // NG), i + (1 + (k + c) // two)))
    for n in range(total - two, total + lag):
        fixed(n)


def wait_count(eng, semaphore, count):
    if not isinstance(count, int) or count > 0:
        eng.wait_ge(semaphore, count)


def build(nc, d, out, adj_lo_dram):
    ctx = ExitStack()
    with ctx:
        def sb(name, shape, dt=F32):
            return ctx.enter_context(nc.sbuf_tensor(name, shape, dt))

        def sem(name):
            return ctx.enter_context(nc.semaphore(name))

        adj_hi = sb("adj_hi", [P, NT, TP], F32R)
        adj_lo = sb("adj_lo", [P, NT, TP], F32R)
        x = sb("x", [P, TP])
        xn = sb("xn", [P, TP])
        split_hi = sb("split_hi", [P, TP], F32R)
        split_lo = sb("split_lo", [P, TP], F32R)
        R = [sb(f"work{i}", [P, TP]) for i in range(5)]
        ident = sb("ident", [P, P])
        ident_r = sb("ident_r", [P, P], F32R)
        ones = sb("ones", [P, P])
        ones_r = sb("ones_r", [P, P], F32R)
        mean_w = sb("mean_w", [P, P])
        gnn_w = sb("gnn_w", [P, 3, P])
        l1_bias = sb("l1_bias", [P, P])
        l2_scale = sb("l2_scale", [P, 1])
        f0_wt = sb("f0_wt", [P, P])
        f0_lnw = sb("f0_lnw", [P, 1])
        f0_lnb = sb("f0_lnb", [P, 1])
        f0_b = sb("f0_b", [P, P])
        f0_lnb_b = sb("f0_lnb_b", [P, P])
        f0_m = sb("f0_m", [P, P])
        a_w = sb("a_w", [P, 448])
        a_whi = sb("a_whi", [P, 448], F32R)
        a_wlo = sb("a_wlo", [P, 448], F32R)
        a_ln1 = sb("a_ln1", [P, 1])
        a_ln2 = sb("a_ln2", [P, 1])
        a_wo = sb("a_wo", [P, P])
        a_router = sb("a_router", [P, E1])
        a_rhi = sb("a_rhi", [P, E1], F32R)
        a_rlo = sb("a_rlo", [P, E1], F32R)
        mask_f = sb("mask_f", [P, 2 * P])
        mask = sb("mask", [P, 2 * P], F32R)
        k_pad = sb("k_pad", [P, 1])
        mxc = sb("mxc", [P, NT * HEADS, NG])
        m_neg = sb("m_neg", [P, 16])
        m_hi = sb("m_hi", [P, 16], F32R)
        lg = sb("lg", [P, NT, 8])
        probs = sb("probs", [P, NT, 8])
        first = sb("first", [P, NT, 8])
        second = sb("second", [P, NT, 8])
        score = sb("score", [P, NT, 8])
        wgt = sb("wgt", [P, NT, 8])
        descend = sb("descend", [P, 8])
        rt = sb("rt", [P, 6, NT])
        w_raw = R[0][:, 0:2 * HID]
        w_hi = [sb(f"w_hi{i}", [P, 2 * HID], F32R) for i in range(2)]
        w_lo = [sb(f"w_lo{i}", [P, 2 * HID], F32R) for i in range(2)]
        w2_both = sb("w2_both", [P, 2 * HID])
        w2 = [w2_both[:, HID * i:HID * (i + 1)] for i in range(2)]
        k_scratch = w2_both[0:64, :]
        select_q, select_k = w_hi[0][:], w_lo[0][:, 0:2 * 96]
        wcol = [sb(f"wcol{i}", [P, NT]) for i in range(2)]
        pcol = [sb(f"pcol{i}", [P, 4]) for i in range(2)]
        par2 = sb("par2", [P, 4, 8])
        par3 = sb("par3", [P, 4, 8])
        bn = sb("bn", [P, 10, 8])
        r2_w1 = sb("r2_w1", [P, P])
        r2_hi = sb("r2_hi", [P, P], F32R)
        r2_lo = sb("r2_lo", [P, P], F32R)
        r2_b1 = sb("r2_b1", [P, 1])
        r2_w2 = sb("r2_w2", [P, 8])
        r2_b2 = sb("r2_b2", [P, 8])
        r3_w = sb("r3_w", [P, 8])
        r3_hi = sb("r3_hi", [P, 8], F32R)
        r3_lo = sb("r3_lo", [P, 8], F32R)
        r3_b = sb("r3_b", [P, 8])
        b3 = sb("b3", [8, 2, P])
        stats = sb("stats", [P, NT, 6])
        mv = sb("mv", [P, NT, 2])
        rs = sb("rs", [P, NT])
        rss = sb("rss", [P, NT])
        deg = sb("deg", [P, NT])
        deg1 = sb("deg1", [P, NT])
        rdeg = sb("rdeg", [P, NT])
        dinv = sb("dinv", [P, NT])
        sinv = sb("sinv", [P, NT])
        power = sb("power", [P, NT])
        eps_h = sb("eps_h", [P, NT])
        ssq = sb("ssq", [P, NT])
        rnorm = sb("rnorm", [P, NT])
        PS = [ctx.enter_context(nc.psum_tensor(f"bank{b}", [P, 512], F32)) for b in range(8)]

        s_small = sem("small_loaded")
        s_x = sem("x_loaded")
        s_adj = [sem(f"adj_loaded{i}") for i in range(4)]
        s_adj_hi = sem("adj_hi_ready")
        s_adj_lo = sem("adj_lo_ready")
        s_adj_out = sem("adj_lo_stored")
        s_consts = sem("constants_ready")
        s_deg_row = sem("degree_rows_summed")
        s_deg_sb = sem("degree_row_copied")
        s_deg_col = sem("degree_columns_done")
        s_deg = sem("degrees_ready")
        s_dinv = sem("inverse_roots_ready")
        s_f0_m = sem("f0_scaled_weight")
        s_f0_mm = sem("f0_column_means")
        s_f0_w = sem("f0_weight_ready")
        s_var = sem("ln_variance_ready")
        s_rstd = sem("ln_rstd_ready")
        s_feat = sem("features_ready")
        s_hi = sem("split_hi_ready")
        s_lo = sem("split_lo_ready")
        s_agg = sem("aggregated")
        s_aggt = sem("aggregate_copied")
        s_mix = sem("mixed")
        s_relu = sem("relu_ready")
        s_ssq = sem("squares_summed")
        s_rnorm = sem("row_norms_ready")
        s_pre = sem("l1_tanh_input")
        s_tanh1 = sem("l1_tanh_ready")
        s_xup = sem("x_updated")
        s_h = sem("h_ready")
        s_t = sem("tanh_ready")
        s_h1 = sem("h_plus_tanh")
        s_sg = sem("sigmoid_ready")
        s_h2 = sem("h_gated")
        s_st = sem("h_stats_ready")
        s_hv = sem("h_variance_ready")
        s_ve = sem("h_variance_eps")
        s_hr = sem("h_rstd_ready")
        s_tr = sem("h_transposed")
        s_ht = sem("h_transposed_copied")
        s_p = sem("h_projected")
        s_tin = sem("to_transpose_ready")
        s_tt = sem("operand_transposed")
        s_thi = sem("operand_hi_ready")
        s_tlo = sem("operand_lo_ready")
        s_small2 = sem("small2_loaded")
        s_trig = sem("rope_tables_loaded")
        s_xn = sem("xn_ready")
        s_sq3 = sem("rms_squares_summed")
        s_rms = sem("rms_ready")
        s_whi = sem("attention_weights_hi")
        s_wlo = sem("attention_weights_lo")
        s_q = sem("qk_projected")
        s_v = sem("v_projected")
        s_vc = sem("v_copied")
        s_qr = sem("q_roped")
        s_qh = sem("q_hi_ready")
        s_ql = sem("q_lo_ready")
        s_kr = sem("k_roped")
        s_kh = sem("k_hi_ready")
        s_kl = sem("k_lo_ready")
        s_stack = sem("qk_stacked")
        s_mx = sem("scores_for_max")
        s_mxr = sem("scores_reduced")
        s_m = sem("max_ready")
        s_mt = sem("max_transposed")
        s_mrow = sem("max_rows_placed")
        s_sc = sem("scores_ready")
        s_e = sem("exp_ready")
        s_pv = sem("pv_done")
        s_y = sem("head_output_ready")
        s_badd = sem("bias_terms_added")
        s_select = sem("selections_loaded")
        s_selected = sem("selections_rounded")
        s_pads = sem("pads_ready")
        s_st3 = sem("stack_product_ready")
        s_yl = sem("head_sums_copied")
        s_wo = sem("attention_projected")
        s_x2 = sem("attention_residual")
        s_lgp = sem("router_product")
        s_lg = sem("logits_shifted")
        s_ex = sem("router_exp")
        s_wgt = sem("expert_weights_ready")
        s_hid = sem("router_hidden_product")
        s_hidc = sem("router_hidden_ready")
        s_m2 = sem("top2_difference")
        s_e2 = sem("top2_exp")
        s_reload = sem("adj_lo_reloaded")
        s_raw = sem("moe_raw_loaded")
        s_w2 = [sem(f"moe_w2_loaded{i}") for i in range(2)]
        s_mhi = sem("moe_weights_hi")
        s_mlo = sem("moe_weights_lo")
        s_mp = sem("moe_up_products")
        s_ms = sem("moe_silu_ready")
        s_mh = sem("moe_hidden_ready")
        s_my = sem("moe_down_product")
        s_ma = sem("moe_accumulated")
        s_wcol = sem("moe_column_ready")
        s_wt = sem("weights_transposed")
        s_wtc = sem("weights_transposed_copied")
        s_b3 = sem("bias_product")
        s_par = sem("bn_ready")
        s_bnr = sem("bn_roots")
        s_exp = [{k: sem(f"l{n}_{k}") for k in ("w1_loaded", "even_loaded", "odd_loaded", "w1_hi", "w1_lo", "product1", "hidden1", "product2", "hidden2",
                                                "product3", "column", "accumulated")} for n in (2, 3)]
        s_final = sem("result_ready")
        s_out = sem("out_stored")
        s_dve = sem("vector_order")
        s_act = sem("scalar_order")
        s_pool = sem("gpsimd_order")

        QS = [adj_lo[:, h, :] for h in range(HEADS)]
        KS = [adj_lo[:, HEADS + v, :] for v in range(KV_HEADS)]
        QH, QL, KHL = (adj_lo[:, HEADS + KV_HEADS + n, :] for n in range(3))
        VA = R[0][:].rearrange("p (t v c) -> p t v c", v=KV_HEADS, c=2 * HD)
        PT = [R[1][:, 0:512], R[1][:, 512:1024], R[2][:, 0:512]]
        RL = R[2][:, 512:1024]
        YT = R[3]
        MT = R[4][:, 0:512].rearrange("p (t h c) -> p t h c", h=HEADS, c=HD)
        HB = [[R[1 + j][:, 512 * b:512 * b + 512] for j in range(3)] for b in range(2)]
        SB = [R[4][:, 512 * b:512 * b + 512] for b in range(2)]
        SMALL2 = [(a_w, "a_w"), (a_ln1, "a_ln1"), (a_ln2, "a_ln2"), (a_wo, "a_wo"), (a_router, "a_router"), (mask_f, "mask"),
                  (k_pad, "k_pad"), (descend, "descend"), (par2, "par2"), (bn, "bn"), (r2_w1, "r2_w1"), (r2_b1, "r2_b1"),
                  (r2_w2, "r2_w2"), (r2_b2, "r2_b2"), (r3_w, "r3_w"), (r3_b, "r3_b"), (b3, "b3")]

        def max_pieces(g, h):
            for t in GROUPS[g]:
                for c in range(g + 1):
                    yield t, 512 * c, (512 if c < g else (t - 4 * g + 1) * P), c

        def key_steps(g):
            for kt in range(GROUPS[g][-1] + 1):
                yield kt, max(0, kt - 4 * g) * P

        STACKS = HEADS + KV_HEADS

        def stack_bank(m):
            return (6, 7)[m % 2] if m < STACKS else (3, 4, 5, 7)[m % 4]

        def stacks_before(m):
            return max([k + 1 for k in range(m) if stack_bank(k) == stack_bank(m)], default=0)

        def keys_before(g, h):
            return sum(HEADS * len(list(key_steps(b))) for b in range(g)) + h * len(list(key_steps(g)))

        schedule = []
        for h in range(HEADS):
            schedule += [("max", 0, h, piece) for piece in max_pieces(0, h)]
            per_head = (NG - 1) * STACKS // HEADS
            schedule += [("stack", 0, 0, m) for m in range(STACKS + h * per_head, STACKS + (h + 1) * per_head)]
        schedule.append(("rows", 0, 0, None))
        for g in range(NG):
            for h in range(HEADS):
                ahead = list(max_pieces(g + 1, h)) if g + 1 < NG else []
                steps = list(key_steps(g))
                for n, step in enumerate(steps):
                    schedule.append(("key", g, h, step))
                    take = len(ahead) // (len(steps) - n)
                    schedule += [("max", g + 1, h, piece) for piece in ahead[:take]]
                    ahead = ahead[take:]
                schedule.append(("head", g, h, None))
            if g + 1 < NG:
                schedule.append(("rows", g + 1, 0, None))

        block = ctx.enter_context(nc.Block())

        @block.sync
        def _(sp):
            for t, src in ((ident, "ident"), (f0_wt, "f0_wt"), (f0_lnw, "f0_lnw"), (f0_lnb, "f0_lnb"), (f0_b, "f0_b")):
                sp.dma_start(t[:], d[src]).then_inc(s_small, 16)
            sp.dma_start(x[:].rearrange("p (t c) -> p t c", c=P),
                         d["x"].rearrange("(t p) c -> p t c", p=P)).then_inc(s_x, 16)
            for k in range(NT):
                if k >= 4:
                    sp.wait_ge(s_adj_lo, k - 3)
                sp.dma_start(R[k % 4][:], d["adj_t"][k * P:(k + 1) * P, :]).then_inc(s_adj[k % 4], 16)
            for t, src in ((gnn_w, "gnn_w"), (l1_bias, "l1_bias"), (l2_scale, "l2_scale")):
                sp.dma_start(t[:], d[src]).then_inc(s_small, 16)
            for t, src in SMALL2:
                sp.dma_start(t[:], d[src]).then_inc(s_small2, 16)
            sp.dma_start(w2_both[:], d["select_q"]).then_inc(s_select, 16)
            sp.wait_ge(s_selected, 1)
            sp.dma_start(w2_both[:, 0:2 * 96], d["select_k"]).then_inc(s_select, 16)
            sp.wait_ge(s_adj_lo, NT)
            sp.dma_start(adj_lo_dram, adj_lo[:].bitcast(F32)).then_inc(s_adj_out, 16)
            sp.wait_ge(s_ssq, NG)
            sp.dma_start(R[3][:], d["cos"]).then_inc(s_trig, 16)
            sp.dma_start(R[4][:], d["sin"]).then_inc(s_trig, 16)

            def moe_up(e):
                sp.dma_start(w_raw.rearrange("p (a n) -> p a n", a=1), d["moe_w13"][:, bass.ds(e, 1), :]).then_inc(s_raw, 16)

            def moe_down(e, s):
                sp.dma_start(w2[s].rearrange("p (a n) -> p a n", a=1), d["moe_w2"][:, bass.ds(e, 1), :]).then_inc(s_w2[s], 16)

            sp.wait_ge(s_kl, NG)
            moe_down(0, 0)
            moe_down(1, 1)
            sp.wait_ge(s_y, NG)
            sp.wait_ge(s_adj_out, 16)
            sp.wait_ge(s_tt, 2 * NG)
            moe_up(0)
            sp.wait_ge(s_mlo, 1)
            moe_up(1)
            with sp.Fori(0, E1 // 2 - 1) as i:
                for s in range(2):
                    sp.wait_ge(s_mlo, i * 2 + (s + 2))
                    moe_up(i * 2 + (s + 2))
                    sp.wait_ge(s_my, i * 6 + 3 * (s + 1))
                    moe_down(i * 2 + (s + 2), s)
                    sp.dma_start(adj_lo[:, bass.ds(i * 2 + s, 1), :].bitcast(F32), adj_lo_dram[:, bass.ds(i * 2 + s, 1), :]).then_inc(s_reload, 16)
            sp.dma_start(adj_lo[:, E1 - 2:NT, :].bitcast(F32), adj_lo_dram[:, E1 - 2:NT, :]).then_inc(s_reload, 16)
            for n, experts, src in ((0, E2, "l2_w"), (1, E3, "l3_w")):
                sems = s_exp[n]
                loaded = (sems["even_loaded"], sems["odd_loaded"])

                def load_first(e):
                    sp.dma_start(w_raw[:, 0:P].rearrange("p (a n) -> p a n", a=1), d[src][:, bass.ds(e, 1), 0:P]).then_inc(sems["w1_loaded"], 16)

                def load_rest(e, s):
                    sp.dma_start(w2[s][:, P:3 * P].rearrange("p (a n) -> p a n", a=1), d[src][:, bass.ds(e, 1), P:3 * P]).then_inc(loaded[s], 16)

                if n == 0:
                    sp.wait_ge(s_my, NG * E1)
                else:
                    sp.wait_ge(s_exp[0]["product3"], 3 * E2)
                load_rest(0, 0)
                load_rest(1, 1)
                sp.wait_ge(s_tt, NG * (n + 3))
                load_first(0)
                sp.wait_ge(sems["w1_lo"], 1)
                load_first(1)
                with sp.Fori(0, experts // 2 - 1) as i:
                    for s in range(2):
                        sp.wait_ge(sems["w1_lo"], i * 2 + (s + 2))
                        load_first(i * 2 + (s + 2))
                        sp.wait_ge(sems["product3"], i * 6 + 3 * (s + 1))
                        load_rest(i * 2 + (s + 2), s)

        @block.tensor
        def _(pe):
            mm = nc.tensor.matmul

            pe.wait_ge(s_consts, 2)
            for k in range(NT):
                pe.wait_ge(s_adj_hi, k + 1)
                pe.wait_ge(s_adj_lo, k + 1)
                for g in range(NG):
                    mm(PS[g][:, 0:WIDTH[g]], ones_r[:], adj_hi[:, k, COLS[g]], start=(k == 0), stop=False)
                    last = mm(PS[g][:, 0:WIDTH[g]], ones_r[:], adj_lo[:, k, COLS[g]], start=False, stop=(k == NT - 1))
            last.then_inc(s_deg_row, 1)
            pe.wait_ge(s_f0_m, 2)
            mm(PS[7][:, 0:P], mean_w[:], f0_m[:], start=True, stop=True)
            mm(PS[7][:, P:2 * P], f0_lnb_b[:], f0_wt[:], start=True, stop=True).then_inc(s_f0_mm, 1)
            pe.wait_ge(s_deg_sb, 1)
            for t in range(NT):
                last = mm(PS[6][:, t:t + 1], R[4][0:1, t * P:(t + 1) * P], ones[0:1, 0:1], start=True, stop=True)
            last.then_inc(s_deg_col, 1)

            def aggregate(q, self_loop):
                for g in range(NG):
                    pe.wait_ge(s_hi, NG * aggregate.calls + g + 1)
                    pe.wait_ge(s_lo, NG * aggregate.calls + g + 1)
                    if g < NG - 1:
                        for k in GROUPS[g]:
                            for c in range(NG):
                                tile_product(k, c, k == 0, False)
                            if self_loop:
                                self_product(k)
                for c in range(NG):
                    for k in GROUPS[-1]:
                        last = tile_product(k, c, False, k == NT - 1 and not (self_loop and c == NG - 1))
                    if self_loop and c == NG - 1:
                        for k in GROUPS[-1]:
                            last = self_product(k, stop=k == NT - 1)
                    last.then_inc(s_agg, 1)
                aggregate.calls += 1

            aggregate.calls = 0

            def tile_product(k, c, first, end):
                dst = PS[c][:, 0:WIDTH[c]]
                mm(dst, tile(split_hi, k), adj_hi[:, k, COLS[c]], start=first, stop=False)
                mm(dst, tile(split_hi, k), adj_lo[:, k, COLS[c]], start=False, stop=False)
                return mm(dst, tile(split_lo, k), adj_hi[:, k, COLS[c]], start=False, stop=end)

            def self_product(k, stop=False):
                dst = tile(PS[k // 4], k % 4)
                mm(dst, tile(split_hi, k), ident_r[:], start=False, stop=False)
                return mm(dst, tile(split_lo, k), ident_r[:], start=False, stop=stop)

            def mix(q, w):
                for g in range(NG):
                    pe.wait_ge(s_aggt, NG * q + g + 1)
                    for t in GROUPS[g]:
                        dst = tile(PS[3 + g], t % 4)
                        if w is None:
                            last = nc.tensor.transpose(dst, tile(R[1], t), ident[:])
                        else:
                            last = mm(dst, tile(R[1], t), gnn_w[:, w, :], start=True, stop=True)
                    last.then_inc(s_mix, 1)

            pe.wait_ge(s_small, 8 * 16)
            aggregate(0, True)
            mix(0, 0)
            pe.wait_ge(s_f0_w, 1)

            def slot(place, count, valid):
                if valid(2):
                    g = place(2)
                    pe.wait_ge(s_h2, count(2))
                    for n, t in enumerate(FG[g]):
                        last = nc.tensor.transpose(tile(PS[g], n), tile(R[0], t), ident[:])
                    last.then_inc(s_tr, 1)
                if valid(1):
                    g = place(1)
                    pe.wait_ge(s_ht, count(1))
                    for n, t in enumerate(FG[g]):
                        last = mm(tile(PS[NF + g], n), tile(R[2], t), f0_m[:], start=True, stop=True)
                    last.then_inc(s_p, 1)

            recurrent_slots(pe, slot)
            aggregate(1, True)
            mix(1, 1)

            def transpose_operand(n):
                for g in range(NG):
                    pe.wait_ge(s_tin, NG * n + g + 1)
                    for t in GROUPS[g]:
                        last = nc.tensor.transpose(tile(PS[g], t % 4), tile(R[0], t), ident[:])
                    last.then_inc(s_tt, 1)

            def three(dst, a_hi, a_lo, b_hi, b_lo, start=True, stop=True):
                mm(dst, a_hi, b_hi, start=start, stop=False)
                mm(dst, a_hi, b_lo, start=False, stop=False)
                return mm(dst, a_lo, b_hi, start=False, stop=stop)

            transpose_operand(0)
            def project_v(g):
                for t in GROUPS[g]:
                    last = three(PS[6 + g % 2][:, (t % 4) * 64:(t % 4 + 1) * 64], tile(split_hi, t), tile(split_lo, t),
                                 a_whi[:, 384:448], a_wlo[:, 384:448])
                last.then_inc(s_v, 1)

            pe.wait_ge(s_wlo, 1)
            for g in range(NG):
                pe.wait_ge(s_tlo, NG if g == 1 else g + 1)
                if g == 2:
                    pe.wait_ge(s_kr, 1)
                banks = (0, 1, 2) if g == 1 else (3, 4, 5)
                for n, b in enumerate(banks):
                    w = slice(P * n, P * (n + 1))
                    last = three(PS[b][:, 0:WIDTH[g]], a_whi[:, w], a_wlo[:, w], split_hi[:, COLS[g]], split_lo[:, COLS[g]])
                last.then_inc(s_q, 1)
                if g < 2:
                    project_v(g)

            def stack(m):
                g, n = m // STACKS, m % STACKS
                pe.wait_ge(s_ql, g + 1)
                pe.wait_ge(s_kl, g + 1)
                if stacks_before(m) > 0:
                    pe.wait_ge(s_stack, stacks_before(m))
                dst = PS[stack_bank(m)][0:96, 0:WIDTH[g]]
                if n < HEADS:
                    mm(dst, select_q[:, 96 * n:96 * (n + 1)], QH[:, COLS[g]], start=True, stop=False)
                    last = mm(dst, select_q[:, 96 * (HEADS + n):96 * (HEADS + n + 1)], QL[:, COLS[g]], start=False, stop=True)
                else:
                    last = mm(dst, select_k[:, 96 * (n - HEADS):96 * (n - HEADS + 1)], KHL[:, COLS[g]], start=True, stop=True)
                last.then_inc(s_st3, 1)

            pe.wait_ge(s_selected, 2)
            pe.wait_ge(s_vc, 2)
            for m in range(STACKS):
                stack(m)
            pe.wait_ge(s_stack, STACKS)
            project_v(2)
            pe.wait_ge(s_kr, NG)

            n_max = n_key = n_head = 0
            pending = []

            def values(n, g, h, step, first_key, last_key):
                kt, o = step
                pe.wait_ge(s_e, n + 1)
                mm(PS[5 + (g * HEADS + h) % 2][0:2 * HD, o:WIDTH[g]], VA[:, kt, h // 2, :], PT[n % 3][:, 0:WIDTH[g] - o],
                   start=first_key, stop=last_key).then_inc(s_pv, 1)

            for kind, g, h, item in schedule:
                if kind == "max":
                    t, k0, width, c = item
                    if n_max >= 3:
                        pe.wait_ge(s_mxr, n_max - 2)
                    dst = PS[n_max % 3]
                    last = mm(dst[:, 0:width], QS[h][0:96, t * P:(t + 1) * P], KS[h // 2][0:96, k0:k0 + width], start=True, stop=c < g)
                    if c == g:
                        last = mm(dst[:, width - P:width], ident_r[:], mask[:, 0:P], start=False, stop=True)
                    last.then_inc(s_mx, 1)
                    n_max += 1
                elif kind == "stack":
                    stack(item)
                elif kind == "rows":
                    if g == 0:
                        pe.wait_ge(s_stack, NG * STACKS)
                    pe.wait_ge(s_m, g + 1)
                    for t in GROUPS[g]:
                        last = nc.tensor.transpose(tile(PS[7], t % 4), R[4][:, (t % 4) * P:(t % 4 + 1) * P], ident[:])
                    last.then_inc(s_mt, 1)
                elif kind == "key":
                    kt, o = item
                    if kt == 0 and h == 0:
                        pe.wait_ge(s_mrow, g + 1)
                        pe.wait_ge(s_vc, NG)
                        pe.wait_ge(s_pads, 1 + KV_HEADS)
                    if n_key >= 2:
                        pe.wait_ge(s_e, n_key - 1)
                    dst = PS[3 + n_key % 2]
                    diagonal = kt >= 4 * g
                    last = mm(dst[:, 0:WIDTH[g] - o], KS[h // 2][:, kt * P:(kt + 1) * P], QS[h][:, 512 * g + o:512 * g + WIDTH[g]],
                              start=True, stop=not diagonal)
                    if diagonal:
                        last = mm(dst[:, 0:P], ident_r[:], mask[:, P:2 * P], start=False, stop=True)
                    last.then_inc(s_sc, 1)
                    if kt == 0 and n_head >= 2:
                        pe.wait_ge(s_yl, n_head - 1)
                    if len(pending) > 0:
                        values(*pending.pop(0))
                    pending.append((n_key, g, h, item, kt == 0, kt == GROUPS[g][-1]))
                    n_key += 1
                else:
                    values(*pending.pop(0))
                    n_head += 1
            for g in range(NG):
                pe.wait_ge(s_y, g + 1)
                if g == 0:
                    pe.wait_ge(s_mxr, n_max)
                for t in GROUPS[g]:
                    last = mm(tile(PS[g], t % 4), tile(YT, t), a_wo[:], start=True, stop=True)
                last.then_inc(s_wo, 1)
            transpose_operand(1)
            pe.wait_ge(s_tlo, 2 * NG)
            for t in range(NT):
                last = three(PS[6][:, t * 8:t * 8 + 8], tile(split_hi, t), tile(split_lo, t), a_rhi[:], a_rlo[:])
            last.then_inc(s_lgp, 1)

            def moe(unit):
                up, down = unit(0), unit(-1)
                if up:
                    s, g = up.slot, up.group
                    if g == 0:
                        pe.wait_ge(s_mlo, up.expert + 1)
                    for j in range(3):
                        wait_count(pe, s_mh, up.n * 3 + (j - 1))
                        for b in (0, 2):
                            w = slice(HID * (b // 2) + P * j, HID * (b // 2) + P * (j + 1))
                            last = three(PS[b + (up.parity + j) % 2][:, 0:WIDTH[g]], w_hi[s][:, w], w_lo[s][:, w], split_hi[:, COLS[g]], split_lo[:, COLS[g]])
                        last.then_inc(s_mp, 1)
                if down:
                    s, g = down.slot, down.group
                    if g == 0:
                        pe.wait_ge(s_w2[s], down.pair * 16 + 16)
                    pe.wait_ge(s_mh, down.n * 3 + 3)
                    wait_count(pe, s_ma, down.n - 1)
                    for t in GROUPS[g]:
                        for j in range(3):
                            last = mm(tile(PS[4 + down.parity], t % 4), tile(HB[down.parity][j], t % 4), w2[s][:, j * P:(j + 1) * P],
                                      start=j == 0, stop=j == 2)
                    last.then_inc(s_my, 1)

            expert_slots(pe, E1, 1, moe)
            pe.wait_ge(s_reload, 16 * (E1 - 1))
            pe.wait_ge(s_ma, NG * E1)
            aggregate(2, False)
            mix(2, None)

            def bias_slots(n, experts):
                def transposed(g):
                    pe.wait_ge(s_wgt, n + 1)
                    if g > 0:
                        pe.wait_ge(s_wtc, NG * n + g)
                    for t in GROUPS[g]:
                        last = mm(PS[7][0:experts, (t % 4) * P:(t % 4 + 1) * P], wgt[:, t, 0:experts], ident[:], start=True, stop=True)
                    last.then_inc(s_wt, 1)

                def product(g):
                    pe.wait_ge(s_wtc, NG * n + g + 1)
                    if g > 0:
                        pe.wait_ge(s_badd, NG * n + g)
                    for t in GROUPS[g]:
                        last = mm(tile(PS[6], t % 4), R[3][0:experts, t * P:(t + 1) * P], b3[0:experts, n, :], start=True, stop=True)
                    last.then_inc(s_b3, 1)

                def after_slot(m):
                    if m >= 3:
                        product(m - 3)
                    if m <= 4:
                        transposed(m - 2)

                return {m: (lambda m=m: after_slot(m)) for m in range(2, 6)}

            def expert_layer(n, experts):
                sems = s_exp[n]

                def work(unit):
                    one, two, three_ = unit(0), unit(-1), unit(-2)
                    if one:
                        if one.group == 0:
                            pe.wait_ge(sems["w1_lo"], one.expert + 1)
                        three(PS[one.parity][:, 0:WIDTH[one.group]], w_hi[one.slot][:, 0:P], w_lo[one.slot][:, 0:P],
                              split_hi[:, COLS[one.group]], split_lo[:, COLS[one.group]]).then_inc(sems["product1"], 1)
                    if two:
                        if two.group == 0:
                            pe.wait_ge(sems["odd_loaded" if two.slot else "even_loaded"], two.pair * 16 + 16)
                        pe.wait_ge(sems["hidden1"], two.n + 1)
                        mm(PS[2 + two.parity][:, 0:WIDTH[two.group]], w2[two.slot][:, P:2 * P], HB[two.parity][0][:, 0:WIDTH[two.group]],
                           start=True, stop=True).then_inc(sems["product2"], 1)
                    if three_:
                        pe.wait_ge(sems["hidden2"], three_.n + 1)
                        wait_count(pe, sems["accumulated"], three_.n - 1)
                        for t in GROUPS[three_.group]:
                            last = mm(tile(PS[4 + three_.parity], t % 4), tile(HB[three_.parity][1], t % 4), w2[three_.slot][:, 2 * P:3 * P],
                                      start=True, stop=True)
                        last.then_inc(sems["product3"], 1)

                expert_slots(pe, experts, 2, work, bias_slots(n, experts))

            transpose_operand(2)
            pe.wait_ge(s_tlo, 3 * NG)
            pe.wait_ge(s_xup, 1)
            pe.wait_ge(s_wlo, 3)
            for g in range(NG):
                three(PS[3 + g][:, 0:WIDTH[g]], r2_hi[:], r2_lo[:], split_hi[:, COLS[g]], split_lo[:, COLS[g]]).then_inc(s_hid, 1)
            for t in range(NT):
                if t % 4 == 0:
                    pe.wait_ge(s_hidc, t // 4 + 1)
                last = mm(PS[6][:, t * 8:t * 8 + E2], R[1][0:64, t * P:(t + 1) * P], r2_w2[0:64, 0:E2], start=True, stop=True)
            last.then_inc(s_lgp, 1)
            expert_layer(0, E2)

            pe.wait_ge(s_exp[0]["accumulated"], NG * E2)
            aggregate(3, False)
            mix(3, 2)
            transpose_operand(3)
            pe.wait_ge(s_tlo, 4 * NG)
            for t in range(NT):
                last = three(PS[6][:, t * 8:t * 8 + 8], tile(split_hi, t), tile(split_lo, t), r3_hi[:], r3_lo[:])
            last.then_inc(s_lgp, 1)
            expert_layer(1, E3)

        @block.scalar
        def _(act):
            order = [0]

            def link(ins):
                order[0] += 1
                ins.then_inc(s_act, 1)
                act.wait_ge(s_act, order[0])

            for k in range(NT):
                act.wait_ge(s_adj[k % 4], 16 * (k // 4 + 1))
                nc.scalar.activation(adj_hi[:, k, :], R[k % 4][:], ACT.Copy).then_inc(s_adj_hi, 1)
            act.wait_ge(s_deg_row, 1)
            for g in range(NG):
                ins = nc.scalar.activation(R[4][0:1, COLS[g]], PS[g][0:1, 0:WIDTH[g]], ACT.Copy)
            ins.then_inc(s_deg_sb, 1)

            def hi_part(n):
                for g in range(NG):
                    act.wait_ge(s_feat, NG * n + g + 1)
                    nc.scalar.activation(split_hi[:, COLS[g]], R[0][:, COLS[g]], ACT.Copy).then_inc(s_hi, 1)

            def copy_aggregate(q):
                for g in range(NG):
                    act.wait_ge(s_agg, NG * q + g + 1)
                    if q == 2:
                        ins = nc.scalar.activation(R[1][:, COLS[g]], PS[g][:, 0:WIDTH[g]], ACT.Identity, scale=l2_scale[:, 0:1])
                    else:
                        ins = nc.scalar.activation(R[1][:, COLS[g]], PS[g][:, 0:WIDTH[g]], ACT.Copy)
                    ins.then_inc(s_aggt, 1)

            hi_part(0)
            copy_aggregate(0)
            for g in range(NG):
                act.wait_ge(s_relu, g + 1)
                for t in GROUPS[g]:
                    ins = nc.scalar.activation(tile(R[3], t), tile(R[2], t), ACT.Square, accum_out=ssq[:, t:t + 1])
                ins.then_inc(s_ssq, 1)
            act.wait_ge(s_select, 16)
            nc.scalar.activation(select_q, w2_both[:], ACT.Copy).then_inc(s_selected, 1)
            nc.scalar.preload_act_table(ACT.Sigmoid)

            def slot(place, count, valid):
                if valid(3):
                    c = FCOLS[place(3)]
                    act.wait_ge(s_h1, count(3))
                    nc.scalar.activation(R[1][:, c], R[0][:, c], ACT.Sigmoid, scale=1 / GAIN).then_inc(s_sg, 1)
                if valid(4):
                    c = FCOLS[place(4)]
                    act.wait_ge(s_h, count(4))
                    nc.scalar.activation(R[1][:, c], R[0][:, c], ACT.Tanh, scale=1 / GAIN).then_inc(s_t, 1)
                if valid(2):
                    g = place(2)
                    act.wait_ge(s_tr, count(2))
                    nc.scalar.activation(R[2][:, FCOLS[g]], PS[g][:, 0:P * len(FG[g])], ACT.Copy).then_inc(s_ht, 1)

            recurrent_slots(act, slot)
            act.wait_ge(s_select, 32)
            nc.scalar.activation(select_k, w2_both[:, 0:2 * 96], ACT.Copy).then_inc(s_selected, 1)
            hi_part(1)
            copy_aggregate(1)
            for g in range(NG):
                act.wait_ge(s_pre, g + 1)
                nc.scalar.activation(R[2][:, COLS[g]], R[2][:, COLS[g]], ACT.Tanh).then_inc(s_tanh1, 1)

            def squares(n):
                for g in range(NG):
                    if n == 0:
                        act.wait_ge(s_xn, g + 1)
                    else:
                        act.wait_ge(s_x2, g + 1)
                    for t in GROUPS[g]:
                        ins = nc.scalar.activation(tile(R[1], t), tile(xn, t), ACT.Square, accum_out=ssq[:, t:t + 1])
                    ins.then_inc(s_sq3, 1)

            def operand_hi(n):
                for g in range(NG):
                    act.wait_ge(s_tt, NG * n + g + 1)
                    nc.scalar.activation(split_hi[:, COLS[g]], PS[g][:, 0:WIDTH[g]], ACT.Copy).then_inc(s_thi, 1)

            act.wait_ge(s_small2, 16 * len(SMALL2))
            nc.scalar.activation(a_whi[:], a_w[:], ACT.Copy, scale=a_ln1[:, 0:1])
            nc.scalar.activation(a_rhi[:], a_router[:], ACT.Copy, scale=a_ln2[:, 0:1])
            nc.scalar.activation(r2_hi[:], r2_w1[:], ACT.Copy)
            nc.scalar.activation(r3_hi[:], r3_w[:], ACT.Copy).then_inc(s_whi, 1)
            nc.scalar.preload_act_table(ACT.Exp)
            squares(0)
            operand_hi(0)

            def copy_stack(m):
                g, n = m // STACKS, m % STACKS
                act.wait_ge(s_st3, m + 1)
                nc.scalar.activation((QS + KS)[n][0:96, COLS[g]], PS[stack_bank(m)][0:96, 0:WIDTH[g]], ACT.Copy).then_inc(s_stack, 1)

            def copy_first_stacks(begin, end):
                for m in range(begin, end):
                    copy_stack(m)

            for g in range(NG):
                act.wait_ge(s_qr, g + 1)
                nc.scalar.activation(QH[:, COLS[g]], R[1][:, COLS[g]], ACT.Copy).then_inc(s_qh, 1)
                if g == 2:
                    copy_first_stacks(2, 4)
                act.wait_ge(s_kr, g + 1)
                nc.scalar.activation(KHL[0:64, COLS[g]], R[2][0:64, COLS[g]], ACT.Copy).then_inc(s_kh, 1)
                if g == 2:
                    copy_first_stacks(4, STACKS)
                act.wait_ge(s_v, g + 1)
                n = len(GROUPS[g])
                nc.scalar.activation(VA[:, 4 * g:4 * g + n, :, 0:HD],
                                     PS[6 + g % 2][:, 0:64 * n].rearrange("p (t v c) -> p t v c", v=KV_HEADS, c=HD), ACT.Copy).then_inc(s_vc, 1)
                if g == 1:
                    copy_first_stacks(0, 2)
            n_key = 0
            finished = None

            def copy_head(g, h):
                act.wait_ge(s_pv, keys_before(g, h) + len(list(key_steps(g))))
                if h == 0 and g > 0:
                    act.wait_ge(s_y, g)
                bank = PS[5 + (g * HEADS + h) % 2]
                nc.scalar.activation(YT[HD * h:HD * (h + 1), COLS[g]], bank[0:HD, 0:WIDTH[g]], ACT.Copy)
                nc.scalar.activation(RL[HD * h:HD * (h + 1), 0:WIDTH[g]], bank[HD:2 * HD, 0:WIDTH[g]], ACT.Copy).then_inc(s_yl, 1)

            for kind, g, h, item in schedule:
                if kind == "stack":
                    copy_stack(item)
                elif kind == "head":
                    finished = (g, h)
                elif kind == "rows":
                    act.wait_ge(s_mt, g + 1)
                    for hh in range(HEADS):
                        ins = nc.scalar.activation(QS[hh][96:128, COLS[g]], PS[7][HD * hh:HD * (hh + 1), 0:WIDTH[g]], ACT.Copy)
                    ins.then_inc(s_mrow, 1)
                elif kind == "key":
                    kt, o = item
                    act.wait_ge(s_sc, n_key + 1)
                    if n_key >= 3:
                        act.wait_ge(s_pv, n_key - 2)
                    nc.scalar.activation(PT[n_key % 3][:, 0:WIDTH[g] - o], PS[3 + n_key % 2][:, 0:WIDTH[g] - o], ACT.Exp,
                                         scale=float(HD) ** -0.5).then_inc(s_e, 1)
                    n_key += 1
                    if kt == 1 and finished:
                        copy_head(*finished)
                        finished = None
            copy_head(*finished)
            squares(1)
            operand_hi(1)

            def router_exp(n):
                act.wait_ge(s_lg, n + 1)
                nc.scalar.activation(probs[:], lg[:], ACT.Exp).then_inc(s_ex, 1)

            def split_moe(s, count):
                act.wait_ge(s_raw, count)
                nc.scalar.activation(w_hi[s][:], w_raw, ACT.Copy, scale=a_ln2[:, 0:1]).then_inc(s_mhi, 1)

            def moe(unit):
                up = unit(0)
                if not up:
                    return
                w = WIDTH[up.group]
                for j in range(3):
                    b = (up.parity + j) % 2
                    act.wait_ge(s_mp, up.n * 3 + (j + 1))
                    nc.scalar.activation(SB[b][:, 0:w], PS[b][:, 0:w], ACT.Silu).then_inc(s_ms, 1)
                if up.group == 1 and unit(NG):
                    split_moe(1 - up.slot, up.expert * 16 + 32)

            split_moe(0, 16)
            router_exp(0)
            nc.scalar.preload_act_table(ACT.Silu)
            expert_slots(act, E1, 0, moe)
            nc.scalar.preload_act_table(ACT.Exp)
            hi_part(2)
            copy_aggregate(2)

            def expert_layer(n, experts, after):
                sems = s_exp[n]

                def hidden(layer, u):
                    act.wait_ge(sems[f"product{layer}"], u.n + 1)
                    w = WIDTH[u.group]
                    nc.scalar.activation(HB[u.parity][layer - 1][:, 0:w], PS[2 * (layer - 1) + u.parity][:, 0:w], ACT.Relu,
                                         scale=pcol[u.slot][:, 2 * layer - 2:2 * layer - 1],
                                         bias=pcol[u.slot][:, 2 * layer - 1:2 * layer]).then_inc(sems[f"hidden{layer}"], 1)

                def work(unit):
                    one, two, ahead = unit(0), unit(-1), unit(NG)
                    if one:
                        hidden(1, one)
                    if two:
                        hidden(2, two)
                    if one and one.group == 1 and ahead:
                        split_expert(n, ahead.slot, ahead.expert * 16 + 16)

                expert_slots(act, experts, 1, work, after)

            def split_expert(n, s, count):
                sems = s_exp[n]
                act.wait_ge(sems["w1_loaded"], count)
                nc.scalar.activation(w_hi[s][:, 0:P], w_raw[:, 0:P], ACT.Copy).then_inc(sems["w1_hi"], 1)

            def transposed_weights(n, experts):
                def copy(g):
                    act.wait_ge(s_wt, NG * n + g + 1)
                    nc.scalar.activation(R[3][0:experts, COLS[g]], PS[7][0:experts, 0:WIDTH[g]], ACT.Copy).then_inc(s_wtc, 1)

                return {2 + g: (lambda g=g: copy(g)) for g in range(NG)}

            operand_hi(2)
            split_expert(0, 0, 16)
            for g in range(NG):
                act.wait_ge(s_hid, g + 1)
                nc.scalar.activation(R[1][:, COLS[g]], PS[3 + g][:, 0:WIDTH[g]], ACT.Relu, bias=r2_b1[:, 0:1]).then_inc(s_hidc, 1)
            router_exp(1)

            def second_exp():
                act.wait_ge(s_m2, 1)
                nc.scalar.activation(rt[:, 5, :], rt[:, 4, :], ACT.Exp).then_inc(s_e2, 1)

            expert_layer(0, E2, {0: second_exp, **transposed_weights(0, E2)})
            hi_part(3)
            copy_aggregate(3)
            operand_hi(3)
            split_expert(1, 0, 16)
            router_exp(2)
            expert_layer(1, E3, transposed_weights(1, E3))

        @block.gpsimd
        def _(pool):
            order = [0]

            def link(ins):
                order[0] += 1
                ins.then_inc(s_pool, 1)
                pool.wait_ge(s_pool, order[0])

            nc.gpsimd.memset(power[:], -0.5)
            nc.gpsimd.memset(eps_h[:], EPS_LN * GAIN * GAIN)
            nc.gpsimd.memset(ones[:], 1.0)
            link(nc.gpsimd.memset(mean_w[:], 1 / P))
            nc.gpsimd.memset(f0_lnb_b[:], 1.0).then_inc(s_consts, 1)

            def rstd(n, scale=None):
                for g in range(NG):
                    c = slice(GROUPS[g][0], GROUPS[g][-1] + 1)
                    pool.wait_ge(s_var, NG * n + g + 1)
                    link(nc.gpsimd.tensor_scalar(rs[:, c], mv[:, c, 1], EPS_LN, None, ALU.add))
                    if scale is None:
                        nc.gpsimd.tensor_tensor(rss[:, c], rs[:, c], power[:, c], ALU.pow).then_inc(s_rstd, 1)
                        continue
                    link(nc.gpsimd.tensor_tensor(rs[:, c], rs[:, c], power[:, c], ALU.pow))
                    if scale is dinv and g == 0:
                        pool.wait_ge(s_deg, 1)
                        nc.gpsimd.tensor_tensor(dinv[:], deg1[:], power[:], ALU.pow).then_inc(s_dinv, 1)
                        pool.wait_ge(s_dinv, 1)
                    if isinstance(scale, float):
                        ins = nc.gpsimd.tensor_scalar(rss[:, c], rs[:, c], scale, None, ALU.mult)
                    else:
                        ins = nc.gpsimd.tensor_tensor(rss[:, c], rs[:, c], scale[:, c], ALU.mult)
                    ins.then_inc(s_rstd, 1)

            rstd(0, dinv)
            nc.gpsimd.tensor_tensor(sinv[:], deg[:], power[:], ALU.pow).then_inc(s_dinv, 1)
            for g in range(NG):
                c = slice(GROUPS[g][0], GROUPS[g][-1] + 1)
                pool.wait_ge(s_ssq, g + 1)
                link(nc.gpsimd.tensor_scalar(ssq[:, c], ssq[:, c], 1e-24, None, ALU.max))
                nc.gpsimd.tensor_tensor(rnorm[:, c], ssq[:, c], power[:, c], ALU.pow).then_inc(s_rnorm, 1)
            rstd(1, GAIN)

            def slot(place, count, valid):
                if valid(1):
                    g = place(1)
                    c = slice(FG[g][0], FG[g][-1] + 1)
                    pool.wait_ge(s_hv, count(1))
                    nc.gpsimd.tensor_tensor(rs[:, c], mv[:, c, 1], eps_h[:, c], ALU.add).then_inc(s_ve, 1)
                    pool.wait_ge(s_ve, count(1))
                    nc.gpsimd.tensor_tensor(rss[:, c], rs[:, c], power[:, c], ALU.pow).then_inc(s_hr, 1)
                if valid(4):
                    c = FCOLS[place(4)]
                    pool.wait_ge(s_t, count(4))
                    nc.gpsimd.tensor_tensor(R[0][:, c], R[0][:, c], R[1][:, c], ALU.add).then_inc(s_h1, 1)

            recurrent_slots(pool, slot)
            rstd(2)

            def rms(n):
                for g in range(NG):
                    c = slice(GROUPS[g][0], GROUPS[g][-1] + 1)
                    pool.wait_ge(s_sq3, NG * n + g + 1)
                    link(nc.gpsimd.tensor_scalar(ssq[:, c], ssq[:, c], 1 / P, EPS_RMS, ALU.mult, ALU.add))
                    nc.gpsimd.tensor_tensor(rnorm[:, c], ssq[:, c], power[:, c], ALU.pow).then_inc(s_rms, 1)

            rstd(3)
            rms(0)
            pool.wait_ge(s_tt, NG)
            nc.gpsimd.memset(VA[:, :, :, HD:2 * HD], 1.0).then_inc(s_pads, 1)
            pool.wait_ge(s_pads, 1)
            pool.wait_ge(s_small2, 16 * len(SMALL2))
            pool.wait_ge(s_adj_out, 16)
            for v in range(KV_HEADS):
                nc.gpsimd.tensor_scalar(KS[v][96:128, :], ones[96:128, 0:1].to_broadcast([32, TP]), k_pad[96:128, 0:1], None,
                                        ALU.mult).then_inc(s_pads, 1)
                pool.wait_ge(s_pads, v + 2)
            pool.wait_ge(s_small2, 16 * len(SMALL2))
            for v in (3, 8):
                link(nc.gpsimd.tensor_scalar(bn[:, v, :], bn[:, v, :], EPS_BN, None, ALU.add))
                nc.gpsimd.tensor_tensor(bn[:, v, :], bn[:, v, :], power[:, 0:8], ALU.pow).then_inc(s_bnr, 1)
            rms(1)
            rstd(4)
            rstd(5)
            rstd(6, sinv)
            rstd(7)

        @block.vector
        def _(dve):
            order = [0]

            def link(ins):
                order[0] += 1
                ins.then_inc(s_dve, 1)
                dve.wait_ge(s_dve, order[0])

            def adj_tile(k):
                dve.wait_ge(s_adj_hi, k + 1)
                nc.vector.tensor_tensor(adj_lo[:, k, :], R[k % 4][:], adj_hi[:, k, :].bitcast(F32), ALU.subtract).then_inc(s_adj_lo, 1)

            def norm_stats(src):
                for g in range(NG):
                    for t in GROUPS[g]:
                        ins = nc.vector.bn_stats(stats[:, t, :], tile(src, t))
                    link(ins)
                    for t in GROUPS[g]:
                        ins = nc.vector.bn_aggr(mv[:, t, :], stats[:, t, :])
                    ins.then_inc(s_var, 1)

            def normalise(dst, n, ready, groups=GROUPS):
                for group in groups:
                    dve.wait_ge(s_rstd, NG * n + group[-1] // 4 + 1)
                    for t in group:
                        ins = nc.vector.tensor_scalar(tile(dst, t), tile(x, t), mv[:, t, 0:1], rss[:, t:t + 1], ALU.subtract, ALU.mult)
                    ins.then_inc(ready, 1)

            def lo_part(n):
                for g in range(NG):
                    dve.wait_ge(s_hi, NG * n + g + 1)
                    nc.vector.tensor_tensor(split_lo[:, COLS[g]], R[0][:, COLS[g]], split_hi[:, COLS[g]].bitcast(F32), ALU.subtract).then_inc(s_lo, 1)

            def operand_lo(n):
                for g in range(NG):
                    dve.wait_ge(s_thi, NG * n + g + 1)
                    nc.vector.tensor_tensor(split_lo[:, COLS[g]], PS[g][:, 0:WIDTH[g]], split_hi[:, COLS[g]].bitcast(F32), ALU.subtract).then_inc(s_tlo, 1)

            def times_rms(n):
                for g in range(NG):
                    dve.wait_ge(s_rms, NG * n + g + 1)
                    for t in GROUPS[g]:
                        ins = nc.vector.tensor_scalar(tile(R[0], t), tile(xn, t), rnorm[:, t:t + 1], None, ALU.mult)
                    ins.then_inc(s_tin, 1)

            def over(small, experts):
                return small.unsqueeze(2).to_broadcast([P, NT, experts])

            def softmax_begin(n, experts, bias):
                dve.wait_ge(s_lgp, n + 1)
                src = PS[6][:, 0:NT * 8].rearrange("p (t e) -> p t e", e=8)[:, :, 0:experts]
                l = lg[:, :, 0:experts]
                if bias is None:
                    link(nc.vector.tensor_copy(l, src))
                else:
                    link(nc.vector.tensor_tensor(l, src, bias[:, 0:experts].unsqueeze(1).to_broadcast([P, NT, experts]), ALU.add))
                link(nc.vector.tensor_reduce(rt[:, 0, :], l, AX.X, ALU.max))
                nc.vector.tensor_tensor(l, l, over(rt[:, 0, :], experts), ALU.subtract).then_inc(s_lg, 1)

            def softmax_end(n, experts):
                p = probs[:, :, 0:experts]
                dve.wait_ge(s_ex, n + 1)
                link(nc.vector.tensor_reduce(rt[:, 0, :], p, AX.X, ALU.add))
                link(nc.vector.reciprocal(rt[:, 1, :], rt[:, 0, :]))
                link(nc.vector.tensor_tensor(p, p, over(rt[:, 1, :], experts), ALU.mult))

            def best(onehot, src, experts, value):
                sc = score[:, :, 0:experts]
                link(nc.vector.tensor_reduce(rt[:, value, :], src, AX.X, ALU.max))
                link(nc.vector.tensor_tensor(sc, src, over(rt[:, value, :], experts), ALU.is_equal))
                link(nc.vector.tensor_tensor(sc, sc, descend[:, 0:experts].unsqueeze(1).to_broadcast([P, NT, experts]), ALU.mult))
                link(nc.vector.tensor_reduce(rt[:, 0, :], sc, AX.X, ALU.max))
                link(nc.vector.tensor_tensor(onehot, sc, over(rt[:, 0, :], experts), ALU.is_equal))

            def top2(experts):
                f, s2, l, p = (b[:, :, 0:experts] for b in (first, second, lg, probs))
                best(f, p, experts, 2)
                link(nc.vector.scalar_tensor_tensor(l, f, -2.0, p, ALU.mult, ALU.add))
                best(s2, l, experts, 3)

            def accumulate(dst_bank, s, g):
                for t in GROUPS[g]:
                    ins = nc.vector.scalar_tensor_tensor(tile(x, t), tile(dst_bank, t % 4), wcol[s][:, t:t + 1], tile(x, t), ALU.mult, ALU.add)
                return ins

            def later_layers():
                dve.wait_ge(s_small2, 16 * len(SMALL2))
                dve.wait_ge(s_whi, 1)
                nc.vector.scalar_tensor_tensor(a_wlo[:], a_w[:], a_ln1[:, 0:1], a_whi[:].bitcast(F32), ALU.mult, ALU.subtract).then_inc(s_wlo, 1)
                nc.vector.scalar_tensor_tensor(a_rlo[:], a_router[:], a_ln2[:, 0:1], a_rhi[:].bitcast(F32), ALU.mult, ALU.subtract)
                nc.vector.tensor_tensor(r2_lo[:], r2_w1[:], r2_hi[:].bitcast(F32), ALU.subtract).then_inc(s_wlo, 1)
                nc.vector.tensor_tensor(r3_lo[:], r3_w[:], r3_hi[:].bitcast(F32), ALU.subtract).then_inc(s_wlo, 1)
                nc.vector.tensor_copy(mask[:], mask_f[:])
                norm_stats(x)
                normalise(xn, 3, s_xn)
                times_rms(0)
                operand_lo(0)
                dve.wait_ge(s_trig, 32)
                dve.wait_ge(s_adj_out, 16)
                for g in range(NG):
                    bq, br, bk = (0, 1, 2) if g == 1 else (3, 4, 5)
                    w, c = WIDTH[g], COLS[g]
                    dve.wait_ge(s_q, g + 1)
                    nc.vector.tensor_tensor(R[1][:, c], PS[bq][:, 0:w], R[3][:, c], ALU.mult)
                    link(nc.vector.tensor_tensor(R[2][:, c], PS[br][:, 0:w], R[4][:, c], ALU.mult))
                    nc.vector.tensor_tensor(R[1][:, c], R[1][:, c], R[2][:, c], ALU.add).then_inc(s_qr, 1)
                    nc.vector.tensor_tensor(k_scratch[:, 0:w], PS[bk][0:64, 0:w], R[3][0:64, c], ALU.mult)
                    dve.wait_ge(s_qr, g + 1)
                    link(nc.vector.tensor_tensor(R[2][0:64, c], PS[bk][64:128, 0:w], R[4][64:128, c], ALU.mult))
                    nc.vector.tensor_tensor(R[2][0:64, c], R[2][0:64, c], k_scratch[:, 0:w], ALU.add).then_inc(s_kr, 1)
                    dve.wait_ge(s_qh, g + 1)
                    nc.vector.tensor_tensor(QL[:, c], R[1][:, c], QH[:, c].bitcast(F32), ALU.subtract).then_inc(s_ql, 1)
                    dve.wait_ge(s_kh, g + 1)
                    nc.vector.tensor_tensor(KHL[64:128, c], R[2][0:64, c], KHL[0:64, c].bitcast(F32), ALU.subtract).then_inc(s_kl, 1)
                dve.wait_ge(s_kl, NG)
                link(nc.vector.memset(R[4][:, 0:512], 0.0))
                n_max = 0
                finished = None

                def divide(g):
                    dve.wait_ge(s_yl, HEADS * (g + 1))
                    link(nc.vector.reciprocal(RL[:, 0:WIDTH[g]], RL[:, 0:WIDTH[g]]))
                    nc.vector.tensor_tensor(YT[:, COLS[g]], YT[:, COLS[g]], RL[:, 0:WIDTH[g]], ALU.mult).then_inc(s_y, 1)

                for kind, g, h, item in schedule:
                    if kind == "max":
                        t, k0, width, c = item
                        dve.wait_ge(s_mx, n_max + 1)
                        nc.vector.tensor_reduce(mxc[:, t * HEADS + h, c:c + 1], PS[n_max % 3][:, 0:width], AX.X, ALU.max).then_inc(s_mxr, 1)
                        n_max += 1
                    elif kind == "rows":
                        n = len(GROUPS[g]) * HEADS
                        dve.wait_ge(s_mxr, n_max)
                        link(nc.vector.tensor_reduce(m_neg[:, 0:n], mxc[:, 4 * g * HEADS:4 * g * HEADS + n, 0:g + 1], AX.X, ALU.max))
                        link(nc.vector.tensor_scalar(m_hi[:, 0:n], m_neg[:, 0:n], -1.0, None, ALU.mult))
                        if g > 0:
                            dve.wait_ge(s_mt, g)
                        nt = len(GROUPS[g])
                        hi3 = m_hi[:, 0:n].bitcast(F32).rearrange("p (t h) -> p t h", h=HEADS)
                        nc.vector.tensor_copy(MT[:, 0:nt, :, 0], hi3)
                        nc.vector.scalar_tensor_tensor(MT[:, 0:nt, :, 1], m_neg[:, 0:n].rearrange("p (t h) -> p t h", h=HEADS), -1.0, hi3,
                                                       ALU.mult, ALU.subtract).then_inc(s_m, 1)
                    elif kind in ("key", "stack"):
                        continue
                    elif h == HEADS - 1:
                        finished = g
                    if finished is not None and (kind == "head" and h == 0 or kind == "max" and c == 0 and t > 4 * g):
                        divide(finished)
                        finished = None
                divide(finished)
                for g in range(NG):
                    dve.wait_ge(s_wo, g + 1)
                    nc.vector.tensor_tensor(xn[:, COLS[g]], xn[:, COLS[g]], PS[g][:, 0:WIDTH[g]], ALU.add).then_inc(s_x2, 1)
                dve.wait_ge(s_x2, NG)
                link(nc.vector.tensor_tensor(x[:], x[:], xn[:], ALU.add))
                times_rms(1)
                operand_lo(1)
                def split_moe(s, count):
                    dve.wait_ge(s_mhi, count)
                    nc.vector.scalar_tensor_tensor(w_lo[s][:], w_raw, a_ln2[:, 0:1], w_hi[s][:].bitcast(F32), ALU.mult, ALU.subtract).then_inc(s_mlo, 1)

                def moe(unit):
                    up, down, ahead = unit(0), unit(-1), unit(NG)
                    if up:
                        w = WIDTH[up.group]
                        for j in range(3):
                            b = (up.parity + j) % 2
                            dve.wait_ge(s_ms, up.n * 3 + (j + 1))
                            wait_count(dve, s_my, up.n - 1)
                            nc.vector.tensor_tensor(HB[up.parity][j][:, 0:w], SB[b][:, 0:w], PS[2 + b][:, 0:w], ALU.mult).then_inc(s_mh, 1)
                        if up.group == 1 and ahead:
                            split_moe(ahead.slot, ahead.expert + 1)
                    if down:
                        wait_count(dve, s_ma, down.n - 2)
                        if down.group == 0:
                            nc.vector.tensor_copy(wcol[down.slot][:].unsqueeze(2), wgt[:, :, bass.ds(down.expert, 1)]).then_inc(s_wcol, 1)
                            dve.wait_ge(s_wcol, down.expert + 1)
                        dve.wait_ge(s_my, down.n + 1)
                        accumulate(PS[4 + down.parity], down.slot, down.group).then_inc(s_ma, 1)

                def route():
                    softmax_end(0, E1)
                    top2(E1)
                    link(nc.vector.tensor_tensor(rt[:, 4, :], rt[:, 2, :], rt[:, 3, :], ALU.add))
                    link(nc.vector.tensor_scalar(rt[:, 4, :], rt[:, 4, :], 1e-9, None, ALU.add))
                    link(nc.vector.reciprocal(rt[:, 5, :], rt[:, 4, :]))
                    link(nc.vector.tensor_tensor(wgt[:], first[:], over(rt[:, 2, :], E1), ALU.mult))
                    link(nc.vector.tensor_tensor(second[:], second[:], over(rt[:, 3, :], E1), ALU.mult))
                    link(nc.vector.tensor_tensor(wgt[:], wgt[:], second[:], ALU.add))
                    link(nc.vector.tensor_tensor(wgt[:], wgt[:], over(rt[:, 5, :], E1), ALU.mult))

                split_moe(0, 1)
                softmax_begin(0, E1, None)
                expert_slots(dve, E1, 1, moe, {0: route})
                dve.wait_ge(s_ma, NG * E1)
                norm_stats(x)
                normalise(R[0], 4, s_feat)
                lo_part(2)
                for g in range(NG):
                    dve.wait_ge(s_mix, 2 * NG + g + 1)
                    ins = nc.vector.tensor_tensor(x[:, COLS[g]], x[:, COLS[g]], PS[3 + g][:, 0:WIDTH[g]], ALU.add)
                ins.then_inc(s_xup, 1)
                dve.wait_ge(s_xup, 1)

                def add_bias_term(n):
                    def add(g):
                        dve.wait_ge(s_exp[n]["accumulated"], g + 2)
                        dve.wait_ge(s_b3, NG * n + g + 1)
                        nc.vector.tensor_tensor(x[:, COLS[g]], x[:, COLS[g]], PS[6][:, 0:WIDTH[g]], ALU.add).then_inc(s_badd, 1)
                        dve.wait_ge(s_badd, NG * n + g + 1)

                    return {3 + g: (lambda g=g: add(g)) for g in range(NG)}

                def split_expert(n, par, e, s):
                    sems = s_exp[n]
                    nc.vector.tensor_copy(pcol[s][:].unsqueeze(2), par[:, :, bass.ds(e, 1)])
                    dve.wait_ge(sems["w1_hi"], e + 1)
                    nc.vector.tensor_tensor(w_lo[s][:, 0:P], w_raw[:, 0:P], w_hi[s][:, 0:P].bitcast(F32), ALU.subtract).then_inc(sems["w1_lo"], 1)

                def expert_layer(n, experts, par, after):
                    sems = s_exp[n]

                    def work(unit):
                        one, three_, ahead = unit(0), unit(-2), unit(NG)
                        if one and one.group == 1 and ahead:
                            wait_count(dve, sems["hidden2"], one.n - 1)
                            split_expert(n, par, ahead.expert, ahead.slot)
                        if three_:
                            wait_count(dve, sems["accumulated"], three_.n - 2)
                            if three_.group == 0:
                                nc.vector.tensor_copy(wcol[three_.slot][:].unsqueeze(2), wgt[:, :, bass.ds(three_.expert, 1)]).then_inc(sems["column"], 1)
                                dve.wait_ge(sems["column"], three_.expert + 1)
                            dve.wait_ge(sems["product3"], three_.n + 1)
                            accumulate(PS[4 + three_.parity], three_.slot, three_.group).then_inc(sems["accumulated"], 1)

                    expert_slots(dve, experts, 2, work, after)
                    dve.wait_ge(sems["accumulated"], NG * experts)

                norm_stats(x)
                normalise(R[0], 5, s_tin)
                operand_lo(2)
                split_expert(0, par2, 0, 0)
                softmax_begin(1, E2, r2_b2)

                def best_two():
                    softmax_end(1, E2)
                    top2(E2)
                    nc.vector.tensor_tensor(rt[:, 4, :], rt[:, 3, :], rt[:, 2, :], ALU.subtract).then_inc(s_m2, 1)

                def weigh_two():
                    dve.wait_ge(s_e2, 1)
                    link(nc.vector.tensor_scalar(rt[:, 0, :], rt[:, 5, :], 1.0, None, ALU.add))
                    link(nc.vector.reciprocal(rt[:, 1, :], rt[:, 0, :]))
                    link(nc.vector.tensor_tensor(rt[:, 5, :], rt[:, 5, :], rt[:, 1, :], ALU.mult))
                    w = wgt[:, :, 0:E2]
                    link(nc.vector.tensor_tensor(w, first[:, :, 0:E2], over(rt[:, 1, :], E2), ALU.mult))
                    link(nc.vector.tensor_tensor(second[:, :, 0:E2], second[:, :, 0:E2], over(rt[:, 5, :], E2), ALU.mult))
                    nc.vector.tensor_tensor(w, w, second[:, :, 0:E2], ALU.add).then_inc(s_wgt, 1)
                    dve.wait_ge(s_wgt, 1)

                expert_layer(0, E2, par2, {0: best_two, 1: weigh_two, **add_bias_term(0)})
                norm_stats(x)
                normalise(R[0], 6, s_feat)
                lo_part(3)
                for g in range(NG):
                    dve.wait_ge(s_mix, 3 * NG + g + 1)
                    for t in GROUPS[g]:
                        ins = nc.vector.scalar_tensor_tensor(tile(x, t), tile(PS[3 + g], t % 4), sinv[:, t:t + 1], tile(x, t), ALU.mult, ALU.add)
                ins.then_inc(s_xup, 1)
                dve.wait_ge(s_xup, 2)
                dve.wait_ge(s_bnr, 2)
                for k in range(2):
                    link(nc.vector.tensor_tensor(par3[:, 2 * k, :], bn[:, 5 * k, :], bn[:, 5 * k + 3, :], ALU.mult))
                    link(nc.vector.tensor_tensor(par3[:, 2 * k + 1, :], bn[:, 5 * k + 4, :], bn[:, 5 * k + 2, :], ALU.subtract))
                    link(nc.vector.tensor_tensor(par3[:, 2 * k + 1, :], par3[:, 2 * k + 1, :], par3[:, 2 * k, :], ALU.mult))
                    link(nc.vector.tensor_tensor(par3[:, 2 * k + 1, :], par3[:, 2 * k + 1, :], bn[:, 5 * k + 1, :], ALU.add))
                norm_stats(x)
                normalise(R[0], 7, s_tin)
                operand_lo(3)
                split_expert(1, par3, 0, 0)
                softmax_begin(2, E3, r3_b)

                def weigh_all():
                    softmax_end(2, E3)
                    nc.vector.tensor_copy(wgt[:], probs[:]).then_inc(s_wgt, 1)
                    dve.wait_ge(s_wgt, 2)

                expert_layer(1, E3, par3, {0: weigh_all, **add_bias_term(1)})

            dve.wait_ge(s_consts, 1)
            nc.vector.tensor_copy(ones_r[:], ones[:]).then_inc(s_consts, 1)
            dve.wait_ge(s_small, 5 * 16)
            link(nc.vector.tensor_copy(ident_r[:], ident[:]))
            nc.vector.tensor_scalar(f0_m[:], f0_wt[:], f0_lnw[:, 0:1], None, ALU.mult).then_inc(s_f0_m, 1)
            nc.vector.tensor_scalar(f0_lnb_b[:], f0_lnb_b[:], f0_lnb[:, 0:1], None, ALU.mult).then_inc(s_f0_m, 1)
            dve.wait_ge(s_x, 16)
            norm_stats(x)
            for k in range(NT):
                adj_tile(k)
            dve.wait_ge(s_f0_mm, 1)
            link(nc.vector.tensor_tensor(f0_m[:], f0_m[:], PS[7][:, 0:P], ALU.subtract))
            link(nc.vector.tensor_tensor(f0_b[:], f0_b[:], PS[7][:, P:2 * P], ALU.add))
            nc.vector.tensor_scalar(f0_m[:], f0_m[:], GAIN, None, ALU.mult)
            nc.vector.tensor_scalar(f0_b[:], f0_b[:], GAIN, None, ALU.mult).then_inc(s_f0_w, 1)
            dve.wait_ge(s_deg_col, 1)
            nc.vector.tensor_copy(deg[:], PS[6][:, 0:NT])
            nc.vector.tensor_scalar(deg1[:], PS[6][:, 0:NT], 1.0, None, ALU.add).then_inc(s_deg, 1)
            dve.wait_ge(s_deg, 1)
            nc.vector.reciprocal(rdeg[:], deg1[:])
            normalise(R[0], 0, s_feat)
            lo_part(0)
            dve.wait_ge(s_dinv, 1)
            for g in range(NG):
                dve.wait_ge(s_mix, g + 1)
                for t in GROUPS[g]:
                    ins = nc.vector.tensor_scalar(tile(R[2], t), tile(PS[3 + g], t % 4), dinv[:, t:t + 1], 0.0, ALU.mult, ALU.max)
                ins.then_inc(s_relu, 1)
            for g in range(NG):
                dve.wait_ge(s_rnorm, g + 1)
                for t in GROUPS[g]:
                    ins = nc.vector.scalar_tensor_tensor(tile(x, t), tile(R[2], t), rnorm[:, t:t + 1], tile(x, t), ALU.mult, ALU.add)
            link(ins)
            norm_stats(x)
            normalise(R[0], 1, s_h, FG)

            def slot(place, count, valid):
                if valid(0):
                    g = place(0)
                    dve.wait_ge(s_hr, count(0))
                    dve.wait_ge(s_p, count(0))
                    for m, t in enumerate(FG[g]):
                        ins = nc.vector.scalar_tensor_tensor(tile(R[0], t), tile(PS[NF + g], m), rss[:, t:t + 1], f0_b[:], ALU.mult, ALU.add)
                    ins.then_inc(s_h, 1)
                if valid(2):
                    g = place(2)
                    dve.wait_ge(s_h2, count(2))
                    for t in FG[g]:
                        ins = nc.vector.bn_stats(stats[:, t, :], tile(R[0], t))
                    ins.then_inc(s_st, 1)
                    dve.wait_ge(s_st, count(2))
                if valid(3):
                    c = FCOLS[place(3)]
                    dve.wait_ge(s_sg, count(3))
                    nc.vector.tensor_tensor(R[0][:, c], R[0][:, c], R[1][:, c], ALU.mult).then_inc(s_h2, 1)
                if valid(2):
                    for t in FG[place(2)]:
                        ins = nc.vector.bn_aggr(mv[:, t, :], stats[:, t, :])
                    ins.then_inc(s_hv, 1)

            recurrent_slots(dve, slot)
            dve.wait_ge(s_h, NF * (ITERS + 1))
            link(nc.vector.scalar_tensor_tensor(x[:], R[0][:], 1 / GAIN, x[:], ALU.mult, ALU.add))
            norm_stats(x)
            normalise(R[0], 2, s_feat)
            lo_part(1)
            for g in range(NG):
                dve.wait_ge(s_mix, NG + g + 1)
                for t in GROUPS[g]:
                    ins = nc.vector.scalar_tensor_tensor(tile(R[2], t), tile(PS[3 + g], t % 4), rdeg[:, t:t + 1], l1_bias[:], ALU.mult, ALU.add)
                ins.then_inc(s_pre, 1)
            for g in range(NG):
                dve.wait_ge(s_tanh1, g + 1)
                ins = nc.vector.tensor_tensor(x[:, COLS[g]], x[:, COLS[g]], R[2][:, COLS[g]], ALU.add)
            link(ins)
            later_layers()
            nc.vector.engine_nop().then_inc(s_final, 1)

        @block.sync
        def _(sp):
            sp.wait_ge(s_final, 1)
            full = NT - 1
            sp.dma_start(out[0:full * P, :].rearrange("(t p) c -> p t c", p=P),
                         x[:, 0:full * P].rearrange("p (t c) -> p t c", c=P)).then_inc(s_out, 16)
            sp.dma_start(out[full * P:T, :], x[0:T - full * P, full * P:]).then_inc(s_out, 16)
            sp.wait_ge(s_out, 32)


def kernel(**inputs):
    import concourse.bacc as bacc
    from concourse.bass_utils import run_bass_kernel_spmd

    a = {k: np.asarray(v) for k, v in inputs.items()}
    f32 = np.float32

    def rep(v):
        return np.broadcast_to(v, (P,) + v.shape)

    adj_t = np.eye(TP, dtype=f32)
    adj_t[:T, :T] = a["adj"].T
    x_pad = np.zeros((TP, P), f32)
    x_pad[:T] = a["x"]
    arrays = {
        "x": x_pad,
        "adj_t": adj_t,
        "ident": np.eye(P, dtype=f32),
        "f0_wt": a["L0_ffn_W"].T,
        "f0_lnw": a["L0_ffn_ln_w"][:, None],
        "f0_lnb": a["L0_ffn_ln_b"][:, None],
        "f0_b": rep(a["L0_ffn_b"]),
        "gnn_w": np.stack([a["L0_gnn_W"], a["L1_gnn_W"], a["L3_gnn_W"].T], axis=1),
        "l1_bias": rep(a["L1_gnn_b"]),
        "l2_scale": a["L2_gnn_W"][:, None],
    }
    inv_freq = 1.0 / 10000.0 ** (np.arange(0, HD, 2, dtype=f32) / HD)
    freqs = np.outer(np.arange(TP, dtype=f32), inv_freq).astype(f32)
    emb = np.concatenate([freqs, freqs], axis=-1)
    sign = np.where(np.arange(HD) < HD // 2, -1, 1).astype(f32)[:, None]
    arrays["cos"] = np.tile(np.cos(emb).T, (P // HD, 1)).astype(f32)
    arrays["sin"] = np.tile(np.sin(emb).T * sign, (P // HD, 1)).astype(f32)

    def rotated(w):
        return w.reshape(-1, 2, HD // 2, P)[:, ::-1].reshape(w.shape)

    wq, wk, wv = a["L1_ffn_wq"], a["L1_ffn_wk"], a["L1_ffn_wv"]
    arrays["a_w"] = np.concatenate([wq, rotated(wq), wk, rotated(wk), wv]).T
    arrays["a_ln1"] = a["L1_ffn_ln1_w"][:, None]
    arrays["a_ln2"] = a["L1_ffn_ln2_w"][:, None]
    arrays["a_wo"] = a["L1_ffn_wo"].T
    arrays["a_router"] = a["L1_ffn_router_w"].T
    later = np.triu(np.ones((P, P), bool), 1)
    arrays["mask"] = np.concatenate([np.where(later, MASKED, 0), np.where(later.T, MASKED, 0)], axis=1).astype(f32)
    pad_rows = np.zeros((P, 1), f32)
    pad_rows[96:98] = 1
    arrays["k_pad"] = pad_rows
    select_q = np.zeros((P, 2 * HEADS, 96), f32)
    select_k = np.zeros((P, KV_HEADS, 96), f32)
    lane = np.arange(HD)
    for h in range(HEADS):
        select_q[HD * h + lane, h, lane] = 1
        select_q[HD * h + lane, h, HD + lane] = 1
        select_q[HD * h + lane, HEADS + h, 2 * HD + lane] = 1
    for v in range(KV_HEADS):
        for part, first_row in enumerate((0, 64, 0)):
            select_k[first_row + HD * v + lane, v, HD * part + lane] = 1
    arrays["select_q"] = select_q.reshape(P, -1)
    arrays["select_k"] = select_k.reshape(P, -1)
    arrays["descend"] = rep(np.arange(8, 0, -1).astype(f32))
    hid = a["L1_ffn_w1"].shape[1]
    w13 = np.zeros((P, E1, 2, HID), f32)
    w13[:, :, 0, :hid] = a["L1_ffn_w1"].transpose(2, 0, 1)
    w13[:, :, 1, :hid] = a["L1_ffn_w3"].transpose(2, 0, 1)
    arrays["moe_w13"] = w13.reshape(P, E1, 2 * HID)
    down = np.zeros((E1, HID, P), f32)
    down[:, :hid] = a["L1_ffn_w2"].transpose(0, 2, 1)
    arrays["moe_w2"] = down.reshape(E1, 3, P, P).transpose(2, 0, 1, 3).reshape(P, E1, HID)

    def layers3(w1, w2, w3):
        return np.concatenate([w.transpose(1, 0, 2) for w in (w1, w2, w3)], axis=2)

    def columns(v, n=8):
        full = np.zeros((P, n), f32)
        full[:, :v.shape[0]] = v.T
        return full

    arrays["l2_w"] = layers3(a["L2_ffn_expert_w1"], a["L2_ffn_expert_w2"], a["L2_ffn_expert_w3"])
    arrays["l3_w"] = layers3(a["L3_ffn_W1"], a["L3_ffn_W2"], a["L3_ffn_Wo"])
    one = np.ones((P, 8), f32)
    arrays["par2"] = np.stack([one, columns(a["L2_ffn_expert_b1"]), one, columns(a["L2_ffn_expert_b2"])], axis=1)
    arrays["bn"] = np.stack([columns(a["L3_ffn_" + k + n]) for n in "12" for k in ("g", "be", "m", "v", "b")], axis=1)
    rw1 = np.zeros((P, P), f32)
    rw1[:, :64] = a["L2_ffn_router_w1"]
    arrays["r2_w1"] = rw1
    rb1 = np.zeros((P, 1), f32)
    rb1[:64, 0] = a["L2_ffn_router_b1"]
    arrays["r2_b1"] = rb1
    rw2 = np.zeros((P, 8), f32)
    rw2[:64, :E2] = a["L2_ffn_router_w2"]
    arrays["r2_w2"] = rw2
    rb2 = np.zeros(8, f32)
    rb2[:E2] = a["L2_ffn_router_b2"]
    arrays["r2_b2"] = rep(rb2)
    arrays["r3_w"] = a["L3_ffn_Wr"]
    arrays["r3_b"] = rep(a["L3_ffn_br"])
    last_bias = np.zeros((8, 2, P), f32)
    last_bias[:E2, 0] = a["L2_ffn_expert_b3"]
    last_bias[:E3, 1] = a["L3_ffn_bo"]
    arrays["b3"] = last_bias
    nc = bacc.Bacc("TRN2", target_bir_lowering=False, num_devices=1)
    sent, d = {}, {}
    for name, v in arrays.items():
        sent[f"in_{name}"] = np.ascontiguousarray(v)
        d[name] = nc.dram_tensor(f"in_{name}", v.shape, F32, kind="ExternalInput").ap()
    out = nc.dram_tensor("out_x", (T, P), F32, kind="ExternalOutput").ap()
    adj_lo_dram = nc.dram_tensor("adj_lo_store", (P, NT, TP), F32).ap()
    build(nc, d, out, adj_lo_dram)
    r = run_bass_kernel_spmd(nc, [sent], core_ids=[0])
    return r.results[0]["out_x"]
```

```python
from contextlib import ExitStack

import numpy as np

import concourse.bass as bass
from concourse import mybir

F32 = mybir.dt.float32
F32R = mybir.dt.float32r
ALU = mybir.AluOpType
ACT = mybir.ActivationFunctionType
AX = mybir.AxisListType

P = 128
T = 1354
NT = -(-T // P)
TP = NT * P
GROUPS = [range(4 * g, min(4 * g + 4, NT)) for g in range(-(-NT // 4))]
NG = len(GROUPS)
WIDTH = [P * len(g) for g in GROUPS]
COLS = [slice(512 * g, 512 * g + WIDTH[g]) for g in range(NG)]
FG = [range(3 * g, min(3 * g + 3, NT)) for g in range(-(-NT // 3))]
NF = len(FG)
FCOLS = [slice(P * g[0], P * (g[-1] + 1)) for g in FG]
EPS_LN = 1e-5
ITERS = 30
HID = 3 * P
EPS_RMS = 1e-6
EPS_BN = 1e-3
E1, E2, E3 = 8, 6, 8
MASKED = -1e30
GAIN = 100.0
HEADS, KV_HEADS, HD = 4, 2, 32


def tile(buf, t):
    return buf[:, t * P:(t + 1) * P]


def recurrent_slots(eng, slot):
    end = ITERS * NF

    def fixed(n):
        slot(lambda c: (n + c) % NF, lambda c: n + c + 1, lambda c: 0 <= n + c < end)

    for n in range(-NF, 0):
        fixed(n)
    with eng.Fori(0, ITERS - 1) as i:
        for k in range(NF):
            slot(lambda c: (k + c) % NF, lambda c: i * NF + (k + c + 1), lambda c: True)
    for n in range(end - NF, end):
        fixed(n)


class Unit:

    def __init__(self, n, at, expert, pair):
        self.n = n
        self.group = at % NG
        self.slot = at // NG % 2
        self.parity = at % 2
        self.expert = expert
        self.pair = pair


def expert_slots(eng, experts, lag, work, after=None):
    two = 2 * NG
    total = NG * experts

    def fixed(n):
        work(lambda c: Unit(n + c, n + c, (n + c) // NG, (n + c) // two) if 0 <= n + c < total else None)

    for n in range(two):
        fixed(n)
        if after and n in after:
            after[n]()
    with eng.Fori(0, experts // 2 - 2) as i:
        for k in range(two):
            work(lambda c: Unit(i * two + (two + k + c), k + c, i * 2 + (2 + (k + c) // NG), i + (1 + (k + c) // two)))
    for n in range(total - two, total + lag):
        fixed(n)


def of_first_expert(unit):
    return isinstance(unit.expert, int) and unit.expert == 0


def wait_count(eng, semaphore, count):
    if not isinstance(count, int) or count > 0:
        eng.wait_ge(semaphore, count)


def build(nc, d, out, adj_lo_dram):
    ctx = ExitStack()
    with ctx:
        def sb(name, shape, dt=F32):
            return ctx.enter_context(nc.sbuf_tensor(name, shape, dt))

        def sem(name):
            return ctx.enter_context(nc.semaphore(name))

        adj_hi = sb("adj_hi", [P, NT, TP], F32R)
        adj_lo = sb("adj_lo", [P, NT, TP], F32R)
        x = sb("x", [P, TP])
        xn = sb("xn", [P, TP])
        split_hi = sb("split_hi", [P, TP], F32R)
        split_lo = sb("split_lo", [P, TP], F32R)
        R = [sb(f"work{i}", [P, TP]) for i in range(5)]
        ident = sb("ident", [P, P])
        ident_r = sb("ident_r", [P, P], F32R)
        ones = sb("ones", [P, P])
        ones_r = sb("ones_r", [P, P], F32R)
        mean_w = sb("mean_w", [P, P])
        gnn_w = sb("gnn_w", [P, 3, P])
        l1_bias = sb("l1_bias", [P, P])
        l2_scale = sb("l2_scale", [P, 1])
        f0_wt = sb("f0_wt", [P, P])
        f0_lnw = sb("f0_lnw", [P, 1])
        f0_lnb = sb("f0_lnb", [P, 1])
        f0_b = sb("f0_b", [P, P])
        f0_lnb_b = sb("f0_lnb_b", [P, P])
        f0_m = sb("f0_m", [P, P])
        a_w = sb("a_w", [P, 448])
        a_whi = sb("a_whi", [P, 448], F32R)
        a_wlo = sb("a_wlo", [P, 448], F32R)
        a_ln1 = sb("a_ln1", [P, 1])
        a_ln2 = sb("a_ln2", [P, 1])
        a_wo = sb("a_wo", [P, P])
        a_router = sb("a_router", [P, E1])
        a_rboth = sb("a_rboth", [P, 2 * E1], F32R)
        a_rhi, a_rlo = a_rboth[:, 0:E1], a_rboth[:, E1:2 * E1]
        mask_f = sb("mask_f", [P, 2 * P])
        mask = sb("mask", [P, 2 * P], F32R)
        k_pad = sb("k_pad", [P, 1])
        mxc = sb("mxc", [P, NT * HEADS, NG])
        m_neg = sb("m_neg", [P, 16])
        m_hi = sb("m_hi", [P, 16], F32R)
        lg = sb("lg", [P, NT, 8])
        probs = sb("probs", [P, NT, 8])
        first = sb("first", [P, NT, 8])
        second = sb("second", [P, NT, 8])
        score = sb("score", [P, NT, 8])
        wgt = sb("wgt", [P, NT, 8])
        descend = sb("descend", [P, 8])
        rt = sb("rt", [P, 6, NT])
        w_raw = [R[1 + n][:, 1024:1024 + HID] for n in range(2)]
        w_hi = [sb(f"w_hi{i}", [P, 2 * HID], F32R) for i in range(2)]
        w_lo = [sb(f"w_lo{i}", [P, 2 * HID], F32R) for i in range(2)]
        w2_both = sb("w2_both", [P, 2 * HID])
        w2 = [w2_both[:, HID * i:HID * (i + 1)] for i in range(2)]
        k_scratch = w2_both[0:64, :]
        select_q, select_k = w_hi[0][:], w_lo[0][:, 0:2 * 96]
        wcol = [sb(f"wcol{i}", [P, NT]) for i in range(2)]
        pcol = [sb(f"pcol{i}", [P, 4]) for i in range(2)]
        par2 = sb("par2", [P, 4, 8])
        par3 = sb("par3", [P, 4, 8])
        bn = sb("bn", [P, 10, 8])
        r2_w1 = sb("r2_w1", [P, P])
        r2_hi = sb("r2_hi", [P, P], F32R)
        r2_lo = sb("r2_lo", [P, P], F32R)
        r2_b1 = sb("r2_b1", [P, 1])
        r2_w2 = sb("r2_w2", [P, 8])
        r2_b2 = sb("r2_b2", [P, 8])
        r3_w = sb("r3_w", [P, 8])
        r3_both = sb("r3_both", [P, 16], F32R)
        r3_hi, r3_lo = r3_both[:, 0:8], r3_both[:, 8:16]
        r3_b = sb("r3_b", [P, 8])
        b3 = sb("b3", [8, 2, P])
        stats = sb("stats", [P, NT, 6])
        mv = sb("mv", [P, NT, 2])
        rs = sb("rs", [P, NT])
        rss = sb("rss", [P, NT])
        deg = sb("deg", [P, NT])
        deg1 = sb("deg1", [P, NT])
        rdeg = sb("rdeg", [P, NT])
        dinv = sb("dinv", [P, NT])
        sinv = sb("sinv", [P, NT])
        power = sb("power", [P, NT])
        eps_h = sb("eps_h", [P, NT])
        ssq = sb("ssq", [P, NT])
        rnorm = sb("rnorm", [P, NT])
        PS = [ctx.enter_context(nc.psum_tensor(f"bank{b}", [P, 512], F32)) for b in range(8)]

        s_small = sem("small_loaded")
        s_x = sem("x_loaded")
        s_adj = [sem(f"adj_loaded{i}") for i in range(4)]
        s_adj_hi = sem("adj_hi_ready")
        s_adj_lo = sem("adj_lo_ready")
        s_adj_out = sem("adj_lo_stored")
        s_consts = sem("constants_ready")
        s_deg_row = sem("degree_rows_summed")
        s_deg_sb = sem("degree_row_copied")
        s_deg_col = sem("degree_columns_done")
        s_deg = sem("degrees_ready")
        s_dinv = sem("inverse_roots_ready")
        s_f0_m = sem("f0_scaled_weight")
        s_f0_mm = sem("f0_column_means")
        s_f0_w = sem("f0_weight_ready")
        s_var = sem("ln_variance_ready")
        s_rstd = sem("ln_rstd_ready")
        s_feat = sem("features_ready")
        s_hi = sem("split_hi_ready")
        s_lo = sem("split_lo_ready")
        s_agg = sem("aggregated")
        s_aggt = sem("aggregate_copied")
        s_mix = sem("mixed")
        s_relu = sem("relu_ready")
        s_ssq = sem("squares_summed")
        s_rnorm = sem("row_norms_ready")
        s_pre = sem("l1_tanh_input")
        s_tanh1 = sem("l1_tanh_ready")
        s_h = sem("h_ready")
        s_t = sem("tanh_ready")
        s_h1 = sem("h_plus_tanh")
        s_sg = sem("sigmoid_ready")
        s_h2 = sem("h_gated")
        s_st = sem("h_stats_ready")
        s_hv = sem("h_variance_ready")
        s_ve = sem("h_variance_eps")
        s_hr = sem("h_rstd_ready")
        s_tr = sem("h_transposed")
        s_ht = sem("h_transposed_copied")
        s_p = sem("h_projected")
        s_tin = sem("to_transpose_ready")
        s_tt = sem("operand_transposed")
        s_thi = sem("operand_hi_ready")
        s_tlo = sem("operand_lo_ready")
        s_small2 = sem("small2_loaded")
        s_trig = sem("rope_tables_loaded")
        s_xn = sem("xn_ready")
        s_sq3 = sem("rms_squares_summed")
        s_rms = sem("rms_ready")
        s_whi = sem("attention_weights_hi")
        s_wlo = sem("attention_weights_lo")
        s_q = sem("qk_projected")
        s_v = sem("v_projected")
        s_vc = sem("v_copied")
        s_qr = sem("q_roped")
        s_qh = sem("q_hi_ready")
        s_ql = sem("q_lo_ready")
        s_kr = sem("k_roped")
        s_kh = sem("k_hi_ready")
        s_kl = sem("k_lo_ready")
        s_stack = sem("qk_stacked")
        s_mx = sem("scores_for_max")
        s_mxr = sem("scores_reduced")
        s_m = sem("max_ready")
        s_mt = sem("max_transposed")
        s_mrow = sem("max_rows_placed")
        s_sc = sem("scores_ready")
        s_e = sem("exp_ready")
        s_pv = sem("pv_done")
        s_y = sem("head_output_ready")
        s_badd = sem("bias_terms_added")
        s_select = sem("selections_loaded")
        s_selected = sem("selections_rounded")
        s_pads = sem("pads_ready")
        s_stacked = sem("stack_product_ready")
        s_yl = sem("head_sums_copied")
        s_wo = sem("attention_projected")
        s_x2 = sem("attention_residual")
        s_lgp = sem("router_product")
        s_lg = sem("logits_shifted")
        s_ex = sem("router_exp")
        s_wgt = sem("expert_weights_ready")
        s_hid = sem("router_hidden_product")
        s_hidc = sem("router_hidden_ready")
        s_m2 = sem("top2_difference")
        s_e2 = sem("top2_exp")
        s_reload = sem("adj_lo_reloaded")
        s_raw = sem("moe_raw_loaded")
        s_w2 = [sem(f"moe_w2_loaded{i}") for i in range(2)]
        s_mhi = sem("moe_weights_hi")
        s_mlo = sem("moe_weights_lo")
        s_mp = sem("moe_up_products")
        s_ms = sem("moe_silu_ready")
        s_mh = sem("moe_hidden_ready")
        s_my = sem("moe_down_product")
        s_ma = sem("moe_accumulated")
        s_wcol = sem("moe_column_ready")
        s_wt = sem("weights_transposed")
        s_wtc = sem("weights_transposed_copied")
        s_b3 = sem("bias_product")
        s_bnr = sem("bn_roots")
        s_exp = [{k: sem(f"l{n}_{k}") for k in ("w1_loaded", "even_loaded", "odd_loaded", "w1_hi", "w1_lo", "product1", "hidden1", "product2", "hidden2",
                                                "product3", "column", "accumulated")} for n in (2, 3)]
        s_final = sem("result_ready")
        s_out = sem("out_stored")
        s_dve = sem("vector_order")
        s_act = sem("scalar_order")
        s_pool = sem("gpsimd_order")

        QS = [adj_lo[:, h, :] for h in range(HEADS)]
        KS = [adj_lo[:, HEADS + v, :] for v in range(KV_HEADS)]
        QH, QL, KHL = (adj_lo[:, HEADS + KV_HEADS + n, :] for n in range(3))
        VA = R[0][:].rearrange("p (t v c) -> p t v c", v=KV_HEADS, c=2 * HD)
        PT = [R[1][:, 0:512], R[1][:, 512:1024], R[2][:, 0:512]]
        RL = R[2][:, 512:1024]
        YT = R[3]
        MT = R[4][:, 0:512].rearrange("p (t h c) -> p t h c", h=HEADS, c=HD)
        HB = [[R[1 + j][:, 512 * b:512 * b + 512] for j in range(3)] for b in range(2)]
        SB = [R[4][:, 512 * b:512 * b + 512] for b in range(2)]
        SMALL2 = [(a_w, "a_w"), (a_ln1, "a_ln1"), (a_ln2, "a_ln2"), (a_wo, "a_wo"), (a_router, "a_router"), (mask_f, "mask"),
                  (k_pad, "k_pad"), (descend, "descend"), (par2, "par2"), (bn, "bn"), (r2_w1, "r2_w1"), (r2_b1, "r2_b1"),
                  (r2_w2, "r2_w2"), (r2_b2, "r2_b2"), (r3_w, "r3_w"), (r3_b, "r3_b"), (b3, "b3")]

        def max_pieces(g, h):
            for t in GROUPS[g]:
                for c in range(g + 1):
                    yield t, 512 * c, (512 if c < g else (t - 4 * g + 1) * P), c

        def key_steps(g):
            for kt in range(GROUPS[g][-1] + 1):
                yield kt, max(0, kt - 4 * g) * P

        STACKS = HEADS + KV_HEADS

        def stack_bank(m):
            return (6, 7)[m % 2] if m < STACKS else (3, 4, 5, 7)[m % 4]

        def stacks_before(m):
            return max([k + 1 for k in range(m) if stack_bank(k) == stack_bank(m)], default=0)

        def keys_before(g, h):
            return sum(HEADS * len(list(key_steps(b))) for b in range(g)) + h * len(list(key_steps(g)))

        schedule = []
        for h in range(HEADS):
            schedule += [("max", 0, h, piece) for piece in max_pieces(0, h)]
            if h == 0:
                schedule.append(("value", 2, 0, None))
            per_head = (NG - 1) * STACKS // HEADS
            schedule += [("stack", 0, 0, m) for m in range(STACKS + h * per_head, STACKS + (h + 1) * per_head)]
        schedule += [("minus", 0, 0, None), ("rows", 0, 0, None)]
        for g in range(NG):
            steps = [(h, step) for h in range(HEADS) for step in key_steps(g)]
            ahead = [(h, piece) for h in range(HEADS) for piece in max_pieces(g + 1, h)] if g + 1 < NG else []
            room = len(steps) - 5
            for n, (h, step) in enumerate(steps):
                schedule.append(("key", g, h, step))
                take = len(ahead) if n == room - 1 else len(ahead) // max(room - n, 1)
                schedule += [("max", g + 1, hh, piece) for hh, piece in ahead[:take]]
                ahead = ahead[take:]
                if step[0] == GROUPS[g][-1]:
                    schedule.append(("head", g, h, None))
                    if g == NG - 1 and h < NG - 1:
                        schedule.append(("out", h, 0, None))
                if g + 1 < NG and n == room - 1:
                    schedule.append(("minus", g + 1, 0, None))
                if g + 1 < NG and n == room + 2:
                    schedule.append(("rows", g + 1, 0, None))

        block = ctx.enter_context(nc.Block())

        @block.sync
        def _(sp):
            for t, src in ((ident, "ident"), (f0_wt, "f0_wt"), (f0_lnw, "f0_lnw"), (f0_lnb, "f0_lnb"), (f0_b, "f0_b")):
                sp.dma_start(t[:], d[src]).then_inc(s_small, 16)
            sp.dma_start(x[:].rearrange("p (t c) -> p t c", c=P),
                         d["x"].rearrange("(t p) c -> p t c", p=P)).then_inc(s_x, 16)
            for k in range(NT):
                if k >= 4:
                    sp.wait_ge(s_adj_lo, k - 3)
                sp.dma_start(R[k % 4][:], d["adj_t"][k * P:(k + 1) * P, :]).then_inc(s_adj[k % 4], 16)
            for t, src in ((gnn_w, "gnn_w"), (l1_bias, "l1_bias"), (l2_scale, "l2_scale")):
                sp.dma_start(t[:], d[src]).then_inc(s_small, 16)
            for t, src in SMALL2:
                sp.dma_start(t[:], d[src]).then_inc(s_small2, 16)
            sp.dma_start(w2_both[:], d["select_q"]).then_inc(s_select, 16)
            sp.wait_ge(s_selected, 1)
            sp.dma_start(w2_both[:, 0:2 * 96], d["select_k"]).then_inc(s_select, 16)
            sp.wait_ge(s_adj_lo, NT)
            sp.dma_start(adj_lo_dram, adj_lo[:].bitcast(F32)).then_inc(s_adj_out, 16)
            sp.wait_ge(s_ssq, NG)
            sp.dma_start(R[3][:], d["cos"]).then_inc(s_trig, 16)
            sp.dma_start(R[4][:], d["sin"]).then_inc(s_trig, 16)

            def moe_up(e):
                for n in range(2):
                    sp.dma_start(w_raw[n].rearrange("p (a n) -> p a n", a=1),
                                 d["moe_w13"][:, bass.ds(e, 1), HID * n:HID * (n + 1)]).then_inc(s_raw, 16)

            def moe_down(e, s):
                sp.dma_start(w2[s].rearrange("p (a n) -> p a n", a=1), d["moe_w2"][:, bass.ds(e, 1), :]).then_inc(s_w2[s], 16)

            sp.wait_ge(s_kl, NG)
            moe_down(0, 0)
            moe_down(1, 1)
            sp.wait_ge(s_ql, NG)
            moe_up(0)
            sp.wait_ge(s_mlo, 1)
            moe_up(1)
            sp.wait_ge(s_y, NG)
            with sp.Fori(0, E1 // 2 - 1) as i:
                for s in range(2):
                    sp.wait_ge(s_mlo, i * 2 + (s + 2))
                    moe_up(i * 2 + (s + 2))
                    sp.wait_ge(s_my, i * 6 + 3 * (s + 1))
                    moe_down(i * 2 + (s + 2), s)
                    sp.dma_start(adj_lo[:, bass.ds(i * 2 + s, 1), :].bitcast(F32), adj_lo_dram[:, bass.ds(i * 2 + s, 1), :]).then_inc(s_reload, 16)
            sp.dma_start(adj_lo[:, E1 - 2:NT, :].bitcast(F32), adj_lo_dram[:, E1 - 2:NT, :]).then_inc(s_reload, 16)
            for n, experts, src in ((0, E2, "l2_w"), (1, E3, "l3_w")):
                sems = s_exp[n]
                loaded = (sems["even_loaded"], sems["odd_loaded"])

                def load_first(e, s):
                    sp.dma_start(w2[s][:, 0:P].rearrange("p (a n) -> p a n", a=1), d[src][:, bass.ds(e, 1), 0:P]).then_inc(sems["w1_loaded"], 16)

                def load_rest(e, s):
                    sp.dma_start(w2[s][:, P:3 * P].rearrange("p (a n) -> p a n", a=1), d[src][:, bass.ds(e, 1), P:3 * P]).then_inc(loaded[s], 16)

                if n == 0:
                    sp.wait_ge(s_my, NG * E1)
                else:
                    sp.wait_ge(s_exp[0]["product3"], 3 * E2)
                load_first(0, 0)
                load_rest(0, 0)
                load_rest(1, 1)
                sp.wait_ge(sems["w1_lo"], 1)
                load_first(1, 1)
                with sp.Fori(0, experts // 2 - 1) as i:
                    for s in range(2):
                        sp.wait_ge(sems["w1_lo"], i * 2 + (s + 2))
                        load_first(i * 2 + (s + 2), s)
                        sp.wait_ge(sems["product3"], i * 6 + 3 * (s + 1))
                        load_rest(i * 2 + (s + 2), s)

        @block.tensor
        def _(pe):
            mm = nc.tensor.matmul

            pe.wait_ge(s_consts, 2)
            for k in range(NT):
                pe.wait_ge(s_adj_hi, k + 1)
                pe.wait_ge(s_adj_lo, k + 1)
                for g in range(NG):
                    mm(PS[g][:, 0:WIDTH[g]], ones_r[:], adj_hi[:, k, COLS[g]], start=(k == 0), stop=False)
                    last = mm(PS[g][:, 0:WIDTH[g]], ones_r[:], adj_lo[:, k, COLS[g]], start=False, stop=(k == NT - 1))
            last.then_inc(s_deg_row, 1)
            pe.wait_ge(s_f0_m, 2)
            mm(PS[7][:, 0:P], mean_w[:], f0_m[:], start=True, stop=True)
            mm(PS[7][:, P:2 * P], f0_lnb_b[:], f0_wt[:], start=True, stop=True).then_inc(s_f0_mm, 1)
            pe.wait_ge(s_deg_sb, 1)
            for t in range(NT):
                last = mm(PS[6][:, t:t + 1], R[4][0:1, t * P:(t + 1) * P], ones[0:1, 0:1], start=True, stop=True)
            last.then_inc(s_deg_col, 1)

            def aggregate(q, self_loop):
                for g in range(NG):
                    pe.wait_ge(s_hi, NG * aggregate.calls + g + 1)
                    if g < NG - 1:
                        for k in GROUPS[g]:
                            for c in range(NG):
                                high_products(k, c, k == 0)
                            if self_loop:
                                mm(tile(PS[k // 4], k % 4), tile(split_hi, k), ident_r[:], start=False, stop=False)
                        pe.wait_ge(s_lo, NG * aggregate.calls + g + 1)
                        for k in GROUPS[g]:
                            for c in range(NG):
                                low_product(k, c, False)
                            if self_loop:
                                mm(tile(PS[k // 4], k % 4), tile(split_lo, k), ident_r[:], start=False, stop=False)
                pe.wait_ge(s_lo, NG * aggregate.calls + NG)
                for c in range(NG):
                    own_loops = self_loop and c == NG - 1
                    for k in GROUPS[-1]:
                        high_products(k, c, False)
                        last = low_product(k, c, k == NT - 1 and not own_loops)
                    if own_loops:
                        for k in GROUPS[-1]:
                            mm(tile(PS[k // 4], k % 4), tile(split_hi, k), ident_r[:], start=False, stop=False)
                            last = mm(tile(PS[k // 4], k % 4), tile(split_lo, k), ident_r[:], start=False, stop=k == NT - 1)
                    last.then_inc(s_agg, 1)
                aggregate.calls += 1

            aggregate.calls = 0

            def high_products(k, c, start):
                dst = PS[c][:, 0:WIDTH[c]]
                mm(dst, tile(split_hi, k), adj_hi[:, k, COLS[c]], start=start, stop=False)
                mm(dst, tile(split_hi, k), adj_lo[:, k, COLS[c]], start=False, stop=False)

            def low_product(k, c, stop):
                return mm(PS[c][:, 0:WIDTH[c]], tile(split_lo, k), adj_hi[:, k, COLS[c]], start=False, stop=stop)

            def mix(q, w):
                for g in range(NG):
                    pe.wait_ge(s_aggt, NG * q + g + 1)
                    for t in GROUPS[g]:
                        dst = tile(PS[3 + g], t % 4)
                        if w is None:
                            last = nc.tensor.transpose(dst, tile(R[1], t), ident[:])
                        else:
                            last = mm(dst, tile(R[1], t), gnn_w[:, w, :], start=True, stop=True)
                    last.then_inc(s_mix, 1)

            pe.wait_ge(s_small, 8 * 16)
            aggregate(0, True)
            mix(0, 0)
            pe.wait_ge(s_f0_w, 1)

            def slot(place, count, valid):
                if valid(2):
                    g = place(2)
                    pe.wait_ge(s_h2, count(2))
                    for n, t in enumerate(FG[g]):
                        last = nc.tensor.transpose(tile(PS[g], n), tile(R[0], t), ident[:])
                    last.then_inc(s_tr, 1)
                if valid(1):
                    g = place(1)
                    pe.wait_ge(s_ht, count(1))
                    for n, t in enumerate(FG[g]):
                        last = mm(tile(PS[NF + g], n), tile(R[2], t), f0_m[:], start=True, stop=True)
                    last.then_inc(s_p, 1)

            recurrent_slots(pe, slot)
            aggregate(1, True)
            mix(1, 1)

            def transpose_operand(n):
                for g in range(NG):
                    pe.wait_ge(s_tin, NG * n + g + 1)
                    for t in GROUPS[g]:
                        last = nc.tensor.transpose(tile(PS[g], t % 4), tile(R[0], t), ident[:])
                    last.then_inc(s_tt, 1)

            def three(dst, a_hi, a_lo, b_hi, b_lo, start=True, stop=True):
                mm(dst, a_hi, b_hi, start=start, stop=False)
                mm(dst, a_hi, b_lo, start=False, stop=False)
                return mm(dst, a_lo, b_hi, start=False, stop=stop)

            transpose_operand(0)
            def project_v(g):
                for t in GROUPS[g]:
                    last = three(PS[6 + g % 2][:, (t % 4) * 64:(t % 4 + 1) * 64], tile(split_hi, t), tile(split_lo, t),
                                 a_whi[:, 384:448], a_wlo[:, 384:448])
                last.then_inc(s_v, 1)

            pe.wait_ge(s_wlo, 1)
            for g in range(NG):
                pe.wait_ge(s_tlo, NG if g == 1 else g + 1)
                if g == 2:
                    pe.wait_ge(s_kr, 1)
                banks = (0, 1, 2) if g == 1 else (3, 4, 5)
                for n, b in enumerate(banks):
                    w = slice(P * n, P * (n + 1))
                    last = three(PS[b][:, 0:WIDTH[g]], a_whi[:, w], a_wlo[:, w], split_hi[:, COLS[g]], split_lo[:, COLS[g]])
                last.then_inc(s_q, 1)
                if g < 2:
                    project_v(g)

            def stack(m):
                g, n = m // STACKS, m % STACKS
                pe.wait_ge(s_ql, g + 1)
                pe.wait_ge(s_kl, g + 1)
                if stacks_before(m) > 0:
                    pe.wait_ge(s_stack, stacks_before(m))
                dst = PS[stack_bank(m)][0:96, 0:WIDTH[g]]
                if n < HEADS:
                    mm(dst, select_q[:, 96 * n:96 * (n + 1)], QH[:, COLS[g]], start=True, stop=False)
                    last = mm(dst, select_q[:, 96 * (HEADS + n):96 * (HEADS + n + 1)], QL[:, COLS[g]], start=False, stop=True)
                else:
                    last = mm(dst, select_k[:, 96 * (n - HEADS):96 * (n - HEADS + 1)], KHL[:, COLS[g]], start=True, stop=True)
                last.then_inc(s_stacked, 1)

            pe.wait_ge(s_selected, 2)
            pe.wait_ge(s_vc, 2)
            for m in range(STACKS):
                stack(m)
            pe.wait_ge(s_stack, STACKS)
            pe.wait_ge(s_kr, NG)

            n_max = n_key = n_head = 0
            pending = []

            def values(n, g, h, step, first_key, last_key):
                kt, o = step
                pe.wait_ge(s_e, n + 1)
                mm(PS[5 + (g * HEADS + h) % 2][0:2 * HD, o:WIDTH[g]], VA[:, kt, h // 2, :], PT[n % 3][:, 0:WIDTH[g] - o],
                   start=first_key, stop=last_key).then_inc(s_pv, 1)

            def project_out(g):
                pe.wait_ge(s_y, g + 1)
                pe.wait_ge(s_mxr, sum(kind == "max" for kind, *_ in schedule))
                for t in GROUPS[g]:
                    last = mm(tile(PS[g], t % 4), tile(YT, t), a_wo[:], start=True, stop=True)
                last.then_inc(s_wo, 1)

            for kind, g, h, item in schedule:
                if kind == "max":
                    t, k0, width, c = item
                    if n_max >= 3:
                        pe.wait_ge(s_mxr, n_max - 2)
                    dst = PS[n_max % 3]
                    last = mm(dst[:, 0:width], QS[h][0:96, t * P:(t + 1) * P], KS[h // 2][0:96, k0:k0 + width], start=True, stop=c < g)
                    if c == g:
                        last = mm(dst[:, width - P:width], ident_r[:], mask[:, 0:P], start=False, stop=True)
                    last.then_inc(s_mx, 1)
                    n_max += 1
                elif kind == "minus":
                    continue
                elif kind == "value":
                    project_v(g)
                elif kind == "out":
                    project_out(g)
                elif kind == "stack":
                    stack(item)
                elif kind == "rows":
                    if g == 0:
                        pe.wait_ge(s_stack, NG * STACKS)
                    pe.wait_ge(s_m, g + 1)
                    for t in GROUPS[g]:
                        last = nc.tensor.transpose(tile(PS[7], t % 4), R[4][:, (t % 4) * P:(t % 4 + 1) * P], ident[:])
                    last.then_inc(s_mt, 1)
                elif kind == "key":
                    kt, o = item
                    if kt == 0 and h == 0:
                        pe.wait_ge(s_mrow, g + 1)
                        pe.wait_ge(s_vc, NG)
                        pe.wait_ge(s_pads, 1 + KV_HEADS)
                    if n_key >= 2:
                        pe.wait_ge(s_e, n_key - 1)
                    dst = PS[3 + n_key % 2]
                    diagonal = kt >= 4 * g
                    last = mm(dst[:, 0:WIDTH[g] - o], KS[h // 2][:, kt * P:(kt + 1) * P], QS[h][:, 512 * g + o:512 * g + WIDTH[g]],
                              start=True, stop=not diagonal)
                    if diagonal:
                        last = mm(dst[:, 0:P], ident_r[:], mask[:, P:2 * P], start=False, stop=True)
                    last.then_inc(s_sc, 1)
                    if kt == 0 and n_head >= 2:
                        pe.wait_ge(s_yl, n_head - 1)
                    if len(pending) > 0:
                        values(*pending.pop(0))
                    pending.append((n_key, g, h, item, kt == 0, kt == GROUPS[g][-1]))
                    n_key += 1
                else:
                    values(*pending.pop(0))
                    n_head += 1
            project_out(NG - 1)
            transpose_operand(1)
            pe.wait_ge(s_tlo, 2 * NG)

            def logits(both):
                for t in range(NT):
                    mm(PS[6][:, t * 16:t * 16 + 16], tile(split_hi, t), both, start=True, stop=False)
                    last = mm(PS[6][:, t * 16:t * 16 + 8], tile(split_lo, t), both[:, 0:8], start=False, stop=True)
                last.then_inc(s_lgp, 1)

            def moe(unit):
                up, down = unit(0), unit(-1)
                for j in range(3):
                    if j == 2 and down:
                        moe_down(down)
                    if up:
                        s, g = up.slot, up.group
                        if g == 0 and j == 0:
                            pe.wait_ge(s_mlo, up.expert + 1)
                        wait_count(pe, s_mh, up.n * 3 + (j - 1))
                        for b in (0, 2):
                            w = slice(HID * (b // 2) + P * j, HID * (b // 2) + P * (j + 1))
                            last = three(PS[b + (up.parity + j) % 2][:, 0:WIDTH[g]], w_hi[s][:, w], w_lo[s][:, w], split_hi[:, COLS[g]], split_lo[:, COLS[g]])
                        last.then_inc(s_mp, 1)

            def moe_down(down):
                s, g = down.slot, down.group
                if g == 0:
                    pe.wait_ge(s_w2[s], down.pair * 16 + 16)
                pe.wait_ge(s_mh, down.n * 3 + 3)
                wait_count(pe, s_ma, down.n - 1)
                for t in GROUPS[g]:
                    for j in range(3):
                        last = mm(tile(PS[4 + down.parity], t % 4), tile(HB[down.parity][j], t % 4), w2[s][:, j * P:(j + 1) * P],
                                  start=j == 0, stop=j == 2)
                last.then_inc(s_my, 1)

            expert_slots(pe, E1, 1, moe, {0: lambda: logits(a_rboth[:])})
            pe.wait_ge(s_reload, 16 * (E1 - 1))
            pe.wait_ge(s_ma, NG * E1)
            aggregate(2, False)
            mix(2, None)

            def bias_slots(n, experts):
                def transposed(g):
                    pe.wait_ge(s_wgt, n + 1)
                    if g > 0:
                        pe.wait_ge(s_wtc, NG * n + g)
                    for t in GROUPS[g]:
                        last = mm(PS[7][0:experts, (t % 4) * P:(t % 4 + 1) * P], wgt[:, t, 0:experts], ident[:], start=True, stop=True)
                    last.then_inc(s_wt, 1)

                def product(g):
                    pe.wait_ge(s_wtc, NG * n + g + 1)
                    if g > 0:
                        pe.wait_ge(s_badd, NG * n + g)
                    for t in GROUPS[g]:
                        last = mm(tile(PS[6], t % 4), R[3][0:experts, t * P:(t + 1) * P], b3[0:experts, n, :], start=True, stop=True)
                    last.then_inc(s_b3, 1)

                def after_slot(m):
                    if m >= 3:
                        product(m - 3)
                    if m <= 4:
                        transposed(m - 2)

                return {m: (lambda m=m: after_slot(m)) for m in range(2, 6)}

            def expert_layer(n, experts, logits):
                sems = s_exp[n]

                def work(unit):
                    one, two, third = unit(0), unit(-1), unit(-2)
                    if one:
                        if one.group == 0:
                            pe.wait_ge(sems["w1_lo"], one.expert + 1)
                        if isinstance(one.n, int) and one.n < NG:
                            pe.wait_ge(s_tlo, NG * (n + 2) + one.n + 1)
                        three(PS[one.parity][:, 0:WIDTH[one.group]], w_hi[one.slot][:, 0:P], w_lo[one.slot][:, 0:P],
                              split_hi[:, COLS[one.group]], split_lo[:, COLS[one.group]]).then_inc(sems["product1"], 1)
                    if two:
                        if isinstance(two.n, int) and two.n == 0:
                            pe.wait_ge(s_tlo, NG * (n + 3))
                        if two.group == 0:
                            pe.wait_ge(sems["odd_loaded" if two.slot else "even_loaded"], two.pair * 16 + 16)
                        pe.wait_ge(sems["hidden1"], two.n + 1)
                        mm(PS[2 + two.parity][:, 0:WIDTH[two.group]], w2[two.slot][:, P:2 * P], HB[two.parity][0][:, 0:WIDTH[two.group]],
                           start=True, stop=True).then_inc(sems["product2"], 1)
                    if third:
                        pe.wait_ge(sems["hidden2"], third.n + 1)
                        wait_count(pe, sems["accumulated"], third.n - 1)
                        for t in GROUPS[third.group]:
                            last = mm(tile(PS[4 + third.parity], t % 4), tile(HB[third.parity][1], t % 4), w2[third.slot][:, 2 * P:3 * P],
                                      start=True, stop=True)
                        last.then_inc(sems["product3"], 1)

                expert_slots(pe, experts, 2, work, {0: logits, **bias_slots(n, experts)})

            transpose_operand(2)
            pe.wait_ge(s_wlo, 3)
            for g in range(NG):
                pe.wait_ge(s_tlo, 2 * NG + g + 1)
                three(PS[3 + g][:, 0:WIDTH[g]], r2_hi[:], r2_lo[:], split_hi[:, COLS[g]], split_lo[:, COLS[g]]).then_inc(s_hid, 1)

            def logits_of_hidden():
                for t in range(NT):
                    if t % 4 == 0:
                        pe.wait_ge(s_hidc, t // 4 + 1)
                    last = mm(PS[6][:, t * 8:t * 8 + E2], R[4][0:64, t * P:(t + 1) * P], r2_w2[0:64, 0:E2], start=True, stop=True)
                last.then_inc(s_lgp, 1)

            expert_layer(0, E2, logits_of_hidden)

            pe.wait_ge(s_exp[0]["accumulated"], NG * E2)
            aggregate(3, False)
            mix(3, 2)
            transpose_operand(3)
            expert_layer(1, E3, lambda: logits(r3_both[:]))

        @block.scalar
        def _(act):
            order = [0]

            def link(ins):
                order[0] += 1
                ins.then_inc(s_act, 1)
                act.wait_ge(s_act, order[0])

            for k in range(NT):
                act.wait_ge(s_adj[k % 4], 16 * (k // 4 + 1))
                nc.scalar.activation(adj_hi[:, k, :], R[k % 4][:], ACT.Copy).then_inc(s_adj_hi, 1)
            act.wait_ge(s_deg_row, 1)
            for g in range(NG):
                ins = nc.scalar.activation(R[4][0:1, COLS[g]], PS[g][0:1, 0:WIDTH[g]], ACT.Copy)
            ins.then_inc(s_deg_sb, 1)

            def hi_part(n):
                for g in range(NG):
                    act.wait_ge(s_feat, NG * n + g + 1)
                    nc.scalar.activation(split_hi[:, COLS[g]], R[0][:, COLS[g]], ACT.Copy).then_inc(s_hi, 1)

            def copy_aggregate(q):
                for g in range(NG):
                    act.wait_ge(s_agg, NG * q + g + 1)
                    if q == 2:
                        ins = nc.scalar.activation(R[1][:, COLS[g]], PS[g][:, 0:WIDTH[g]], ACT.Identity, scale=l2_scale[:, 0:1])
                    else:
                        ins = nc.scalar.activation(R[1][:, COLS[g]], PS[g][:, 0:WIDTH[g]], ACT.Copy)
                    ins.then_inc(s_aggt, 1)

            hi_part(0)
            copy_aggregate(0)
            for g in range(NG):
                act.wait_ge(s_relu, g + 1)
                for t in GROUPS[g]:
                    ins = nc.scalar.activation(tile(R[3], t), tile(R[2], t), ACT.Square, accum_out=ssq[:, t:t + 1])
                ins.then_inc(s_ssq, 1)
            act.wait_ge(s_select, 16)
            nc.scalar.activation(select_q, w2_both[:], ACT.Copy).then_inc(s_selected, 1)
            nc.scalar.preload_act_table(ACT.Sigmoid)

            def slot(place, count, valid):
                if valid(3):
                    c = FCOLS[place(3)]
                    act.wait_ge(s_h1, count(3))
                    nc.scalar.activation(R[1][:, c], R[0][:, c], ACT.Sigmoid, scale=1 / GAIN).then_inc(s_sg, 1)
                if valid(4):
                    c = FCOLS[place(4)]
                    act.wait_ge(s_h, count(4))
                    nc.scalar.activation(R[1][:, c], R[0][:, c], ACT.Tanh, scale=1 / GAIN).then_inc(s_t, 1)
                if valid(2):
                    g = place(2)
                    act.wait_ge(s_tr, count(2))
                    nc.scalar.activation(R[2][:, FCOLS[g]], PS[g][:, 0:P * len(FG[g])], ACT.Copy).then_inc(s_ht, 1)

            recurrent_slots(act, slot)
            hi_part(1)
            act.wait_ge(s_select, 32)
            nc.scalar.activation(select_k, w2_both[:, 0:2 * 96], ACT.Copy).then_inc(s_selected, 1)
            act.wait_ge(s_small2, 16 * len(SMALL2))
            nc.scalar.activation(a_whi[:], a_w[:], ACT.Copy, scale=a_ln1[:, 0:1])
            nc.scalar.activation(a_rhi, a_router[:], ACT.Copy, scale=a_ln2[:, 0:1])
            nc.scalar.activation(r2_hi[:], r2_w1[:], ACT.Copy)
            nc.scalar.activation(r3_hi, r3_w[:], ACT.Copy).then_inc(s_whi, 1)
            copy_aggregate(1)
            for g in range(NG):
                act.wait_ge(s_pre, g + 1)
                nc.scalar.activation(R[2][:, COLS[g]], R[2][:, COLS[g]], ACT.Tanh).then_inc(s_tanh1, 1)

            def squares(g, ready, dump):
                act.wait_ge(ready, g + 1)
                for t in GROUPS[g]:
                    ins = nc.scalar.activation(tile(dump, t), tile(xn, t), ACT.Square, accum_out=ssq[:, t:t + 1])
                ins.then_inc(s_sq3, 1)

            def operand_hi(n):
                for g in range(NG):
                    act.wait_ge(s_tt, NG * n + g + 1)
                    nc.scalar.activation(split_hi[:, COLS[g]], PS[g][:, 0:WIDTH[g]], ACT.Copy).then_inc(s_thi, 1)

            nc.scalar.preload_act_table(ACT.Exp)
            for g in range(NG):
                squares(g, s_xn, R[1])
            operand_hi(0)

            def copy_stack(m):
                g, n = m // STACKS, m % STACKS
                act.wait_ge(s_stacked, m + 1)
                nc.scalar.activation((QS + KS)[n][0:96, COLS[g]], PS[stack_bank(m)][0:96, 0:WIDTH[g]], ACT.Copy).then_inc(s_stack, 1)

            def copy_v(g):
                act.wait_ge(s_v, g + 1)
                n = len(GROUPS[g])
                nc.scalar.activation(VA[:, 4 * g:4 * g + n, :, 0:HD],
                                     PS[6 + g % 2][:, 0:64 * n].rearrange("p (t v c) -> p t v c", v=KV_HEADS, c=HD), ACT.Copy).then_inc(s_vc, 1)

            def copy_first_stacks(begin, end):
                for m in range(begin, end):
                    copy_stack(m)

            for g in range(NG):
                act.wait_ge(s_qr, g + 1)
                nc.scalar.activation(QH[:, COLS[g]], R[1][:, COLS[g]], ACT.Copy).then_inc(s_qh, 1)
                if g == 2:
                    copy_first_stacks(2, 4)
                act.wait_ge(s_kr, g + 1)
                nc.scalar.activation(KHL[0:64, COLS[g]], R[2][0:64, COLS[g]], ACT.Copy).then_inc(s_kh, 1)
                if g == 2:
                    copy_first_stacks(4, STACKS)
                if g < 2:
                    copy_v(g)
                if g == 1:
                    copy_first_stacks(0, 2)
            n_key = 0
            finished = None

            def split_moe(s, count):
                act.wait_ge(s_raw, count)
                for n in range(2):
                    ins = nc.scalar.activation(w_hi[s][:, HID * n:HID * (n + 1)], w_raw[n], ACT.Copy, scale=a_ln2[:, 0:1])
                ins.then_inc(s_mhi, 1)

            def copy_head(g, h):
                act.wait_ge(s_pv, keys_before(g, h) + len(list(key_steps(g))))
                if h == 0 and g > 0:
                    act.wait_ge(s_y, g)
                bank = PS[5 + (g * HEADS + h) % 2]
                nc.scalar.activation(YT[HD * h:HD * (h + 1), COLS[g]], bank[0:HD, 0:WIDTH[g]], ACT.Copy)
                nc.scalar.activation(RL[HD * h:HD * (h + 1), 0:WIDTH[g]], bank[HD:2 * HD, 0:WIDTH[g]], ACT.Copy).then_inc(s_yl, 1)

            for kind, g, h, item in schedule:
                if kind == "stack":
                    copy_stack(item)
                elif kind == "value":
                    copy_v(g)
                elif kind == "head":
                    finished = (g, h)
                elif kind == "out":
                    split_moe(g, 32 * (g + 1))
                    if g > 0:
                        squares(g - 1, s_x2, R[4])
                elif kind == "rows":
                    act.wait_ge(s_mt, g + 1)
                    for hh in range(HEADS):
                        ins = nc.scalar.activation(QS[hh][96:128, COLS[g]], PS[7][HD * hh:HD * (hh + 1), 0:WIDTH[g]], ACT.Copy)
                    ins.then_inc(s_mrow, 1)
                elif kind == "key":
                    kt, o = item
                    act.wait_ge(s_sc, n_key + 1)
                    if n_key >= 3:
                        act.wait_ge(s_pv, n_key - 2)
                    nc.scalar.activation(PT[n_key % 3][:, 0:WIDTH[g] - o], PS[3 + n_key % 2][:, 0:WIDTH[g] - o], ACT.Exp,
                                         scale=float(HD) ** -0.5).then_inc(s_e, 1)
                    n_key += 1
                    if kt == 1 and finished:
                        copy_head(*finished)
                        finished = None
            copy_head(*finished)
            squares(NG - 2, s_x2, R[4])
            squares(NG - 1, s_x2, R[4])
            operand_hi(1)

            def router_exp(n):
                act.wait_ge(s_lg, n + 1)
                nc.scalar.activation(probs[:], lg[:], ACT.Exp).then_inc(s_ex, 1)

            def moe(unit):
                up = unit(0)
                if not up:
                    return
                w = WIDTH[up.group]
                for j in range(3):
                    b = (up.parity + j) % 2
                    act.wait_ge(s_mp, up.n * 3 + (j + 1))
                    nc.scalar.activation(SB[b][:, 0:w], PS[b][:, 0:w], ACT.Silu).then_inc(s_ms, 1)
                if up.group == 1 and unit(NG) and not of_first_expert(up):
                    split_moe(1 - up.slot, up.expert * 32 + 64)

            nc.scalar.preload_act_table(ACT.Silu)
            expert_slots(act, E1, 0, moe, {0: lambda: router_exp(0)})
            nc.scalar.preload_act_table(ACT.Exp)
            hi_part(2)
            copy_aggregate(2)

            def expert_layer(n, experts, after):
                sems = s_exp[n]

                def hidden(layer, u):
                    act.wait_ge(sems[f"product{layer}"], u.n + 1)
                    w = WIDTH[u.group]
                    nc.scalar.activation(HB[u.parity][layer - 1][:, 0:w], PS[2 * (layer - 1) + u.parity][:, 0:w], ACT.Relu,
                                         scale=pcol[u.slot][:, 2 * layer - 2:2 * layer - 1],
                                         bias=pcol[u.slot][:, 2 * layer - 1:2 * layer]).then_inc(sems[f"hidden{layer}"], 1)

                def work(unit):
                    one, two, ahead = unit(0), unit(-1), unit(NG)
                    if one:
                        hidden(1, one)
                    if two:
                        hidden(2, two)
                    if one and one.group == 1 and ahead:
                        split_expert(n, ahead.slot, ahead.expert * 16 + 16)

                expert_slots(act, experts, 1, work, after)

            def split_expert(n, s, count):
                sems = s_exp[n]
                act.wait_ge(sems["w1_loaded"], count)
                nc.scalar.activation(w_hi[s][:, 0:P], w2[s][:, 0:P], ACT.Copy).then_inc(sems["w1_hi"], 1)

            def transposed_weights(n, experts):
                def copy(g):
                    act.wait_ge(s_wt, NG * n + g + 1)
                    nc.scalar.activation(R[3][0:experts, COLS[g]], PS[7][0:experts, 0:WIDTH[g]], ACT.Copy).then_inc(s_wtc, 1)

                return {2 + g: (lambda g=g: copy(g)) for g in range(NG)}

            operand_hi(2)
            split_expert(0, 0, 16)
            for g in range(NG):
                act.wait_ge(s_hid, g + 1)
                nc.scalar.activation(R[4][:, COLS[g]], PS[3 + g][:, 0:WIDTH[g]], ACT.Relu, bias=r2_b1[:, 0:1]).then_inc(s_hidc, 1)

            def second_exp():
                act.wait_ge(s_m2, 1)
                nc.scalar.activation(rt[:, 5, :], rt[:, 4, :], ACT.Exp).then_inc(s_e2, 1)

            expert_layer(0, E2, {0: lambda: router_exp(1), 1: second_exp, **transposed_weights(0, E2)})
            hi_part(3)
            copy_aggregate(3)
            operand_hi(3)
            split_expert(1, 0, 16)
            expert_layer(1, E3, {0: lambda: router_exp(2), **transposed_weights(1, E3)})

        @block.gpsimd
        def _(pool):
            order = [0]

            def link(ins):
                order[0] += 1
                ins.then_inc(s_pool, 1)
                pool.wait_ge(s_pool, order[0])

            nc.gpsimd.memset(power[:], -0.5)
            nc.gpsimd.memset(eps_h[:], EPS_LN * GAIN * GAIN)
            nc.gpsimd.memset(ones[:], 1.0)
            link(nc.gpsimd.memset(mean_w[:], 1 / P))
            nc.gpsimd.memset(f0_lnb_b[:], 1.0).then_inc(s_consts, 1)

            def rstd(n, scale=None):
                for g in range(NG):
                    c = slice(GROUPS[g][0], GROUPS[g][-1] + 1)
                    pool.wait_ge(s_var, NG * n + g + 1)
                    link(nc.gpsimd.tensor_scalar(rs[:, c], mv[:, c, 1], EPS_LN, None, ALU.add))
                    if scale is None:
                        nc.gpsimd.tensor_tensor(rss[:, c], rs[:, c], power[:, c], ALU.pow).then_inc(s_rstd, 1)
                    else:
                        link(nc.gpsimd.tensor_tensor(rs[:, c], rs[:, c], power[:, c], ALU.pow))
                        if isinstance(scale, float):
                            ins = nc.gpsimd.tensor_scalar(rss[:, c], rs[:, c], scale, None, ALU.mult)
                        else:
                            ins = nc.gpsimd.tensor_tensor(rss[:, c], rs[:, c], scale[:, c], ALU.mult)
                        ins.then_inc(s_rstd, 1)

            for g in range(NG):
                c = slice(GROUPS[g][0], GROUPS[g][-1] + 1)
                pool.wait_ge(s_var, g + 1)
                link(nc.gpsimd.tensor_scalar(rs[:, c], mv[:, c, 1], EPS_LN, None, ALU.add))
                link(nc.gpsimd.tensor_tensor(rs[:, c], rs[:, c], power[:, c], ALU.pow))
            pool.wait_ge(s_deg, 1)
            for g in range(NG):
                c = slice(GROUPS[g][0], GROUPS[g][-1] + 1)
                nc.gpsimd.tensor_tensor(dinv[:, c], deg1[:, c], power[:, c], ALU.pow).then_inc(s_dinv, 1)
                pool.wait_ge(s_dinv, g + 1)
                nc.gpsimd.tensor_tensor(rss[:, c], rs[:, c], dinv[:, c], ALU.mult).then_inc(s_rstd, 1)
            nc.gpsimd.tensor_tensor(sinv[:], deg[:], power[:], ALU.pow).then_inc(s_dinv, 1)
            for g in range(NG):
                c = slice(GROUPS[g][0], GROUPS[g][-1] + 1)
                pool.wait_ge(s_ssq, g + 1)
                link(nc.gpsimd.tensor_scalar(ssq[:, c], ssq[:, c], 1e-24, None, ALU.max))
                nc.gpsimd.tensor_tensor(rnorm[:, c], ssq[:, c], power[:, c], ALU.pow).then_inc(s_rnorm, 1)
            rstd(1, GAIN)

            def slot(place, count, valid):
                if valid(1):
                    g = place(1)
                    c = slice(FG[g][0], FG[g][-1] + 1)
                    pool.wait_ge(s_hv, count(1))
                    nc.gpsimd.tensor_tensor(rs[:, c], mv[:, c, 1], eps_h[:, c], ALU.add).then_inc(s_ve, 1)
                    pool.wait_ge(s_ve, count(1))
                    nc.gpsimd.tensor_tensor(rss[:, c], rs[:, c], power[:, c], ALU.pow).then_inc(s_hr, 1)
                if valid(4):
                    c = FCOLS[place(4)]
                    pool.wait_ge(s_t, count(4))
                    nc.gpsimd.tensor_tensor(R[0][:, c], R[0][:, c], R[1][:, c], ALU.add).then_inc(s_h1, 1)

            recurrent_slots(pool, slot)
            rstd(2)

            def rms(n):
                for g in range(NG):
                    c = slice(GROUPS[g][0], GROUPS[g][-1] + 1)
                    pool.wait_ge(s_sq3, NG * n + g + 1)
                    link(nc.gpsimd.tensor_scalar(ssq[:, c], ssq[:, c], 1 / P, EPS_RMS, ALU.mult, ALU.add))
                    nc.gpsimd.tensor_tensor(rnorm[:, c], ssq[:, c], power[:, c], ALU.pow).then_inc(s_rms, 1)

            rstd(3)
            rms(0)
            pool.wait_ge(s_tt, NG)
            nc.gpsimd.memset(VA[:, :, :, HD:2 * HD], 1.0).then_inc(s_pads, 1)
            pool.wait_ge(s_pads, 1)
            pool.wait_ge(s_small2, 16 * len(SMALL2))
            pool.wait_ge(s_adj_out, 16)
            for v in range(KV_HEADS):
                nc.gpsimd.tensor_scalar(KS[v][96:128, :], ones[96:128, 0:1].to_broadcast([32, TP]), k_pad[96:128, 0:1], None,
                                        ALU.mult).then_inc(s_pads, 1)
                pool.wait_ge(s_pads, v + 2)
            pool.wait_ge(s_small2, 16 * len(SMALL2))
            for v in (3, 8):
                link(nc.gpsimd.tensor_scalar(bn[:, v, :], bn[:, v, :], EPS_BN, None, ALU.add))
                nc.gpsimd.tensor_tensor(bn[:, v, :], bn[:, v, :], power[:, 0:8], ALU.pow).then_inc(s_bnr, 1)
            rms(1)
            rstd(4)
            rstd(5)
            rstd(6, sinv)
            rstd(7)

        @block.vector
        def _(dve):
            order = [0]

            def link(ins):
                order[0] += 1
                ins.then_inc(s_dve, 1)
                dve.wait_ge(s_dve, order[0])

            def adj_tile(k):
                dve.wait_ge(s_adj_hi, k + 1)
                nc.vector.tensor_tensor(adj_lo[:, k, :], R[k % 4][:], adj_hi[:, k, :].bitcast(F32), ALU.subtract).then_inc(s_adj_lo, 1)

            def norm_stats(src, update=None):
                for g in range(NG):
                    if update:
                        link(update(g))
                    for t in GROUPS[g]:
                        ins = nc.vector.bn_stats(stats[:, t, :], tile(src, t))
                    link(ins)
                    for t in GROUPS[g]:
                        ins = nc.vector.bn_aggr(mv[:, t, :], stats[:, t, :])
                    ins.then_inc(s_var, 1)

            def normalise(dst, n, ready, groups=GROUPS, then=None):
                for g, group in enumerate(groups):
                    dve.wait_ge(s_rstd, NG * n + group[-1] // 4 + 1)
                    for t in group:
                        ins = nc.vector.tensor_scalar(tile(dst, t), tile(x, t), mv[:, t, 0:1], rss[:, t:t + 1], ALU.subtract, ALU.mult)
                    ins.then_inc(ready, 1)
                    if then and g > 0:
                        then(g - 1)
                if then:
                    then(len(groups) - 1)

            def features(n, layer):
                def low(g):
                    dve.wait_ge(s_hi, NG * layer + g + 1)
                    nc.vector.tensor_tensor(split_lo[:, COLS[g]], R[0][:, COLS[g]], split_hi[:, COLS[g]].bitcast(F32), ALU.subtract).then_inc(s_lo, 1)

                normalise(R[0], n, s_feat, GROUPS, low)

            def operand_lo(n):
                for g in range(NG):
                    dve.wait_ge(s_thi, NG * n + g + 1)
                    nc.vector.tensor_tensor(split_lo[:, COLS[g]], PS[g][:, 0:WIDTH[g]], split_hi[:, COLS[g]].bitcast(F32), ALU.subtract).then_inc(s_tlo, 1)

            def times_rms(n):
                for g in range(NG):
                    dve.wait_ge(s_rms, NG * n + g + 1)
                    for t in GROUPS[g]:
                        ins = nc.vector.tensor_scalar(tile(R[0], t), tile(xn, t), rnorm[:, t:t + 1], None, ALU.mult)
                    ins.then_inc(s_tin, 1)

            def over(small, experts):
                return small.unsqueeze(2).to_broadcast([P, NT, experts])

            def softmax_begin(n, experts, bias):
                dve.wait_ge(s_lgp, n + 1)
                parts = 1 if n == 1 else 2
                src = PS[6][:, 0:NT * 8 * parts].rearrange("p (t e) -> p t e", e=8 * parts)
                l = lg[:, :, 0:experts]
                if bias is None:
                    link(nc.vector.tensor_copy(l, src[:, :, 0:experts]))
                else:
                    link(nc.vector.tensor_tensor(l, src[:, :, 0:experts], bias[:, 0:experts].unsqueeze(1).to_broadcast([P, NT, experts]), ALU.add))
                if parts == 2:
                    link(nc.vector.tensor_tensor(l, l, src[:, :, 8:8 + experts], ALU.add))
                link(nc.vector.tensor_reduce(rt[:, 0, :], l, AX.X, ALU.max))
                nc.vector.tensor_tensor(l, l, over(rt[:, 0, :], experts), ALU.subtract).then_inc(s_lg, 1)

            def softmax_end(n, experts):
                p = probs[:, :, 0:experts]
                dve.wait_ge(s_ex, n + 1)
                link(nc.vector.tensor_reduce(rt[:, 0, :], p, AX.X, ALU.add))
                link(nc.vector.reciprocal(rt[:, 1, :], rt[:, 0, :]))
                link(nc.vector.tensor_tensor(p, p, over(rt[:, 1, :], experts), ALU.mult))

            def best(onehot, src, experts, value):
                sc = score[:, :, 0:experts]
                link(nc.vector.tensor_reduce(rt[:, value, :], src, AX.X, ALU.max))
                link(nc.vector.tensor_tensor(sc, src, over(rt[:, value, :], experts), ALU.is_equal))
                link(nc.vector.tensor_tensor(sc, sc, descend[:, 0:experts].unsqueeze(1).to_broadcast([P, NT, experts]), ALU.mult))
                link(nc.vector.tensor_reduce(rt[:, 0, :], sc, AX.X, ALU.max))
                link(nc.vector.tensor_tensor(onehot, sc, over(rt[:, 0, :], experts), ALU.is_equal))

            def next_best(f, s2, l, p, experts):
                link(nc.vector.scalar_tensor_tensor(l, f, -2.0, p, ALU.mult, ALU.add))
                best(s2, l, experts, 3)

            def top2(experts):
                f, s2, l, p = (b[:, :, 0:experts] for b in (first, second, lg, probs))
                best(f, p, experts, 2)
                next_best(f, s2, l, p, experts)

            def accumulate(dst_bank, s, g):
                for t in GROUPS[g]:
                    ins = nc.vector.scalar_tensor_tensor(tile(x, t), tile(dst_bank, t % 4), wcol[s][:, t:t + 1], tile(x, t), ALU.mult, ALU.add)
                return ins

            def later_layers():
                def add_second(g):
                    dve.wait_ge(s_tanh1, g + 1)
                    return nc.vector.tensor_tensor(x[:, COLS[g]], x[:, COLS[g]], R[2][:, COLS[g]], ALU.add)

                norm_stats(x, add_second)
                normalise(xn, 3, s_xn)
                times_rms(0)
                operand_lo(0)
                dve.wait_ge(s_trig, 32)
                dve.wait_ge(s_adj_out, 16)
                for g in range(NG):
                    bq, br, bk = (0, 1, 2) if g == 1 else (3, 4, 5)
                    w, c = WIDTH[g], COLS[g]
                    dve.wait_ge(s_q, g + 1)
                    nc.vector.tensor_tensor(R[1][:, c], PS[bq][:, 0:w], R[3][:, c], ALU.mult)
                    link(nc.vector.tensor_tensor(R[2][:, c], PS[br][:, 0:w], R[4][:, c], ALU.mult))
                    nc.vector.tensor_tensor(R[1][:, c], R[1][:, c], R[2][:, c], ALU.add).then_inc(s_qr, 1)
                    nc.vector.tensor_tensor(k_scratch[:, 0:w], PS[bk][0:64, 0:w], R[3][0:64, c], ALU.mult)
                    dve.wait_ge(s_qr, g + 1)
                    link(nc.vector.tensor_tensor(R[2][0:64, c], PS[bk][64:128, 0:w], R[4][64:128, c], ALU.mult))
                    nc.vector.tensor_tensor(R[2][0:64, c], R[2][0:64, c], k_scratch[:, 0:w], ALU.add).then_inc(s_kr, 1)
                    dve.wait_ge(s_qh, g + 1)
                    nc.vector.tensor_tensor(QL[:, c], R[1][:, c], QH[:, c].bitcast(F32), ALU.subtract).then_inc(s_ql, 1)
                    dve.wait_ge(s_kh, g + 1)
                    nc.vector.tensor_tensor(KHL[64:128, c], R[2][0:64, c], KHL[0:64, c].bitcast(F32), ALU.subtract).then_inc(s_kl, 1)
                dve.wait_ge(s_kl, NG)
                link(nc.vector.memset(R[4][:, 0:512], 0.0))
                n_max = 0
                finished = None

                def divide(g):
                    dve.wait_ge(s_yl, HEADS * (g + 1))
                    link(nc.vector.reciprocal(RL[:, 0:WIDTH[g]], RL[:, 0:WIDTH[g]]))
                    nc.vector.tensor_tensor(YT[:, COLS[g]], YT[:, COLS[g]], RL[:, 0:WIDTH[g]], ALU.mult).then_inc(s_y, 1)

                def split_moe(s, count):
                    dve.wait_ge(s_mhi, count)
                    for n in range(2):
                        w = slice(HID * n, HID * (n + 1))
                        ins = nc.vector.scalar_tensor_tensor(w_lo[s][:, w], w_raw[n], a_ln2[:, 0:1], w_hi[s][:, w].bitcast(F32), ALU.mult, ALU.subtract)
                    ins.then_inc(s_mlo, 1)

                def add_attention(g):
                    dve.wait_ge(s_wo, g + 1)
                    nc.vector.tensor_tensor(xn[:, COLS[g]], xn[:, COLS[g]], PS[g][:, 0:WIDTH[g]], ALU.add).then_inc(s_x2, 1)

                for kind, g, h, item in schedule:
                    if kind == "max":
                        t, k0, width, c = item
                        dve.wait_ge(s_mx, n_max + 1)
                        nc.vector.tensor_reduce(mxc[:, t * HEADS + h, c:c + 1], PS[n_max % 3][:, 0:width], AX.X, ALU.max).then_inc(s_mxr, 1)
                        n_max += 1
                    elif kind == "minus":
                        n = len(GROUPS[g]) * HEADS
                        dve.wait_ge(s_mxr, n_max)
                        link(nc.vector.tensor_reduce(m_neg[:, 0:n], mxc[:, 4 * g * HEADS:4 * g * HEADS + n, 0:g + 1], AX.X, ALU.max))
                        link(nc.vector.tensor_scalar(m_hi[:, 0:n], m_neg[:, 0:n], -1.0, None, ALU.mult))
                        if g > 0:
                            dve.wait_ge(s_mt, g)
                        nt = len(GROUPS[g])
                        hi3 = m_hi[:, 0:n].bitcast(F32).rearrange("p (t h) -> p t h", h=HEADS)
                        nc.vector.tensor_copy(MT[:, 0:nt, :, 0], hi3)
                        nc.vector.scalar_tensor_tensor(MT[:, 0:nt, :, 1], m_neg[:, 0:n].rearrange("p (t h) -> p t h", h=HEADS), -1.0, hi3,
                                                       ALU.mult, ALU.subtract).then_inc(s_m, 1)
                    elif kind == "out":
                        add_attention(g)
                        split_moe(g, g + 1)
                    elif kind in ("key", "stack", "rows", "value"):
                        continue
                    elif kind == "head" and h == HEADS - 1:
                        finished = g
                    if finished is not None and (kind == "head" and h == 0 or kind == "max" and c == 0 and t > 4 * g):
                        divide(finished)
                        finished = None
                divide(finished)
                add_attention(NG - 1)
                dve.wait_ge(s_x2, NG)
                link(nc.vector.tensor_tensor(x[:], x[:], xn[:], ALU.add))
                times_rms(1)
                operand_lo(1)
                def moe(unit):
                    up, down, ahead = unit(0), unit(-1), unit(NG)
                    weighed = not (up and isinstance(up.n, int) and up.n == 1)
                    for j in range(3):
                        if j == 2 and down and weighed:
                            sums(down)
                        if up:
                            w = WIDTH[up.group]
                            b = (up.parity + j) % 2
                            dve.wait_ge(s_ms, up.n * 3 + (j + 1))
                            wait_count(dve, s_my, up.n - 1)
                            nc.vector.tensor_tensor(HB[up.parity][j][:, 0:w], SB[b][:, 0:w], PS[2 + b][:, 0:w], ALU.mult).then_inc(s_mh, 1)
                    if up and up.group == 1 and ahead and not of_first_expert(up):
                        split_moe(ahead.slot, ahead.expert + 1)
                    if not weighed:
                        weigh()
                        sums(down)

                def sums(down):
                    wait_count(dve, s_ma, down.n - 2)
                    if down.group == 0:
                        nc.vector.tensor_copy(wcol[down.slot][:].unsqueeze(2), wgt[:, :, bass.ds(down.expert, 1)]).then_inc(s_wcol, 1)
                        dve.wait_ge(s_wcol, down.expert + 1)
                    dve.wait_ge(s_my, down.n + 1)
                    accumulate(PS[4 + down.parity], down.slot, down.group).then_inc(s_ma, 1)

                def route():
                    softmax_begin(0, E1, None)
                    softmax_end(0, E1)
                    best(first[:], probs[:], E1, 2)

                def weigh():
                    next_best(first[:], second[:], lg[:], probs[:], E1)
                    link(nc.vector.tensor_tensor(rt[:, 4, :], rt[:, 2, :], rt[:, 3, :], ALU.add))
                    link(nc.vector.tensor_scalar(rt[:, 4, :], rt[:, 4, :], 1e-9, None, ALU.add))
                    link(nc.vector.reciprocal(rt[:, 5, :], rt[:, 4, :]))
                    link(nc.vector.tensor_tensor(wgt[:], first[:], over(rt[:, 2, :], E1), ALU.mult))
                    link(nc.vector.tensor_tensor(second[:], second[:], over(rt[:, 3, :], E1), ALU.mult))
                    link(nc.vector.tensor_tensor(wgt[:], wgt[:], second[:], ALU.add))
                    link(nc.vector.tensor_tensor(wgt[:], wgt[:], over(rt[:, 5, :], E1), ALU.mult))

                expert_slots(dve, E1, 1, moe, {0: route})
                dve.wait_ge(s_ma, NG * E1)
                norm_stats(x)
                features(4, 2)

                def add_third(g):
                    dve.wait_ge(s_mix, 2 * NG + g + 1)
                    return nc.vector.tensor_tensor(x[:, COLS[g]], x[:, COLS[g]], PS[3 + g][:, 0:WIDTH[g]], ALU.add)

                def add_bias_term(n):
                    def add(g):
                        dve.wait_ge(s_exp[n]["accumulated"], g + 2)
                        dve.wait_ge(s_b3, NG * n + g + 1)
                        nc.vector.tensor_tensor(x[:, COLS[g]], x[:, COLS[g]], PS[6][:, 0:WIDTH[g]], ALU.add).then_inc(s_badd, 1)
                        dve.wait_ge(s_badd, NG * n + g + 1)

                    return {3 + g: (lambda g=g: add(g)) for g in range(NG)}

                def split_expert(n, par, e, s):
                    sems = s_exp[n]
                    nc.vector.tensor_copy(pcol[s][:].unsqueeze(2), par[:, :, bass.ds(e, 1)])
                    dve.wait_ge(sems["w1_hi"], e + 1)
                    nc.vector.tensor_tensor(w_lo[s][:, 0:P], w2[s][:, 0:P], w_hi[s][:, 0:P].bitcast(F32), ALU.subtract).then_inc(sems["w1_lo"], 1)

                def expert_layer(n, experts, par, after):
                    sems = s_exp[n]

                    def work(unit):
                        one, third, ahead = unit(0), unit(-2), unit(NG)
                        if one and one.group == 1 and ahead:
                            wait_count(dve, sems["hidden2"], one.n - 1)
                            split_expert(n, par, ahead.expert, ahead.slot)
                        if third:
                            wait_count(dve, sems["accumulated"], third.n - 2)
                            if third.group == 0:
                                nc.vector.tensor_copy(wcol[third.slot][:].unsqueeze(2), wgt[:, :, bass.ds(third.expert, 1)]).then_inc(sems["column"], 1)
                                dve.wait_ge(sems["column"], third.expert + 1)
                            dve.wait_ge(sems["product3"], third.n + 1)
                            accumulate(PS[4 + third.parity], third.slot, third.group).then_inc(sems["accumulated"], 1)

                    expert_slots(dve, experts, 2, work, after)
                    dve.wait_ge(sems["accumulated"], NG * experts)

                norm_stats(x, add_third)
                normalise(R[0], 5, s_tin)
                operand_lo(2)
                split_expert(0, par2, 0, 0)

                def best_two():
                    softmax_begin(1, E2, r2_b2)
                    softmax_end(1, E2)
                    top2(E2)
                    nc.vector.tensor_tensor(rt[:, 4, :], rt[:, 3, :], rt[:, 2, :], ALU.subtract).then_inc(s_m2, 1)

                def weigh_two():
                    dve.wait_ge(s_e2, 1)
                    link(nc.vector.tensor_scalar(rt[:, 0, :], rt[:, 5, :], 1.0, None, ALU.add))
                    link(nc.vector.reciprocal(rt[:, 1, :], rt[:, 0, :]))
                    link(nc.vector.tensor_tensor(rt[:, 5, :], rt[:, 5, :], rt[:, 1, :], ALU.mult))
                    w = wgt[:, :, 0:E2]
                    link(nc.vector.tensor_tensor(w, first[:, :, 0:E2], over(rt[:, 1, :], E2), ALU.mult))
                    link(nc.vector.tensor_tensor(second[:, :, 0:E2], second[:, :, 0:E2], over(rt[:, 5, :], E2), ALU.mult))
                    nc.vector.tensor_tensor(w, w, second[:, :, 0:E2], ALU.add).then_inc(s_wgt, 1)
                    dve.wait_ge(s_wgt, 1)

                expert_layer(0, E2, par2, {0: best_two, 1: weigh_two, **add_bias_term(0)})
                norm_stats(x)
                features(6, 3)

                def add_fourth(g):
                    dve.wait_ge(s_mix, 3 * NG + g + 1)
                    for t in GROUPS[g]:
                        ins = nc.vector.scalar_tensor_tensor(tile(x, t), tile(PS[3 + g], t % 4), sinv[:, t:t + 1], tile(x, t), ALU.mult, ALU.add)
                    return ins

                dve.wait_ge(s_bnr, 2)
                for k in range(2):
                    link(nc.vector.tensor_tensor(par3[:, 2 * k, :], bn[:, 5 * k, :], bn[:, 5 * k + 3, :], ALU.mult))
                    link(nc.vector.tensor_tensor(par3[:, 2 * k + 1, :], bn[:, 5 * k + 4, :], bn[:, 5 * k + 2, :], ALU.subtract))
                    link(nc.vector.tensor_tensor(par3[:, 2 * k + 1, :], par3[:, 2 * k + 1, :], par3[:, 2 * k, :], ALU.mult))
                    link(nc.vector.tensor_tensor(par3[:, 2 * k + 1, :], par3[:, 2 * k + 1, :], bn[:, 5 * k + 1, :], ALU.add))
                norm_stats(x, add_fourth)
                normalise(R[0], 7, s_tin)
                operand_lo(3)
                split_expert(1, par3, 0, 0)

                def weigh_all():
                    softmax_begin(2, E3, r3_b)
                    softmax_end(2, E3)
                    nc.vector.tensor_copy(wgt[:], probs[:]).then_inc(s_wgt, 1)
                    dve.wait_ge(s_wgt, 2)

                expert_layer(1, E3, par3, {0: weigh_all, **add_bias_term(1)})

            dve.wait_ge(s_consts, 1)
            nc.vector.tensor_copy(ones_r[:], ones[:]).then_inc(s_consts, 1)
            dve.wait_ge(s_small, 5 * 16)
            link(nc.vector.tensor_copy(ident_r[:], ident[:]))
            nc.vector.tensor_scalar(f0_m[:], f0_wt[:], f0_lnw[:, 0:1], None, ALU.mult).then_inc(s_f0_m, 1)
            nc.vector.tensor_scalar(f0_lnb_b[:], f0_lnb_b[:], f0_lnb[:, 0:1], None, ALU.mult).then_inc(s_f0_m, 1)
            dve.wait_ge(s_x, 16)
            norm_stats(x)
            for k in range(NT):
                adj_tile(k)
            dve.wait_ge(s_f0_mm, 1)
            link(nc.vector.tensor_tensor(f0_m[:], f0_m[:], PS[7][:, 0:P], ALU.subtract))
            link(nc.vector.tensor_tensor(f0_b[:], f0_b[:], PS[7][:, P:2 * P], ALU.add))
            nc.vector.tensor_scalar(f0_m[:], f0_m[:], GAIN, None, ALU.mult)
            nc.vector.tensor_scalar(f0_b[:], f0_b[:], GAIN, None, ALU.mult).then_inc(s_f0_w, 1)
            dve.wait_ge(s_deg_col, 1)
            nc.vector.tensor_copy(deg[:], PS[6][:, 0:NT])
            nc.vector.tensor_scalar(deg1[:], PS[6][:, 0:NT], 1.0, None, ALU.add).then_inc(s_deg, 1)
            dve.wait_ge(s_deg, 1)
            nc.vector.reciprocal(rdeg[:], deg1[:])
            features(0, 0)
            dve.wait_ge(s_dinv, NG)
            for g in range(NG):
                dve.wait_ge(s_mix, g + 1)
                for t in GROUPS[g]:
                    ins = nc.vector.tensor_scalar(tile(R[2], t), tile(PS[3 + g], t % 4), dinv[:, t:t + 1], 0.0, ALU.mult, ALU.max)
                ins.then_inc(s_relu, 1)

            def add_first(g):
                dve.wait_ge(s_rnorm, g + 1)
                for t in GROUPS[g]:
                    ins = nc.vector.scalar_tensor_tensor(tile(x, t), tile(R[2], t), rnorm[:, t:t + 1], tile(x, t), ALU.mult, ALU.add)
                return ins

            norm_stats(x, add_first)
            normalise(R[0], 1, s_h, FG)

            def slot(place, count, valid):
                if valid(0):
                    g = place(0)
                    dve.wait_ge(s_hr, count(0))
                    dve.wait_ge(s_p, count(0))
                    for m, t in enumerate(FG[g]):
                        ins = nc.vector.scalar_tensor_tensor(tile(R[0], t), tile(PS[NF + g], m), rss[:, t:t + 1], f0_b[:], ALU.mult, ALU.add)
                    ins.then_inc(s_h, 1)
                if valid(2):
                    g = place(2)
                    dve.wait_ge(s_h2, count(2))
                    for t in FG[g]:
                        ins = nc.vector.bn_stats(stats[:, t, :], tile(R[0], t))
                    ins.then_inc(s_st, 1)
                    dve.wait_ge(s_st, count(2))
                if valid(3):
                    c = FCOLS[place(3)]
                    dve.wait_ge(s_sg, count(3))
                    nc.vector.tensor_tensor(R[0][:, c], R[0][:, c], R[1][:, c], ALU.mult).then_inc(s_h2, 1)
                if valid(2):
                    for t in FG[place(2)]:
                        ins = nc.vector.bn_aggr(mv[:, t, :], stats[:, t, :])
                    ins.then_inc(s_hv, 1)

            recurrent_slots(dve, slot)
            dve.wait_ge(s_h, NF * (ITERS + 1))
            norm_stats(x, lambda g: nc.vector.scalar_tensor_tensor(x[:, COLS[g]], R[0][:, COLS[g]], 1 / GAIN, x[:, COLS[g]], ALU.mult, ALU.add))
            features(2, 1)
            dve.wait_ge(s_small2, 16 * len(SMALL2))
            dve.wait_ge(s_whi, 1)
            nc.vector.scalar_tensor_tensor(a_wlo[:], a_w[:], a_ln1[:, 0:1], a_whi[:].bitcast(F32), ALU.mult, ALU.subtract).then_inc(s_wlo, 1)
            nc.vector.scalar_tensor_tensor(a_rlo, a_router[:], a_ln2[:, 0:1], a_rhi.bitcast(F32), ALU.mult, ALU.subtract)
            nc.vector.tensor_tensor(r2_lo[:], r2_w1[:], r2_hi[:].bitcast(F32), ALU.subtract).then_inc(s_wlo, 1)
            nc.vector.tensor_tensor(r3_lo, r3_w[:], r3_hi.bitcast(F32), ALU.subtract).then_inc(s_wlo, 1)
            nc.vector.tensor_copy(mask[:], mask_f[:])
            for g in range(NG):
                dve.wait_ge(s_mix, NG + g + 1)
                for t in GROUPS[g]:
                    ins = nc.vector.scalar_tensor_tensor(tile(R[2], t), tile(PS[3 + g], t % 4), rdeg[:, t:t + 1], l1_bias[:], ALU.mult, ALU.add)
                ins.then_inc(s_pre, 1)
            later_layers()
            nc.vector.engine_nop().then_inc(s_final, 1)

        @block.sync
        def _(sp):
            sp.wait_ge(s_final, 1)
            full = NT - 1
            sp.dma_start(out[0:full * P, :].rearrange("(t p) c -> p t c", p=P),
                         x[:, 0:full * P].rearrange("p (t c) -> p t c", c=P)).then_inc(s_out, 16)
            sp.dma_start(out[full * P:T, :], x[0:T - full * P, full * P:]).then_inc(s_out, 16)
            sp.wait_ge(s_out, 32)


def kernel(**inputs):
    import concourse.bacc as bacc
    from concourse.bass_utils import run_bass_kernel_spmd

    a = {k: np.asarray(v) for k, v in inputs.items()}
    f32 = np.float32

    def rep(v):
        return np.broadcast_to(v, (P,) + v.shape)

    adj_t = np.eye(TP, dtype=f32)
    adj_t[:T, :T] = a["adj"].T
    x_pad = np.zeros((TP, P), f32)
    x_pad[:T] = a["x"]
    arrays = {
        "x": x_pad,
        "adj_t": adj_t,
        "ident": np.eye(P, dtype=f32),
        "f0_wt": a["L0_ffn_W"].T,
        "f0_lnw": a["L0_ffn_ln_w"][:, None],
        "f0_lnb": a["L0_ffn_ln_b"][:, None],
        "f0_b": rep(a["L0_ffn_b"]),
        "gnn_w": np.stack([a["L0_gnn_W"], a["L1_gnn_W"], a["L3_gnn_W"].T], axis=1),
        "l1_bias": rep(a["L1_gnn_b"]),
        "l2_scale": a["L2_gnn_W"][:, None],
    }
    inv_freq = 1.0 / 10000.0 ** (np.arange(0, HD, 2, dtype=f32) / HD)
    freqs = np.outer(np.arange(TP, dtype=f32), inv_freq).astype(f32)
    emb = np.concatenate([freqs, freqs], axis=-1)
    sign = np.where(np.arange(HD) < HD // 2, -1, 1).astype(f32)[:, None]
    arrays["cos"] = np.tile(np.cos(emb).T, (P // HD, 1)).astype(f32)
    arrays["sin"] = np.tile(np.sin(emb).T * sign, (P // HD, 1)).astype(f32)

    def rotated(w):
        return w.reshape(-1, 2, HD // 2, P)[:, ::-1].reshape(w.shape)

    wq, wk, wv = a["L1_ffn_wq"], a["L1_ffn_wk"], a["L1_ffn_wv"]
    arrays["a_w"] = np.concatenate([wq, rotated(wq), wk, rotated(wk), wv]).T
    arrays["a_ln1"] = a["L1_ffn_ln1_w"][:, None]
    arrays["a_ln2"] = a["L1_ffn_ln2_w"][:, None]
    arrays["a_wo"] = a["L1_ffn_wo"].T
    arrays["a_router"] = a["L1_ffn_router_w"].T
    later = np.triu(np.ones((P, P), bool), 1)
    arrays["mask"] = np.concatenate([np.where(later, MASKED, 0), np.where(later.T, MASKED, 0)], axis=1).astype(f32)
    pad_rows = np.zeros((P, 1), f32)
    pad_rows[96:98] = 1
    arrays["k_pad"] = pad_rows
    select_q = np.zeros((P, 2 * HEADS, 96), f32)
    select_k = np.zeros((P, KV_HEADS, 96), f32)
    lane = np.arange(HD)
    for h in range(HEADS):
        select_q[HD * h + lane, h, lane] = 1
        select_q[HD * h + lane, h, HD + lane] = 1
        select_q[HD * h + lane, HEADS + h, 2 * HD + lane] = 1
    for v in range(KV_HEADS):
        for part, first_row in enumerate((0, 64, 0)):
            select_k[first_row + HD * v + lane, v, HD * part + lane] = 1
    arrays["select_q"] = select_q.reshape(P, -1)
    arrays["select_k"] = select_k.reshape(P, -1)
    arrays["descend"] = rep(np.arange(8, 0, -1).astype(f32))
    hid = a["L1_ffn_w1"].shape[1]
    w13 = np.zeros((P, E1, 2, HID), f32)
    w13[:, :, 0, :hid] = a["L1_ffn_w1"].transpose(2, 0, 1)
    w13[:, :, 1, :hid] = a["L1_ffn_w3"].transpose(2, 0, 1)
    arrays["moe_w13"] = w13.reshape(P, E1, 2 * HID)
    down = np.zeros((E1, HID, P), f32)
    down[:, :hid] = a["L1_ffn_w2"].transpose(0, 2, 1)
    arrays["moe_w2"] = down.reshape(E1, 3, P, P).transpose(2, 0, 1, 3).reshape(P, E1, HID)

    def layers3(w1, w2, w3):
        return np.concatenate([w.transpose(1, 0, 2) for w in (w1, w2, w3)], axis=2)

    def columns(v, n=8):
        full = np.zeros((P, n), f32)
        full[:, :v.shape[0]] = v.T
        return full

    arrays["l2_w"] = layers3(a["L2_ffn_expert_w1"], a["L2_ffn_expert_w2"], a["L2_ffn_expert_w3"])
    arrays["l3_w"] = layers3(a["L3_ffn_W1"], a["L3_ffn_W2"], a["L3_ffn_Wo"])
    one = np.ones((P, 8), f32)
    arrays["par2"] = np.stack([one, columns(a["L2_ffn_expert_b1"]), one, columns(a["L2_ffn_expert_b2"])], axis=1)
    arrays["bn"] = np.stack([columns(a["L3_ffn_" + k + n]) for n in "12" for k in ("g", "be", "m", "v", "b")], axis=1)
    rw1 = np.zeros((P, P), f32)
    rw1[:, :64] = a["L2_ffn_router_w1"]
    arrays["r2_w1"] = rw1
    rb1 = np.zeros((P, 1), f32)
    rb1[:64, 0] = a["L2_ffn_router_b1"]
    arrays["r2_b1"] = rb1
    rw2 = np.zeros((P, 8), f32)
    rw2[:64, :E2] = a["L2_ffn_router_w2"]
    arrays["r2_w2"] = rw2
    rb2 = np.zeros(8, f32)
    rb2[:E2] = a["L2_ffn_router_b2"]
    arrays["r2_b2"] = rep(rb2)
    arrays["r3_w"] = a["L3_ffn_Wr"]
    arrays["r3_b"] = rep(a["L3_ffn_br"])
    last_bias = np.zeros((8, 2, P), f32)
    last_bias[:E2, 0] = a["L2_ffn_expert_b3"]
    last_bias[:E3, 1] = a["L3_ffn_bo"]
    arrays["b3"] = last_bias
    nc = bacc.Bacc("TRN2", target_bir_lowering=False, num_devices=1)
    sent, d = {}, {}
    for name, v in arrays.items():
        sent[f"in_{name}"] = np.ascontiguousarray(v)
        d[name] = nc.dram_tensor(f"in_{name}", v.shape, F32, kind="ExternalInput").ap()
    out = nc.dram_tensor("out_x", (T, P), F32, kind="ExternalOutput").ap()
    adj_lo_dram = nc.dram_tensor("adj_lo_store", (P, NT, TP), F32).ap()
    build(nc, d, out, adj_lo_dram)
    r = run_bass_kernel_spmd(nc, [sent], core_ids=[0])
    return r.results[0]["out_x"]
```
